# Optimizing a Trainium2 kernel written in Bass

```python
import numpy as np
import jax
import jax.numpy as jnp

def _softmax(x, axis=-1):
    return jax.nn.softmax(x, axis=axis)

def _gelu(x):
    return jax.nn.gelu(x, approximate=True)

def _silu(x):
    return jax.nn.silu(x)

def _sigmoid(x):
    return jax.nn.sigmoid(x)

def _layernorm(x, axis=-1, eps=1e-05):
    m = jnp.mean(x, axis=axis, keepdims=True)
    v = jnp.var(x, axis=axis, keepdims=True)
    return (x - m) / jnp.sqrt(v + eps)

def _scatter_add(tgt, idx, src, axis=0):
    return tgt.at[idx].add(src)

def _segment_sum(src, seg, n):
    return jax.ops.segment_sum(src, seg, n)
kernel_name = 'mk_gnn_preln_d2_gnn_r64_ec29e5'

def setup_inputs(seed: int=0):
    np.random.seed(seed)
    _w = jnp.asarray

    def _rec_inputs():
        import jax
        import jax.numpy as jnp
        _gk = jax.random.key(seed)
        x = -1.686e-05 + 1 * jax.random.normal(jax.random.fold_in(_gk, 1), (100000, 160), jnp.float32)
        src = jax.random.randint(jax.random.fold_in(_gk, 2), (25000,), 0, 100000, jnp.int32)
        dst = jnp.minimum((100000 * jax.random.uniform(jax.random.fold_in(_gk, 3), (25000,)) ** 2.0).astype(jnp.int32), 99999)
        _o = jnp.argsort(dst, stable=True)
        src = src[_o]
        dst = dst[_o]
        edge_attr_4 = -0.000107899 + 1.00008 * jax.random.normal(jax.random.fold_in(_gk, 12), (25000, 4), jnp.float32)
        edge_attr_8 = 0.000398945 + 1.00003 * jax.random.normal(jax.random.fold_in(_gk, 13), (25000, 8), jnp.float32)
        node_vec1 = jax.random.uniform(jax.random.fold_in(_gk, 15), (100000, 1), jnp.float32, 0.0, 1)
        return (x, src, dst, edge_attr_4, edge_attr_8, node_vec1)
    x, src, dst, edge_attr_4, edge_attr_8, node_vec1 = _rec_inputs()

    def _L0_gnn_setup():
        import jax, jax.numpy as jnp
        import numpy as np
        INV3 = 1.0 / np.sqrt(3.0)

        def _fctp(x_s, x_v, attr, w0, w1):
            s = x_s @ w0 * (1.0 / np.sqrt(x_s.shape[-1])) * attr
            v = jnp.einsum('nud,uw->nwd', x_v, w1) * (1.0 / np.sqrt(x_v.shape[-2])) * attr[..., None]
            return (s, v)
        key = jax.random.key(seed)
        ks = jax.random.split(key, 16)
        N, E = (50000, 12500)
        inp = {'node_input': jax.random.normal(ks[0], (N, 160), jnp.float32), 'node_attr': jnp.ones((N, 1), jnp.float32), 'edge_attr': jax.random.normal(ks[1], (E, 4), jnp.float32), 'edge_scalars': jax.random.normal(ks[2], (E, 8), jnp.float32), 'sc_w0': jax.random.normal(ks[3], (64, 64), jnp.float32), 'sc_w1': jax.random.normal(ks[4], (32, 32), jnp.float32), 'lin1_w0': jax.random.normal(ks[5], (64, 64), jnp.float32), 'lin1_w1': jax.random.normal(ks[6], (32, 32), jnp.float32), 'fc_w1': jax.random.normal(ks[7], (8, 64), jnp.float32), 'fc_w2': jax.random.normal(ks[8], (64, 192), jnp.float32), 'lin2_w0': jax.random.normal(ks[9], (96, 64), jnp.float32), 'lin2_w1': jax.random.normal(ks[10], (96, 32), jnp.float32), 'lin3_w': jax.random.normal(ks[11], (96, 1), jnp.float32), 'edge_src': jax.random.randint(ks[12], (E,), 0, N), 'edge_dst': jax.random.randint(ks[13], (E,), 0, N), 'num_neighbors': 16}
        return inp
    _L0_gnn_all = _L0_gnn_setup()
    _L0_gnn_in = {k: v for k, v in _L0_gnn_all.items() if k in ('sc_w0', 'sc_w1', 'lin1_w0', 'lin1_w1', 'fc_w1', 'fc_w2', 'lin2_w0', 'lin2_w1', 'lin3_w')}
    del _L0_gnn_all

    def _L1_gnn_setup():
        import jax, jax.numpy as jnp
        import numpy as np
        N, E = (50000, 12500)
        MUL0, MUL1 = (64, 32)
        D = MUL0 + 3 * MUL1
        INV3 = float(1.0 / np.sqrt(3.0))
        INV6 = float(1.0 / np.sqrt(6.0))
        C0 = float(1.0 / np.sqrt(MUL0 + MUL1))
        C1 = float(np.sqrt(3.0 / (MUL0 + 2 * MUL1)))
        LIN_S = float(1.0 / np.sqrt(MUL0))
        LIN_V = float(1.0 / np.sqrt(MUL1))
        key = jax.random.key(seed)
        ks = jax.random.split(key, 10)
        x = jax.random.normal(ks[0], (N, D), dtype=jnp.float32)
        sh = jax.random.normal(ks[1], (E, 4), dtype=jnp.float32)
        edge_index = jax.random.randint(ks[2], (2, E), 0, N, dtype=jnp.int64)
        W1 = jax.random.normal(ks[3], (MUL0, MUL0), dtype=jnp.float32)
        W2 = jax.random.normal(ks[4], (MUL1, MUL0), dtype=jnp.float32)
        W3 = jax.random.normal(ks[5], (MUL0, MUL1), dtype=jnp.float32)
        W4 = jax.random.normal(ks[6], (MUL1, MUL1), dtype=jnp.float32)
        W5 = jax.random.normal(ks[7], (MUL1, MUL1), dtype=jnp.float32)
        Ws = jax.random.normal(ks[8], (MUL0, MUL0), dtype=jnp.float32)
        Wv = jax.random.normal(ks[9], (MUL1, MUL1), dtype=jnp.float32)
        return {'x': x, 'sh': sh, 'W1': W1, 'W2': W2, 'W3': W3, 'W4': W4, 'W5': W5, 'Ws': Ws, 'Wv': Wv, 'edge_index': edge_index}
    _L1_gnn_all = _L1_gnn_setup()
    _L1_gnn_in = {k: v for k, v in _L1_gnn_all.items() if k in ('W1', 'W2', 'W3', 'W4', 'W5', 'Ws', 'Wv')}
    del _L1_gnn_all
    return {'x': x, 'src': src, 'dst': dst, 'edge_attr_4': edge_attr_4, 'edge_attr_8': edge_attr_8, 'node_vec1': node_vec1, 'L0_gnn_sc_w0': _L0_gnn_in['sc_w0'], 'L0_gnn_sc_w1': _L0_gnn_in['sc_w1'], 'L0_gnn_lin1_w0': _L0_gnn_in['lin1_w0'], 'L0_gnn_lin1_w1': _L0_gnn_in['lin1_w1'], 'L0_gnn_fc_w1': _L0_gnn_in['fc_w1'], 'L0_gnn_fc_w2': _L0_gnn_in['fc_w2'], 'L0_gnn_lin2_w0': _L0_gnn_in['lin2_w0'], 'L0_gnn_lin2_w1': _L0_gnn_in['lin2_w1'], 'L0_gnn_lin3_w': _L0_gnn_in['lin3_w'], 'L1_gnn_W1': _L1_gnn_in['W1'], 'L1_gnn_W2': _L1_gnn_in['W2'], 'L1_gnn_W3': _L1_gnn_in['W3'], 'L1_gnn_W4': _L1_gnn_in['W4'], 'L1_gnn_W5': _L1_gnn_in['W5'], 'L1_gnn_Ws': _L1_gnn_in['Ws'], 'L1_gnn_Wv': _L1_gnn_in['Wv']}

def reference(x, src, dst, edge_attr_4, edge_attr_8, node_vec1, L0_gnn_sc_w0, L0_gnn_sc_w1, L0_gnn_lin1_w0, L0_gnn_lin1_w1, L0_gnn_fc_w1, L0_gnn_fc_w2, L0_gnn_lin2_w0, L0_gnn_lin2_w1, L0_gnn_lin3_w, L1_gnn_W1, L1_gnn_W2, L1_gnn_W3, L1_gnn_W4, L1_gnn_W5, L1_gnn_Ws, L1_gnn_Wv):
    import jax
    import jax.numpy as jnp

    def _L0_gnn_ref(node_input, node_attr, edge_attr, edge_scalars, sc_w0, sc_w1, lin1_w0, lin1_w1, fc_w1, fc_w2, lin2_w0, lin2_w1, lin3_w, edge_src, edge_dst, num_neighbors):
        import jax, jax.numpy as jnp
        import numpy as np
        INV3 = 1.0 / np.sqrt(3.0)

        def _fctp(x_s, x_v, attr, w0, w1):
            s = x_s @ w0 * (1.0 / np.sqrt(x_s.shape[-1])) * attr
            v = jnp.einsum('nud,uw->nwd', x_v, w1) * (1.0 / np.sqrt(x_v.shape[-2])) * attr[..., None]
            return (s, v)
        N = node_input.shape[0]
        h = jax.nn.silu(edge_scalars @ fc_w1 * (1.0 / np.sqrt(8.0)))
        weight = h @ fc_w2 * (1.0 / np.sqrt(64.0))
        xs, xv = (node_input[:, :64], node_input[:, 64:].reshape(N, 32, 3))
        sc_s, sc_v = _fctp(xs, xv, node_attr, sc_w0, sc_w1)
        f_s, f_v = _fctp(xs, xv, node_attr, lin1_w0, lin1_w1)
        gs = f_s[edge_src]
        gv = f_v[edge_src]
        ys, yv = (edge_attr[:, :1], edge_attr[:, 1:])
        w1_, w2_ = (weight[:, :64], weight[:, 64:128])
        w3_, w4_ = (weight[:, 128:160], weight[:, 160:192])
        m0a = gs * ys * w1_
        m0b = jnp.sum(gv * yv[:, None, :], -1) * INV3 * w4_
        m1a = gs[..., None] * yv[:, None, :] * w2_[..., None]
        m1b = gv * ys[..., None] * w3_[..., None]
        E = m0a.shape[0]
        edge_feat = jnp.concatenate([m0a, m0b, m1a.reshape(E, 192), m1b.reshape(E, 96)], -1)
        mid = jax.ops.segment_sum(edge_feat, edge_dst, num_segments=N)
        mid = mid / np.sqrt(float(num_neighbors))
        mid_s, mid_v = (mid[:, :96], mid[:, 96:].reshape(N, 96, 3))
        c_s, c_v = _fctp(mid_s, mid_v, node_attr, lin2_w0, lin2_w1)
        conv = jnp.concatenate([c_s, c_v.reshape(N, -1)], -1)
        scfeat = jnp.concatenate([sc_s, sc_v.reshape(N, -1)], -1)
        angle = 0.1 * (mid_s @ lin3_w) * (1.0 / np.sqrt(96.0)) * node_attr
        return jnp.cos(angle) * scfeat + jnp.sin(angle) * conv

    def _L1_gnn_ref(x, sh, W1, W2, W3, W4, W5, Ws, Wv, edge_index):
        import jax, jax.numpy as jnp
        import numpy as np
        N, E = (50000, 12500)
        MUL0, MUL1 = (64, 32)
        D = MUL0 + 3 * MUL1
        INV3 = float(1.0 / np.sqrt(3.0))
        INV6 = float(1.0 / np.sqrt(6.0))
        C0 = float(1.0 / np.sqrt(MUL0 + MUL1))
        C1 = float(np.sqrt(3.0 / (MUL0 + 2 * MUL1)))
        LIN_S = float(1.0 / np.sqrt(MUL0))
        LIN_V = float(1.0 / np.sqrt(MUL1))
        n = x.shape[0]
        src, dst = (edge_index[0], edge_index[1])
        s = x[:, :MUL0]
        v = x[:, MUL0:].reshape(n, MUL1, 3)
        ss, vv = (s[src], v[src])
        e0 = sh[:, 0:1]
        e1 = sh[:, 1:4]
        dot = jnp.einsum('eui,ei->eu', vv, e1)
        out0 = C0 * (ss * e0 @ W1 + dot * INV3 @ W2)
        p3 = (ss @ W3)[:, :, None] * e1[:, None, :] * INV3
        p4 = jnp.einsum('eui,uw->ewi', vv * e0[:, :, None], W4) * INV3
        p5 = jnp.einsum('eui,uw->ewi', jnp.cross(vv, e1[:, None, :]), W5) * INV6
        out1 = C1 * (p3 + p4 + p5)
        m = jnp.concatenate([out0, out1.reshape(-1, 3 * MUL1)], axis=1)
        m_agg = jax.ops.segment_sum(m, dst, num_segments=n)
        hs = m_agg[:, :MUL0] @ Ws * LIN_S
        hv = jnp.einsum('nui,uw->nwi', m_agg[:, MUL0:].reshape(n, MUL1, 3), Wv) * LIN_V
        h = jnp.concatenate([hs, hv.reshape(n, 3 * MUL1)], axis=1)
        return x + jax.nn.relu(h)
    edge_index = jnp.stack([src, dst])
    h = jnp.maximum(_layernorm(x, axis=-1), 0.0)
    x = x + _L0_gnn_ref(h, node_vec1, edge_attr_4, edge_attr_8, L0_gnn_sc_w0, L0_gnn_sc_w1, L0_gnn_lin1_w0, L0_gnn_lin1_w1, L0_gnn_fc_w1, L0_gnn_fc_w2, L0_gnn_lin2_w0, L0_gnn_lin2_w1, L0_gnn_lin3_w, src, dst, 16)
    h = jnp.maximum(_layernorm(x, axis=-1), 0.0)
    x = x + _L1_gnn_ref(h, edge_attr_4, L1_gnn_W1, L1_gnn_W2, L1_gnn_W3, L1_gnn_W4, L1_gnn_W5, L1_gnn_Ws, L1_gnn_Wv, edge_index)
    return x

_drawn_inputs = setup_inputs


def setup_inputs(seed=0):
    import zlib

    import numpy as np

    out = dict(_drawn_inputs(seed))
    spreads = {}
    factors = {'edge_attr_8': 8.0,
     'L0_gnn_lin1_w0': 8.0,
     'L0_gnn_lin1_w1': 8.0,
     'L0_gnn_fc_w1': 8.0,
     'L0_gnn_fc_w2': 8.0,
     'L0_gnn_lin2_w0': 8.0,
     'L0_gnn_lin2_w1': 8.0,
     'L0_gnn_lin3_w': 8.0,
     'L0_gnn_sc_w0': 30.622,
     'L0_gnn_sc_w1': 34.575,
     'L1_gnn_W1': 34.376,
     'L1_gnn_W2': 46.287,
     'L1_gnn_W3': 28.774,
     'L1_gnn_W4': 38.256,
     'L1_gnn_W5': 39.913,
     'L1_gnn_Ws': 26.78,
     'L1_gnn_Wv': 8.0}
    for name, (base, spread) in spreads.items():
        noise = np.random.default_rng([zlib.crc32(name.encode()), seed]).standard_normal(out[name].shape)
        drawn = base * np.exp(spread * noise) if base else spread * noise
        out[name] = jnp.asarray(drawn.astype(out[name].dtype))
    for name, factor in factors.items():
        out[name] = (out[name] * factor).astype(out[name].dtype)
    return out
```

```python
from contextlib import ExitStack

import concourse.bass as bass
from concourse import mybir

P = 128
GD = 8
GQ = 4
D = 160
DS, DU, DV = 64, 32, 96
XW = D + 1
EW = 6
SW = 8
CW = D + 1
EPS = 1e-5
FAR = 1 << 20

W_SC, W_L1, W_FC1, W_FC2, W_R1, W_R2, W_R3 = 0, 416, 832, 1088, 1472, 1569, 1730
W_W1T, W_W2T, W_W3T, W_W4T, W_W5T = 1795, 1859, 1955, 2019, 2115
W_WS, W_WVK, W_WV, W_WVA, W_WVB, W_END = 2211, 2275, 2371, 2403, 2499, 2595

U_C, U_A, U_D, U_B = 0, 32, 97, 193
U_SEG = 2 * P


class At:

    def __init__(self, i, c, period=4):
        self.i, self.c, self.period = i + c // period, c % period, period

    def __add__(self, n):
        return At(self.i, self.c + n, self.period)

    def __sub__(self, n):
        return At(self.i, self.c - n, self.period)

    def times(self, m, plus=0):
        return self.i * (self.period * m) + (self.c * m + plus)

    def over(self, k, m=1, plus=0):
        return self.i * (self.period // k * m) + (self.c // k * m + plus)

    def mod(self, k):
        return self.c % k


def wait(eng, sem, value):
    if not (isinstance(value, int) and value <= 0):
        eng.wait_ge(sem, value)


def gnn_kernel(nc, xa, src, dst, edges, scalars, wpack, out):
    f32, i32 = mybir.dt.float32, mybir.dt.int32
    ALU, ACT = mybir.AluOpType, mybir.ActivationFunctionType
    N = xa.shape[0]
    T = src.shape[1]
    Q = T // GQ
    UROWS = P * GD
    U = -(-N // UROWS)
    assert U == 2 * Q and Q % 2 == 1 and Q >= 5
    TA = min(T, P)

    def scratch(name, shape, dt=f32):
        return nc.dram_tensor(name, shape, dt).ap()

    src_tab = scratch("src_tab", (Q, P, GQ), i32)
    dst_tab = scratch("dst_tab", (Q, P, GQ), i32)
    put_tab = scratch("put_tab", (Q, P, GQ), i32)
    key_tab = scratch("key_tab", (Q, P, 2 * GQ))
    row_tab = scratch("row_tab", (T, P))
    hid_tab = scratch("hid_tab", (Q, P, 256))
    sum_tab = scratch("sum_tab", (Q, P, GQ * CW))
    y_tab = scratch("y_tab", (Q, P, GQ * D))
    h1_all = scratch("h1_all", (N, D))

    row_q = row_tab.rearrange("(q c) p -> q (c p)", c=GQ)
    ed_q = edges.rearrange("p (q c) f -> q p (c f)", c=GQ)
    sc_q = scalars.rearrange("p (q c) f -> q p (c f)", c=GQ)
    NU = U - 1
    x_u = xa[0:NU * UROWS, :].rearrange("(u p g) f -> u p (g f)", p=P, g=GD)
    o_u = out[0:NU * UROWS, :].rearrange("(u p g) f -> u p (g f)", p=P, g=GD)
    h_u = h1_all[0:NU * UROWS, :].rearrange("(u p g) f -> u p (g f)", p=P, g=GD)
    x_l = xa[N - UROWS:N, :].rearrange("(p g) f -> p (g f)", p=P)
    o_l = out[N - UROWS:N, :].rearrange("(p g) f -> p (g f)", p=P)
    h_l = h1_all[N - UROWS:N, :].rearrange("(p g) f -> p (g f)", p=P)

    with ExitStack() as ctx:
        def sb(name, shape, dt=f32):
            return ctx.enter_context(nc.sbuf_tensor(name, shape, dt))

        def two(name, shape, dt=f32):
            return [sb(f"{name}{i}", shape, dt) for i in range(2)]

        def sem(name):
            return ctx.enter_context(nc.semaphore(name))

        def sem2(name):
            return [sem(f"{name}{i}") for i in range(2)]

        bank = [ctx.enter_context(nc.psum_tensor(f"bank{i}", [P, 512], f32)) for i in range(8)]

        wp = sb("wp", [P, W_END])
        ident = sb("ident", [P, P])
        msg1 = [sb("msg1a", [P, D]), sb("msg1b", [P, D]), sb("msg1c", [P, DV]), sb("msg1d", [P, DV])]
        msg1s = sb("msg1s", [P, DU])
        t_src = sb("t_src", [P, T], i32)
        t_dst = sb("t_dst", [P, T], i32)
        t_next = sb("t_next", [P, T], i32)
        t_prev = sb("t_prev", [P, T], i32)
        t_gat = sb("t_gat", [P, T], i32)
        t_put = sb("t_put", [P, T], i32)
        f_dst = sb("f_dst", [P, T])
        f_next = sb("f_next", [P, T])
        f_put = sb("f_put", [P, T])
        f_key = sb("f_key", [P, Q, 2 * GQ])
        t_row = two("t_row", [P, P])
        x_in = two("x_in", [P, GD * XW])
        st1 = two("st1", [P, GD, 6])
        su1 = two("su1", [P, GD, 2])
        df1 = two("df1", [P, GD])
        sq1 = two("sq1", [P, GD])
        m2a = two("m2a", [P, GD])
        neg1 = two("neg1", [P, GD])
        var1 = two("var1", [P, GD])
        sd1 = two("sd1", [P, GD])
        inv1 = two("inv1", [P, GD])
        scl1 = two("scl1", [P, GD])
        st2 = two("st2", [P, GD, 6])
        su2 = two("su2", [P, GD, 2])
        df2 = two("df2", [P, GD])
        sq2 = two("sq2", [P, GD])
        m2b = two("m2b", [P, GD])
        neg2 = two("neg2", [P, GD])
        var2 = two("var2", [P, GD])
        sd2 = two("sd2", [P, GD])
        inv2 = two("inv2", [P, GD])
        nmr2 = two("nmr2", [P, GD])
        hb = two("hb", [P, GD * P])
        hr = two("hr", [P, GD * 32])
        hT = two("hT", [P, 512])
        hR = two("hR", [P, P])
        x1 = two("x1", [P, GD * D])
        h1 = two("h1", [P, GD * D])
        yo = two("yo", [P, GD * D])
        i_src = two("i_src", [P, GQ], i32)
        i_dst = two("i_dst", [P, GQ], i32)
        i_put = two("i_put", [P, GQ], i32)
        q_key = two("q_key", [P, 2 * GQ])
        q_row = two("q_row", [P, GQ * P])
        q_ed = two("q_ed", [P, GQ * EW])
        q_sc = two("q_sc", [P, GQ * SW])
        q_hid = two("q_hid", [P, 256])
        same = [two(f"same{t}", [P, P]) for t in range(GQ)]
        carry = [two(f"carry{t}", [P, P]) for t in range(GQ)]
        x_e = two("x_e", [P, GQ * XW])
        h_e = sb("h_e", [P, GQ * P])
        hr_e = two("hr_e", [P, GQ * 32])
        part2 = two("part2", [P, GQ * D])
        eT = sb("eT", [P, 512])
        eR = sb("eR", [P, P])
        g_e = two("g_e", [P, D])
        feat = two("feat", [P, 512])
        fT = two("fT", [P, 512])
        xr = two("xr", [P, CW])
        v_e = two("v_e", [P, CW])
        tot = two("tot", [P, GQ * CW])
        cv = two("cv", [P, GQ * CW])
        trig = [two(f"trig{n}", [P, 2 * GQ]) for n in range(8)]

        st_e = two("st_e", [P, GQ, 6])
        su_e = two("su_e", [P, GQ, 2])
        df_e = two("df_e", [P, GQ])
        sq_e = two("sq_e", [P, GQ])
        m2_e = two("m2_e", [P, GQ])
        neg_e = two("neg_e", [P, GQ])
        var_e = two("var_e", [P, GQ])
        sd_e = two("sd_e", [P, GQ])
        inv_e = two("inv_e", [P, GQ])
        scl_e = two("scl_e", [P, GQ])

        s_w = sem("weights_loaded")
        s_tab_in = sem("edge_tables_loaded")
        s_fill = sem("table_edges_filled")
        s_id = sem("identity_built")
        s_tabc = sem("tables_computed")
        s_wscaled = sem("weights_scaled")
        s_rowps = sem("rows_transposed")
        s_rowsb = sem("rows_copied")
        s_tab_out = sem("tables_stored")
        s_turn = sem("indirect_dmas_may_start")
        s_mz = sem("message_weights_cleared")
        s_mp = sem("message_weights_multiplied")
        s_mc = sem("message_weights_copied")

        block = ctx.enter_context(nc.Block())

        n_in = sem2("net_rows_loaded")
        n_tr = sem("net_rows_transposed")
        n_te = sem("net_transposes_copied")
        n_mm = sem("net_products_done")
        n_act = sem("net_hidden_ready")
        n_st = sem2("net_hidden_stored")
        d_in = sem2("x_loaded")
        d_ln1 = sem("dense_moments1")
        d_relu = sem("dense_h_ready")
        d_sq1 = sem("dense_root1")
        d_tr = sem("dense_h_transposed")
        d_hT = sem("dense_hT_copied")
        d_mm = sem("dense_product_done")
        d_scl = sem("dense_scale_ready")
        d_x1 = sem("dense_x1_ready")
        d_ln2 = sem("dense_moments2")
        d_sq2 = sem("dense_root2")
        d_nmr = sem("dense_norm2_ready")
        d_h1 = sem("dense_h1_ready")
        d_y = sem("dense_y_ready")
        d_sth = sem2("dense_h1_stored")
        d_sto = sem2("dense_out_stored")
        e_ix = sem2("p1_index_loaded")
        e_tb = sem2("p1_tables_loaded")
        e_hd = sem2("p1_hidden_loaded")
        e_g = sem2("p1_source_rows")
        e_ln = sem("p1_moments")
        e_relu = sem("p1_h_ready")
        e_sq = sem("p1_root")
        e_scl = sem("p1_scale_ready")
        e_sc = sem("p1_selectors_ready")
        e_tr = sem("p1_h_transposed")
        e_hT = sem("p1_hT_copied")
        e_pw = sem("p1_products_done")
        e_gg = sem("p1_g_ready")
        e_fm = sem("p1_feature_step")
        e_ft = sem("p1_features_ready")
        e_ftr = sem("p1_features_transposed")
        e_fte = sem("p1_featuresT_copied")
        e_u = sem("p1_message_parts_done")
        e_xb = sem("p1_rest_copied")
        e_vx = sem("p1_rest_ready")
        e_v = sem("p1_message_ready")
        e_seg = sem("p1_sum_done")
        e_tot = sem("p1_sum_copied")
        e_st = sem2("p1_sum_stored")
        e_z = sem("p1_first_carry_cleared")
        r_ix = sem2("p2_index_loaded")
        r_px = sem2("p2_put_loaded")
        r_cv = sem2("p2_sums_loaded")
        r_g = sem2("p2_node_rows")
        r_ln1 = sem("p2_moments1")
        r_ang = sem("p2_angle_steps")
        r_relu = sem("p2_h_ready")
        r_sq1 = sem("p2_root1")
        r_sin = sem("p2_sines_ready")
        r_tr = sem("p2_h_transposed")
        r_hT = sem("p2_hT_copied")
        r_mm = sem("p2_product_done")
        r_scl = sem("p2_scale_steps")
        r_x1 = sem("p2_x1_steps")
        r_ln2 = sem("p2_moments2")
        r_sq2 = sem("p2_root2")
        r_nmr = sem("p2_norm2_ready")
        r_h1 = sem("p2_h1_ready")
        r_y = sem("p2_y_ready")
        r_put = sem2("p2_h1_scattered")
        r_sty = sem2("p2_y_stored")
        m_ix = sem2("p3_index_loaded")
        m_px = sem2("p3_put_loaded")
        m_tb = sem2("p3_tables_loaded")
        m_y = sem2("p3_y_loaded")
        m_g = sem2("p3_h1_rows")
        m_sc = sem("p3_selectors_ready")
        m_ft = sem("p3_features_ready")
        m_ss = sem("p3_scalars_copied")
        m_ftr = sem("p3_features_transposed")
        m_fte = sem("p3_featuresT_copied")
        m_u = sem("p3_message_parts_done")
        m_cs = sem("p3_scalar_message_copied")
        m_vx = sem("p3_outer_part_ready")
        m_v = sem("p3_message_ready")
        m_seg = sem("p3_sum_done")
        m_tot = sem("p3_sum_copied")
        m_o = sem("p3_out_ready")
        m_put = sem2("p3_out_scattered")
        m_z = sem("p3_first_carry_cleared")

        def x3(t, w, g):
            return t[:, :].rearrange("p (g f) -> p g f", g=g, f=w)

        def ed(par, t, a, b):
            return q_ed[par][:, t * EW + a:t * EW + b]

        def bc_mid(ap, n):
            return ap.unsqueeze(1).to_broadcast([P, n, ap.shape[1]])

        def bc_last(ap, n):
            return ap.unsqueeze(2).to_broadcast([P, ap.shape[1], n])

        @block.sync
        def _(sp):
            sp.dma_start(wp[:, :], wpack).then_inc(s_w, 16)
            sp.dma_start(t_src[:, :], src).then_inc(s_tab_in, 16)
            sp.dma_start(t_dst[:, :], dst).then_inc(s_tab_in, 16)
            sp.wait_ge(s_fill, 2)
            sp.dma_start(t_next[0:P - 1, :], dst[1:P, :]).then_inc(s_tab_in, 16)
            sp.dma_start(t_next[P - 1:P, 0:T - 1], dst[0:1, 1:T]).then_inc(s_tab_in, 16)
            sp.dma_start(t_prev[P - 1:P, 1:T], dst[P - 1:P, 0:T - 1]).then_inc(s_tab_in, 16)
            sp.wait_ge(s_tabc, 6)
            sp.dma_start(src_tab.rearrange("q p c -> p q c"), t_src[:, :].rearrange("p (q c) -> p q c", c=GQ)).then_inc(s_tab_out, 16)
            sp.dma_start(dst_tab.rearrange("q p c -> p q c"), t_gat[:, :].rearrange("p (q c) -> p q c", c=GQ)).then_inc(s_tab_out, 16)
            sp.dma_start(put_tab.rearrange("q p c -> p q c"), t_put[:, :].rearrange("p (q c) -> p q c", c=GQ)).then_inc(s_tab_out, 16)
            sp.dma_start(key_tab.rearrange("q p c -> p q c"), f_key[:, :, :]).then_inc(s_tab_out, 16)
            sp.wait_ge(s_rowsb, 1)
            sp.dma_start(row_tab[0:TA, :], t_row[0][0:TA, :]).then_inc(s_tab_out, 16)
            n_out = 5
            if T > P:
                sp.wait_ge(s_rowsb, 2)
                sp.dma_start(row_tab[P:T, :], t_row[1][0:T - P, :]).then_inc(s_tab_out, 16)
                n_out = 6

            def net_load(q):
                wait(sp, n_tr, q.times(1, -1))
                sp.dma_start(q_sc[q.mod(2)][:, :], sc_q[q.times(1)]).then_inc(n_in[q.mod(2)], 16)

            def net_store(q):
                sp.wait_ge(n_act, q.times(1, 1))
                sp.dma_start(hid_tab[q.times(1)], q_hid[q.mod(2)][:, :]).then_inc(n_st[q.mod(2)], 16)

            net_load(At(0, 0, 2))
            net_load(At(0, 1, 2))
            net_store(At(0, 0, 2))
            with sp.Fori(0, (Q - 3) // 2) as i:
                for c in (2, 3):
                    net_load(At(i, c, 2))
                    net_store(At(i, c, 2) - 1)
            net_load(At(0, Q - 1, 2))
            net_store(At(0, Q - 2, 2))
            net_store(At(0, Q - 1, 2))
            sp.wait_ge(n_st[0], 16 * ((Q + 1) // 2))
            sp.wait_ge(n_st[1], 16 * (Q // 2))
            sp.wait_ge(s_tab_out, 16 * n_out)

            def x_load(u, last=False):
                wait(sp, d_x1, u.times(4, -4))
                sp.dma_start(x_in[u.mod(2)][:, :], x_l if last else x_u[u.times(1)]).then_inc(d_in[u.mod(2)], 16)

            def dense_store(u, last=False):
                j = u.mod(2)
                if last:
                    sp.wait_ge(d_sth[1 - j], 16 * (U // 2))
                    sp.wait_ge(d_sto[1 - j], 16 * (U // 2))
                sp.wait_ge(d_h1, u.times(1, 1))
                sp.dma_start(h_l if last else h_u[u.times(1)], h1[j][:, :]).then_inc(d_sth[j], 16)
                sp.wait_ge(d_y, u.times(1, 1))
                sp.dma_start(o_l if last else o_u[u.times(1)], yo[j][:, :]).then_inc(d_sto[j], 16)

            def p1_load(q):
                j = q.mod(2)
                wait(sp, e_tot, q.times(GQ, -GQ))
                sp.dma_start(i_src[j][:, :], src_tab[q.times(1)]).then_inc(e_ix[j], 16)
                sp.dma_start(q_key[j][:, :], key_tab[q.times(1)]).then_inc(e_tb[j], 16)
                sp.dma_start(q_ed[j][:, :], ed_q[q.times(1)]).then_inc(e_tb[j], 16)
                sp.dma_start(q_row[j][:, :], row_q[q.times(1)].partition_broadcast(P)).then_inc(e_tb[j], 16)
                sp.dma_start(q_hid[j][:, :], hid_tab[q.times(1)]).then_inc(e_hd[j], 16)

            def p1_store(q):
                sp.wait_ge(e_tot, q.times(GQ, GQ))
                sp.dma_start(sum_tab[q.times(1)], tot[q.mod(2)][:, :]).then_inc(e_st[q.mod(2)], 16)

            def step(u, store=True, load=True, nextlast=False, quad=True, nextquad=True, laststore=False):
                q = At(u.i, u.c // 2, 2)
                odd = u.mod(2) == 1 and quad
                if odd and nextquad:
                    p1_load(q + 1)
                if store:
                    dense_store(u - 2, laststore)
                if load:
                    x_load(u + 1, nextlast)
                if odd:
                    p1_store(q)

            p1_load(At(0, 0, 2))
            x_load(At(0, 0))
            for u in range(4):
                step(At(0, u), store=u >= 2)
            with sp.Fori(1, U // 4) as i:
                for c in range(4):
                    step(At(i, c))
            step(At(0, U - 2), nextlast=True)
            step(At(0, U - 1), load=False, nextquad=False)
            step(At(0, U), load=False, quad=False)
            step(At(0, U + 1), load=False, quad=False, laststore=True)
            for j in range(2):
                sp.wait_ge(e_st[j], 16 * ((Q + 1 - j) // 2))

            def p2_load(q):
                j = q.mod(2)
                wait(sp, r_g[j], q.over(2, 64))
                sp.dma_start(i_dst[j][:, :], dst_tab[q.times(1)]).then_inc(r_ix[j], 16)
                wait(sp, r_x1, q.times(2, -2))
                sp.dma_start(cv[j][:, :], sum_tab[q.times(1)]).then_inc(r_cv[j], 16)

            def p2_put(q):
                j = q.mod(2)
                wait(sp, r_put[j], q.over(2, 64))
                sp.dma_start(i_put[j][:, :], put_tab[q.times(1)]).then_inc(r_px[j], 16)

            def p2_store(q):
                sp.wait_ge(r_y, q.times(1, 1))
                sp.dma_start(y_tab[q.times(1)], yo[q.mod(2)][:, 0:GQ * D]).then_inc(r_sty[q.mod(2)], 16)

            def p2_step(q, load=True, put=True, store=True):
                if load:
                    p2_load(q + 1)
                if put:
                    p2_put(q - 1)
                if store:
                    p2_store(q - 2)

            p2_load(At(0, 0, 2))
            p2_step(At(0, 0, 2), put=False, store=False)
            p2_step(At(0, 1, 2), store=False)
            with sp.Fori(1, (Q - 1) // 2) as i:
                for c in range(2):
                    p2_step(At(i, c, 2))
            p2_step(At(0, Q - 1, 2), load=False)
            p2_step(At(0, Q, 2), load=False)
            p2_step(At(0, Q + 1, 2), load=False, put=False)
            for j in range(2):
                sp.wait_ge(r_sty[j], 16 * ((Q + 1 - j) // 2))
                sp.wait_ge(r_put[j], 64 * ((Q + 1 - j) // 2))

            def p3_load(q):
                j = q.mod(2)
                wait(sp, m_g[j], q.over(2, 64))
                sp.dma_start(i_src[j][:, :], src_tab[q.times(1)]).then_inc(m_ix[j], 16)
                wait(sp, m_o, q.times(GQ, -GQ))
                sp.dma_start(q_key[j][:, :], key_tab[q.times(1)]).then_inc(m_tb[j], 16)
                sp.dma_start(q_ed[j][:, :], ed_q[q.times(1)]).then_inc(m_tb[j], 16)
                sp.dma_start(q_row[j][:, :], row_q[q.times(1)].partition_broadcast(P)).then_inc(m_tb[j], 16)
                sp.dma_start(x1[j][:, 0:GQ * D], y_tab[q.times(1)]).then_inc(m_y[j], 16)
                wait(sp, m_put[j], q.over(2, 64))
                sp.dma_start(i_put[j][:, :], put_tab[q.times(1)]).then_inc(m_px[j], 16)

            p3_load(At(0, 0, 2))
            p3_load(At(0, 1, 2))
            with sp.Fori(1, (Q - 1) // 2) as i:
                for c in range(2):
                    p3_load(At(i, c, 2))
            p3_load(At(0, Q - 1, 2))
            for j in range(2):
                sp.wait_ge(m_put[j], 64 * ((Q + 1 - j) // 2))

        @block.gpsimd
        def _(pool):
            nc.gpsimd.memset(t_next[:, :], N + 5).then_inc(s_fill, 1)
            nc.gpsimd.memset(t_prev[:, :], -1).then_inc(s_fill, 1)
            nc.gpsimd.memset(ident[:, :], 0.0).then_inc(s_id, 1)
            pool.wait_ge(s_id, 1)
            nc.gpsimd.affine_select(out=ident[:, :], in_=ident[:, :], compare_op=ALU.not_equal, fill=1.0, base=0,
                                    pattern=[[-1, P]], channel_multiplier=1).then_inc(s_id, 1)

            def gather(rows, into, width, index, signal):
                pool.sem_inc(s_turn, 1)
                for t in range(GQ):
                    nc.gpsimd.indirect_dma_start(
                        into[:, t * width:(t + 1) * width], None, rows,
                        bass.IndirectOffsetOnAxis(ap=index[:, t:t + 1], axis=0)).then_inc(signal, 16)

            def scatter_tile(rows, tile, index, t, signal):
                pool.sem_inc(s_turn, 1)
                nc.gpsimd.indirect_dma_start(
                    rows, bass.IndirectOffsetOnAxis(ap=index[:, t:t + 1], axis=0), tile, None,
                    bounds_check=N - 1, oob_is_err=False).then_inc(signal, 16)

            def p1_gather(q):
                j = q.mod(2)
                pool.wait_ge(e_ix[j], q.over(2, 16, 16))
                wait(pool, e_tot, q.times(GQ, -GQ))
                gather(xa, x_e[j], XW, i_src[j], e_g[j])

            def dense_y(u):
                j = u.mod(2)
                pool.wait_ge(d_h1, u.times(1, 1))
                wait(pool, d_sto[j], u.over(2, 16))
                nc.gpsimd.tensor_tensor(yo[j][:, :], x1[j][:, :], h1[j][:, :], ALU.add).then_inc(d_y, 1)

            def step(u, y=True, nextquad=True):
                if u.mod(2) == 1 and nextquad:
                    p1_gather(At(u.i, u.c // 2, 2) + 1)
                if y:
                    dense_y(u - 2)

            p1_gather(At(0, 0, 2))
            for u in range(4):
                step(At(0, u), y=u >= 2)
            with pool.Fori(1, U // 4) as i:
                for c in range(4):
                    step(At(i, c))
            for u in range(U - 2, U + 2):
                step(At(0, u), nextquad=False)
            for j in range(2):
                pool.wait_ge(d_sth[j], 16 * (U // 2))
                pool.wait_ge(d_sto[j], 16 * (U // 2))

            def p2_gather(q):
                j = q.mod(2)
                pool.wait_ge(r_ix[j], q.over(2, 16, 16))
                wait(pool, r_x1, q.times(2, -2))
                gather(xa, x_e[j], XW, i_dst[j], r_g[j])

            def p2_scatter(q):
                j = q.mod(2)
                pool.wait_ge(r_px[j], q.over(2, 16, 16))
                pool.wait_ge(r_h1, q.times(1, 1))
                for t in range(GQ):
                    scatter_tile(h1_all, h1[j][:, t * D:(t + 1) * D], i_put[j], t, r_put[j])

            def p2_step(q, g=True, s=True):
                if g:
                    p2_gather(q + 1)
                if s:
                    p2_scatter(q - 2)

            pool.wait_ge(e_tot, Q * GQ)
            p2_gather(At(0, 0, 2))
            p2_step(At(0, 0, 2), s=False)
            p2_step(At(0, 1, 2), s=False)
            with pool.Fori(1, (Q - 1) // 2) as i:
                for c in range(2):
                    p2_step(At(i, c, 2))
            for q in range(Q - 1, Q + 2):
                p2_step(At(0, q, 2), g=False)
            for j in range(2):
                pool.wait_ge(r_put[j], 64 * ((Q + 1 - j) // 2))
            pool.wait_ge(r_y, Q)

            def p3_gather(q):
                j = q.mod(2)
                pool.wait_ge(m_ix[j], q.over(2, 16, 16))
                wait(pool, m_ft, q.times(GQ, -GQ))
                wait(pool, m_ss, q.times(GQ, -GQ))
                gather(h1_all, h1[j], D, i_src[j], m_g[j])

            def p3_scatter(q):
                j = q.mod(2)
                pool.wait_ge(m_px[j], q.over(2, 16, 16))
                for t in range(GQ):
                    pool.wait_ge(m_o, q.times(GQ, t + 1))
                    scatter_tile(out, yo[j][:, t * D:(t + 1) * D], i_put[j], t, m_put[j])

            p3_gather(At(0, 0, 2))
            p3_gather(At(0, 1, 2))
            p3_scatter(At(0, 0, 2))
            with pool.Fori(0, (Q - 3) // 2) as i:
                for c in (2, 3):
                    p3_gather(At(i, c, 2))
                    p3_scatter(At(i, c, 2) - 1)
            p3_gather(At(0, Q - 1, 2))
            p3_scatter(At(0, Q - 2, 2))
            p3_scatter(At(0, Q - 1, 2))

        @block.scalar
        def _(act):
            def net_copy(q):
                act.wait_ge(n_tr, q.times(1, 1))
                wait(act, n_mm, q.times(1, -1))
                nc.scalar.activation(fT[q.mod(2)][0:32, 0:P], bank[0 + q.mod(2)][0:32, 0:P], ACT.Copy).then_inc(n_te, 1)

            def net_silu(q):
                act.wait_ge(n_mm, q.times(1, 1))
                wait(act, n_st[q.mod(2)], q.over(2, 16))
                nc.scalar.activation(q_hid[q.mod(2)][:, :], bank[2 + q.mod(2)][:, 0:256], ACT.Silu,
                                     scale=8.0 ** -0.5).then_inc(n_act, 1)

            net_copy(At(0, 0, 2))
            net_copy(At(0, 1, 2))
            net_silu(At(0, 0, 2))
            with act.Fori(0, (Q - 3) // 2) as i:
                for c in (2, 3):
                    net_copy(At(i, c, 2))
                    net_silu(At(i, c, 2) - 1)
            net_copy(At(0, Q - 1, 2))
            net_silu(At(0, Q - 2, 2))
            net_silu(At(0, Q - 1, 2))

            def dense_h1(u, k):
                j = u.mod(2)
                if k == 0:
                    act.wait_ge(d_nmr, u.times(2, 2))
                    wait(act, d_y, u.times(1, -1))
                    wait(act, d_sth[j], u.over(2, 16))
                ins = nc.scalar.activation(h1[j][:, k * D:(k + 1) * D], x1[j][:, k * D:(k + 1) * D], ACT.Relu,
                                           bias=nmr2[j][:, k:k + 1], scale=inv2[j][:, k:k + 1])
                if k == GD - 1:
                    ins.then_inc(d_h1, 1)

            def dense_relu(u):
                j = u.mod(2)
                act.wait_ge(d_ln1, u.times(6, 3))
                for k in range(GD):
                    ins = nc.scalar.activation(hb[j][:, k * P:(k + 1) * P], x_in[j][:, k * XW + 32:k * XW + D], ACT.Relu,
                                               bias=neg1[j][:, k:k + 1])
                    if k % 4 == 3:
                        ins.then_inc(d_relu, 1)
                act.wait_ge(d_ln1, u.times(6, 5))
                nc.scalar.activation(sd1[j][:, :], var1[j][:, :], ACT.Sqrt).then_inc(d_sq1, 1)

            def dense_root2(u):
                j = u.mod(2)
                act.wait_ge(d_ln2, u.times(5, 5))
                nc.scalar.activation(sd2[j][:, :], var2[j][:, :], ACT.Sqrt).then_inc(d_sq2, 1)

            def dense_copy(u, h):
                act.wait_ge(d_tr, u.times(2, h + 1))
                wait(act, d_mm, u.times(4, 2 * h - 2))
                nc.scalar.activation(hT[h][:, :], bank[0][:, :], ACT.Copy)
                nc.scalar.activation(hR[h][:, :], bank[1][:, 0:P], ACT.Relu).then_inc(d_hT, 1)

            def p1_relu(q):
                j = q.mod(2)
                act.wait_ge(e_ln, q.times(6, 3))
                for t in range(GQ):
                    ins = nc.scalar.activation(h_e[:, t * P:(t + 1) * P], x_e[j][:, t * XW + 32:t * XW + D], ACT.Relu,
                                               bias=neg_e[j][:, t:t + 1])
                ins.then_inc(e_relu, 1)
                act.wait_ge(e_ln, q.times(6, 5))
                nc.scalar.activation(sd_e[j][:, :], var_e[j][:, :], ACT.Sqrt).then_inc(e_sq, 1)

            def p1_copy(q):
                act.wait_ge(e_tr, q.times(1, 1))
                wait(act, e_pw, q.times(GQ))
                nc.scalar.activation(eT[:, :], bank[4][:, :], ACT.Copy)
                nc.scalar.activation(eR[:, :], bank[1][:, P:2 * P], ACT.Relu).then_inc(e_hT, 1)

            def p1_slot(q, k):
                if k < GQ:
                    n = k
                    act.wait_ge(e_pw, q.times(GQ, n + 1))
                    if k == 0:
                        act.wait_ge(e_scl, q.times(2, 2))
                    wait(act, e_ft, q.times(GQ, n - 1))
                    nc.scalar.activation(g_e[n % 2][:, :], bank[5 + n % 2][:, 0:D], ACT.Copy,
                                         scale=scl_e[q.mod(2)][:, n:n + 1]).then_inc(e_gg, 1)
                if 0 <= k - 2 < GQ:
                    n = k - 2
                    act.wait_ge(e_u, q.times(GQ, n + 1))
                    wait(act, e_v, q.times(GQ, n - 1))
                    nc.scalar.activation(xr[n % 2][:, 0:65], bank[7][:, U_B:U_B + 65], ACT.Copy).then_inc(e_xb, 1)
                if 0 <= k - 1 < GQ:
                    n = k - 1
                    act.wait_ge(e_ftr, q.times(GQ, n + 1))
                    wait(act, e_u, q.times(GQ, n - 1))
                    nc.scalar.activation(fT[n % 2][:, 0:384], bank[4][:, 0:384], ACT.Copy).then_inc(e_fte, 1)
                if 0 <= k - 3 < GQ:
                    n = k - 3
                    act.wait_ge(e_seg, q.times(GQ, n + 1))
                    if n == 0:
                        wait(act, e_st[q.mod(2)], q.over(2, 16))
                    nc.scalar.activation(tot[q.mod(2)][:, n * CW:(n + 1) * CW], bank[1][:, U_SEG:U_SEG + CW],
                                         ACT.Copy).then_inc(e_tot, 1)

            def step(u, h=True, b=True, root2=True, quad=True):
                q = At(u.i, u.c // 2, 2)
                for k in range(GD):
                    if h:
                        dense_h1(u - 2, k)
                    if u.mod(2) == 1 and quad:
                        p1_slot(q, k)
                if b:
                    dense_relu(u)
                if u.mod(2) == 0 and quad:
                    p1_relu(q)
                if root2:
                    dense_root2(u - 1)
                if b:
                    dense_copy(u, 0)
                    dense_copy(u, 1)
                if u.mod(2) == 0 and quad:
                    p1_copy(q)

            for u in range(4):
                step(At(0, u), h=u >= 2, root2=u >= 1)
            with act.Fori(1, U // 4) as i:
                for c in range(4):
                    step(At(i, c))
            for u in range(U - 2, U):
                step(At(0, u))
            step(At(0, U), b=False, quad=False)
            step(At(0, U + 1), b=False, root2=False, quad=False)

            def p2_h1(q):
                j = q.mod(2)
                act.wait_ge(r_nmr, q.times(2, 2))
                wait(act, r_y, q.times(1, -1))
                wait(act, r_put[j], q.over(2, 64))
                for t in range(GQ):
                    ins = nc.scalar.activation(h1[j][:, t * D:(t + 1) * D], x1[j][:, t * D:(t + 1) * D], ACT.Relu,
                                               bias=nmr2[j][:, t:t + 1], scale=inv2[j][:, t:t + 1])
                ins.then_inc(r_h1, 1)

            def p2_relu(q):
                j = q.mod(2)
                act.wait_ge(r_ln1, q.times(6, 3))
                for t in range(GQ):
                    ins = nc.scalar.activation(h_e[:, t * P:(t + 1) * P], x_e[j][:, t * XW + 32:t * XW + D], ACT.Relu,
                                               bias=neg_e[j][:, t:t + 1])
                ins.then_inc(r_relu, 1)

            def p2_copy(q):
                act.wait_ge(r_tr, q.times(1, 1))
                wait(act, r_mm, q.times(1))
                nc.scalar.activation(eT[:, :], bank[0][:, :], ACT.Copy)
                nc.scalar.activation(eR[:, :], bank[1][:, 0:P], ACT.Relu).then_inc(r_hT, 1)

            def p2_root1(q):
                j = q.mod(2)
                act.wait_ge(r_ln1, q.times(6, 5))
                nc.scalar.activation(sd_e[j][:, :], var_e[j][:, :], ACT.Sqrt).then_inc(r_sq1, 1)

            def p2_root2(q):
                j = q.mod(2)
                act.wait_ge(r_ln2, q.times(5, 5))
                nc.scalar.activation(sd2[j][:, 0:GQ], var2[j][:, 0:GQ], ACT.Sqrt).then_inc(r_sq2, 1)

            def p2_sines(q):
                j = q.mod(2)
                act.wait_ge(r_ang, q.times(8, 8))
                nc.scalar.activation(trig[4][j][:, :], trig[3][j][:, :], ACT.Sin).then_inc(r_sin, 1)

            def p2_step(q, a=True, root2=True, h=True):
                if h:
                    p2_h1(q - 2)
                if a:
                    p2_relu(q)
                    p2_copy(q)
                    p2_root1(q)
                if root2:
                    p2_root2(q - 1)
                if a:
                    p2_sines(q)

            p2_step(At(0, 0, 2), root2=False, h=False)
            p2_step(At(0, 1, 2), h=False)
            p2_step(At(0, 2, 2))
            p2_step(At(0, 3, 2))
            with act.Fori(2, (Q - 1) // 2) as i:
                for c in range(2):
                    p2_step(At(i, c, 2))
            p2_step(At(0, Q - 1, 2))
            p2_step(At(0, Q, 2), a=False)
            p2_step(At(0, Q + 1, 2), a=False, root2=False)

            def p3_scalars(n):
                if n.mod(4) == 0:
                    act.wait_ge(m_g[n.c // 4 % 2], n.over(8, 64, 64))
                wait(act, m_ftr, n.times(1, -1))
                j = n.c // 4 % 2
                t = n.mod(4)
                nc.scalar.activation(feat[n.mod(2)][:, 448:512], h1[j][:, t * D:t * D + DS], ACT.Copy).then_inc(m_ss, 1)

            def p3_featT(n):
                act.wait_ge(m_ftr, n.times(1, 1))
                wait(act, m_u, n.times(1, -1))
                nc.scalar.activation(fT[n.mod(2)][:, :], bank[n.mod(2)][:, :], ACT.Copy).then_inc(m_fte, 1)

            def p3_smsg(n):
                act.wait_ge(m_u, n.times(1, 1))
                wait(act, m_seg, n.times(1, -1))
                nc.scalar.activation(v_e[n.mod(2)][:, 0:DS], bank[2 + n.mod(2)][:, 0:DS], ACT.Copy).then_inc(m_cs, 1)

            def p3_total(n):
                act.wait_ge(m_seg, n.times(1, 1))
                nc.scalar.activation(tot[n.mod(2)][:, 0:D], bank[4 + n.mod(2)][:, 0:D], ACT.Copy).then_inc(m_tot, 1)

            def p3_slot(n, lo=0, hi=4):
                if hi > 0 and lo <= 0:
                    p3_scalars(n)
                if lo <= 2 < hi:
                    p3_smsg(n - 2)
                if lo <= 1 < hi:
                    p3_featT(n - 1)
                if lo <= 3 < hi:
                    p3_total(n - 3)

            for n in range(8):
                p3_slot(At(0, n, 8), 0, n + 1)
            with act.Fori(1, (Q - 1) // 2) as i:
                for c in range(8):
                    p3_slot(At(i, c, 8))
            for n in range(T - GQ, T + 3):
                p3_slot(At(0, n, 8), max(0, n - T + 1))

        @block.tensor
        def _(pe):
            def transpose_rows(main, rest, ps_main, ps_rest, tr_sem):
                for t in range(GQ):
                    nc.tensor.transpose(ps_main[:, t * P:(t + 1) * P], main[:, t * P:(t + 1) * P], ident[:, :])
                nc.tensor.transpose(ps_rest, rest, ident[:, :]).then_inc(tr_sem, 1)

            def linear(dst_ps, main, rest, w, t):
                nc.tensor.matmul(dst_ps, main[:, t * P:(t + 1) * P], wp[:, w:w + D], start=True, stop=False)
                return nc.tensor.matmul(dst_ps[:, 0:DS], rest[:, :], wp[:, w + D + t * DS:w + D + (t + 1) * DS],
                                        start=False, stop=True)

            pe.wait_ge(s_id, 2)
            pe.wait_ge(s_tabc, 1)
            nc.tensor.transpose(bank[6][0:TA, 0:P], f_dst[:, 0:TA], ident[:, :]).then_inc(s_rowps, 1)
            if T > P:
                nc.tensor.transpose(bank[7][0:T - P, 0:P], f_dst[:, P:T], ident[:, :]).then_inc(s_rowps, 1)

            pe.wait_ge(s_w, 16)
            pieces = [(b, W_W1T, 64, b, W_WS, 64) for b in (0, 1)] \
                + [(2 + b, W_W4T, 96, b, W_WVK, 96) for b in range(3)] \
                + [(5 + b, W_W2T, 64, b, W_WS, 64) for b in range(3)] \
                + [(8 + b, W_W5T, 96, b, W_WVA, 96) for b in range(3)] \
                + [(11 + b, W_W5T, 96, b, W_WVB, 96) for b in range(3)] \
                + [(14 + b, W_W3T, 32, b, W_WV, 32) for b in (0, 1)]
            for r, wl, kk, b, wr, cols in pieces:
                where = 32 * (r % 4)
                nc.tensor.matmul(bank[r // 4][where:where + 32, 0:cols],
                                 wp[0:kk, wl + 32 * b:wl + 32 * (b + 1)], wp[0:kk, wr:wr + cols],
                                 start=True, stop=True).then_inc(s_mp, 1)
            pe.wait_ge(s_mc, 1)
            pe.wait_ge(s_wscaled, 1)

            def net_tr(q):
                pe.wait_ge(n_in[q.mod(2)], q.over(2, 16, 16))
                wait(pe, n_te, q.times(1, -1))
                nc.tensor.transpose(bank[q.mod(2)][0:32, 0:P],
                                    q_sc[q.mod(2)][:, :], ident[:, :]) \
                    .then_inc(n_tr, 1)

            def net_mm(q):
                pe.wait_ge(n_te, q.times(1, 1))
                wait(pe, n_act, q.times(1, -1))
                for h in range(2):
                    ins = nc.tensor.matmul(bank[2 + q.mod(2)][:, h * P:(h + 1) * P],
                                           wp[0:32, W_FC1 + h * P:W_FC1 + (h + 1) * P], fT[q.mod(2)][0:32, 0:P],
                                           start=True, stop=True)
                ins.then_inc(n_mm, 1)

            net_tr(At(0, 0, 2))
            net_tr(At(0, 1, 2))
            net_mm(At(0, 0, 2))
            with pe.Fori(0, (Q - 3) // 2) as i:
                for c in (2, 3):
                    net_tr(At(i, c, 2))
                    net_mm(At(i, c, 2) - 1)
            net_tr(At(0, Q - 1, 2))
            net_mm(At(0, Q - 2, 2))
            net_mm(At(0, Q - 1, 2))
            pe.wait_ge(n_act, Q)

            def dense_mm(u, k):
                h, pair = k // 4, k // 2
                if k % 4 == 0:
                    pe.wait_ge(d_hT, u.times(2, h + 1))
                if k % 2 == 0:
                    wait(pe, d_x1, u.times(4, pair - 1))
                ins = linear(bank[2 + k % 4 // 2][:, k % 2 * D:(k % 2 + 1) * D], hT[h], hR[h], W_SC, k % 4)
                if k % 2 == 1:
                    ins.then_inc(d_mm, 1)

            def dense_tr(u, h):
                pe.wait_ge(d_relu, u.times(2, h + 1))
                wait(pe, d_hT, u.times(2, h))
                if h == 0:
                    if u.mod(2) == 1:
                        pe.wait_ge(e_tot, u.over(2, GQ, GQ))
                    else:
                        wait(pe, e_hT, u.over(2))
                pe.wait_ge(d_ln1, u.times(6, 6))
                j = u.mod(2)
                transpose_rows(hb[j][:, h * 4 * P:(h + 1) * 4 * P], hr[j][:, h * P:(h + 1) * P], bank[0],
                               bank[1][:, 0:P], d_tr)

            def p1_tr(q):
                pe.wait_ge(e_relu, q.times(1, 1))
                wait(pe, e_fte, q.times(GQ))
                pe.wait_ge(d_hT, q.times(4, 2))
                pe.wait_ge(e_ln, q.times(6, 6))
                transpose_rows(h_e[:, :], hr_e[q.mod(2)][:, :], bank[4], bank[1][:, P:2 * P], e_tr)

            def p1_slot(q, k):
                j = q.mod(2)
                if 0 <= k - 2 < GQ:
                    n = k - 2
                    pe.wait_ge(e_fte, q.times(GQ, n + 1))
                    wait(pe, e_v, q.times(GQ, n))
                    f = fT[n % 2]
                    nc.tensor.matmul(bank[7][:, U_C:U_C + 97], f[:, 0:P], wp[:, W_R1:W_R1 + 97], start=True, stop=True)
                    nc.tensor.matmul(bank[7][:, U_D:U_D + 161], f[:, P:2 * P], wp[:, W_R2:W_R2 + 161],
                                     start=True, stop=False)
                    nc.tensor.matmul(bank[7][:, U_B:U_B + 65], f[:, 2 * P:3 * P], wp[:, W_R3:W_R3 + 65],
                                     start=False, stop=True).then_inc(e_u, 1)
                if k < GQ:
                    n = k
                    if k == 0:
                        pe.wait_ge(e_hT, q.times(1, 1))
                        pe.wait_ge(e_hd[j], q.over(2, 16, 16))
                    wait(pe, e_ft, q.times(GQ, n - 1))
                    linear(bank[5 + n % 2][:, 0:D], eT, eR, W_L1, n)
                    nc.tensor.matmul(bank[5 + n % 2][:, D:D + 192], q_hid[j][:, n // 2 * P:(n // 2 + 1) * P],
                                     wp[:, W_FC2 + n % 2 * 192:W_FC2 + (n % 2 + 1) * 192],
                                     start=True, stop=True).then_inc(e_pw, 1)
                if 0 <= k - 1 < GQ:
                    n = k - 1
                    pe.wait_ge(e_ft, q.times(GQ, n + 1))
                    pe.wait_ge(e_hT, q.times(1, 1))
                    wait(pe, e_fte, q.times(GQ, n))
                    for c, at in enumerate((0, 128, 192)):
                        ins = nc.tensor.transpose(bank[4][:, c * P:(c + 1) * P], feat[n % 2][:, at:at + P], ident[:, :])
                    ins.then_inc(e_ftr, 1)
                if 0 <= k - 3 < GQ:
                    n = k - 3
                    if n == 0:
                        pe.wait_ge(e_sc, q.times(1, 1))
                        pe.wait_ge(d_hT, q.times(4, 2))
                        pe.wait_ge(e_hT, q.times(1, 1))
                    pe.wait_ge(e_v, q.times(GQ, n + 1))
                    wait(pe, e_tot, q.times(GQ, n))
                    before = tot[j][:, (n - 1) * CW:n * CW] if n else tot[1 - j][:, (GQ - 1) * CW:GQ * CW]
                    nc.tensor.matmul(bank[1][:, U_SEG:U_SEG + CW], same[n][j][:, :], v_e[n % 2][:, :],
                                     start=True, stop=False)
                    nc.tensor.matmul(bank[1][:, U_SEG:U_SEG + CW], carry[n][j][:, :], before,
                                     start=False, stop=True).then_inc(e_seg, 1)

            def step(u, mm=True, tr=True, quad=True):
                q = At(u.i, u.c // 2, 2)
                for k in range(GD):
                    if mm and k == 0:
                        for kk in range(4):
                            dense_mm(u - 1, kk)
                    if mm and k in (2, 4):
                        dense_mm(u - 1, k + 2)
                        dense_mm(u - 1, k + 3)
                    if u.mod(2) == 1 and quad:
                        p1_slot(q, k)
                if tr:
                    dense_tr(u, 0)
                    dense_tr(u, 1)
                if u.mod(2) == 0 and quad:
                    p1_tr(q)

            pe.wait_ge(e_z, 1)
            for u in range(4):
                step(At(0, u), mm=u >= 1)
            with pe.Fori(1, U // 4) as i:
                for c in range(4):
                    step(At(i, c))
            for u in range(U - 2, U):
                step(At(0, u))
            step(At(0, U), tr=False, quad=False)

            def p2_step(q):
                j = q.mod(2)
                pe.wait_ge(r_relu, q.times(1, 1))
                wait(pe, r_hT, q.times(1))
                pe.wait_ge(r_ln1, q.times(6, 6))
                transpose_rows(h_e[:, :], hr_e[j][:, :], bank[0], bank[1][:, 0:P], r_tr)
                pe.wait_ge(r_hT, q.times(1, 1))
                wait(pe, r_x1, q.times(2, -2))
                for t in range(GQ):
                    ins = linear(bank[2 + 2 * j + t // 2][:, t % 2 * D:(t % 2 + 1) * D], eT, eR, W_SC, t)
                ins.then_inc(r_mm, 1)

            pe.wait_ge(d_x1, 4 * U)
            for q in range(2):
                p2_step(At(0, q, 2))
            with pe.Fori(1, (Q - 1) // 2) as i:
                for c in range(2):
                    p2_step(At(i, c, 2))
            p2_step(At(0, Q - 1, 2))
            pe.wait_ge(r_x1, 2 * Q)
            pe.wait_ge(m_z, 1)

            def p3_tr(n):
                pe.wait_ge(m_ft, n.times(1, 1))
                pe.wait_ge(m_ss, n.times(1, 1))
                wait(pe, m_fte, n.times(1, -1))
                for c in range(4):
                    ins = nc.tensor.transpose(bank[n.mod(2)][:, c * P:(c + 1) * P],
                                              feat[n.mod(2)][:, c * P:(c + 1) * P], ident[:, :])
                ins.then_inc(m_ftr, 1)

            def p3_parts(n):
                pe.wait_ge(m_fte, n.times(1, 1))
                wait(pe, m_v, n.times(1, -1))
                f, b = fT[n.mod(2)], bank[2 + n.mod(2)]
                nc.tensor.matmul(b[:, D:D + DU], f[:, 3 * P:4 * P], msg1s[:, :], start=True, stop=True)
                nc.tensor.matmul(b[:, 0:D], f[:, 0:P], msg1[0][:, :], start=True, stop=False)
                nc.tensor.matmul(b[:, 0:D], f[:, P:2 * P], msg1[1][:, :], start=False, stop=False)
                nc.tensor.matmul(b[:, DS:D], f[:, 2 * P:3 * P], msg1[2][:, :], start=False, stop=False)
                nc.tensor.matmul(b[:, DS:D], f[:, 3 * P:4 * P], msg1[3][:, :], start=False, stop=True).then_inc(m_u, 1)

            def p3_sum(n):
                j, t = n.c // 4 % 2, n.mod(4)
                if t == 0:
                    pe.wait_ge(m_sc, n.over(4, 1, 1))
                pe.wait_ge(m_v, n.times(1, 1))
                wait(pe, m_tot, n.times(1))
                wait(pe, m_o, n.times(1, -1))
                b = bank[4 + n.mod(2)]
                nc.tensor.matmul(b[:, 0:D], same[t][j][:, :], v_e[n.mod(2)][:, 0:D], start=True, stop=False)
                nc.tensor.matmul(b[:, 0:D], carry[t][j][:, :], tot[1 - n.mod(2)][:, 0:D],
                                 start=False, stop=True).then_inc(m_seg, 1)

            def p3_slot(n, lo=0, hi=4):
                if lo <= 2 < hi:
                    p3_parts(n - 2)
                if lo <= 1 < hi:
                    p3_tr(n - 1)
                if lo <= 3 < hi:
                    p3_sum(n - 3)

            for n in range(8):
                p3_slot(At(0, n, 8), 0, n + 1)
            with pe.Fori(1, (Q - 1) // 2) as i:
                for c in range(8):
                    p3_slot(At(i, c, 8))
            for n in range(T - GQ, T + 3):
                p3_slot(At(0, n, 8), max(0, n - T + 1))

        @block.vector
        def _(v):
            V = nc.vector

            def moments(st, su, df, sq, m2, neg, var, n, signal, base):
                v.wait_ge(signal, base(1))
                V.tensor_tensor(su[:, 0:n, :], st[:, 0:n, 1:3], st[:, 0:n, 4:6], ALU.add)
                V.tensor_tensor(df[:, 0:n], st[:, 0:n, 1], st[:, 0:n, 4], ALU.subtract).then_inc(signal, 1)
                v.wait_ge(signal, base(2))
                V.tensor_scalar(neg[:, 0:n], su[:, 0:n, 0], -0.5, None, ALU.mult)
                V.tensor_tensor(sq[:, 0:n], df[:, 0:n], df[:, 0:n], ALU.mult).then_inc(signal, 1)
                v.wait_ge(signal, base(3))
                V.scalar_tensor_tensor(m2[:, 0:n], sq[:, 0:n], D / 4.0, su[:, 0:n, 1], ALU.mult, ALU.add) \
                    .then_inc(signal, 1)
                v.wait_ge(signal, base(4))
                V.tensor_scalar(var[:, 0:n], m2[:, 0:n], 1.0 / D, EPS, ALU.mult, ALU.add).then_inc(signal, 1)

            def rest_of(into, rows, neg, n, signal):
                V.tensor_tensor(x3(into, 32, n), x3(rows, XW, n)[:, :, 0:32], bc_last(neg[:, 0:n], 32), ALU.add) \
                    .then_inc(signal, 1)

            v.wait_ge(s_tab_in, 80)
            V.tensor_copy(f_dst[:, :], t_dst[:, :]).then_inc(s_tabc, 1)
            V.tensor_copy(f_next[:, :], t_next[:, :])
            V.tensor_copy(f_key[:, :, GQ:2 * GQ], t_prev[:, :].rearrange("p (q c) -> p q c", c=GQ)).then_inc(s_tabc, 1)
            v.wait_ge(s_tabc, 2)
            V.tensor_copy(f_key[:, :, 0:GQ], f_dst[:, :].rearrange("p (q c) -> p q c", c=GQ))
            V.tensor_scalar(t_gat[:, :], f_dst[:, :], float(N - 1), None, ALU.min)
            V.tensor_tensor(f_put[:, :], f_dst[:, :], f_next[:, :], ALU.is_equal).then_inc(s_tabc, 1)
            v.wait_ge(s_tabc, 3)
            V.scalar_tensor_tensor(f_next[:, :], f_put[:, :], float(FAR), f_dst[:, :], ALU.mult, ALU.add) \
                .then_inc(s_tabc, 1)
            v.wait_ge(s_tabc, 4)
            V.tensor_copy(t_put[:, :], f_next[:, :]).then_inc(s_tabc, 2)
            v.wait_ge(s_rowps, 1)
            V.tensor_copy(t_row[0][0:TA, :], bank[6][0:TA, 0:P]).then_inc(s_rowsb, 1)
            if T > P:
                v.wait_ge(s_rowps, 2)
                V.tensor_copy(t_row[1][0:T - P, :], bank[7][0:T - P, 0:P]).then_inc(s_rowsb, 1)

            v.wait_ge(s_w, 16)
            V.memset(msg1[0][:, :], 0.0)
            V.memset(msg1[1][:, :], 0.0)
            V.memset(msg1s[:, :], 0.0).then_inc(s_mz, 1)
            LS, LV, I3, I6 = DS ** -0.5, DU ** -0.5, 3.0 ** -0.5, 6.0 ** -0.5
            C0, C1 = (DS + DU) ** -0.5, (3.0 / (DS + 2 * DU)) ** 0.5
            v.wait_ge(s_mz, 1)
            v.wait_ge(s_mp, 16)

            def piece(r, cols, into, at, factor):
                w = 32 * (r % 4)
                return V.tensor_scalar(into[w:w + 32, at:at + cols], bank[r // 4][w:w + 32, 0:cols], factor, None, ALU.mult)

            for r in range(16):
                if r < 2:
                    ins = piece(r, DS, msg1[0], 0, C0 * LS)
                elif r < 4:
                    ins = piece(r, DV, msg1[0], DS, C1 * I3 * LV)
                elif r < 5:
                    ins = piece(r, DV, msg1[1], DS, C1 * I3 * LV)
                elif r < 8:
                    ins = piece(r, DS, msg1[1], 0, C0 * I3 * LS)
                elif r < 11:
                    ins = piece(r, DV, msg1[2], 0, C1 * I6 * LV)
                elif r < 12:
                    ins = piece(r, DV, msg1[2], 0, -C1 * I6 * LV)
                elif r < 14:
                    ins = piece(r, DV, msg1[3], 0, -C1 * I6 * LV)
                else:
                    ins = piece(r, DU, msg1s, 0, C1 * I3 * LV)
            V.memset(msg1[3][DS:P, :], 0.0).then_inc(s_mc, 1)
            for w in (W_SC, W_L1):
                V.tensor_scalar(wp[:, w:w + DS], wp[:, w:w + DS], LS, None, ALU.mult)
                V.tensor_scalar(wp[:, w + DS:w + D], wp[:, w + DS:w + D], LV, None, ALU.mult)
                V.tensor_scalar(wp[:, w + D:w + D + 4 * DS], wp[:, w + D:w + D + 4 * DS], LS, None, ALU.mult)
            V.tensor_scalar(wp[:, W_FC2:W_FC2 + 384], wp[:, W_FC2:W_FC2 + 384], DS ** -0.5, None, ALU.mult)
            FS = 0.25 * float(DV) ** -0.5
            V.tensor_scalar(wp[:, W_R1:W_R1 + 32], wp[:, W_R1:W_R1 + 32], FS, None, ALU.mult)
            V.tensor_scalar(wp[:, W_R1 + 32:W_R1 + 33], wp[:, W_R1 + 32:W_R1 + 33], 0.1 * FS, None, ALU.mult)
            V.tensor_scalar(wp[:, W_R1 + 33:W_R1 + 97], wp[:, W_R1 + 33:W_R1 + 97], FS, None, ALU.mult)
            V.tensor_scalar(wp[:, W_R2:W_R2 + 96], wp[:, W_R2:W_R2 + 96], FS, None, ALU.mult)
            for w in (W_R2 + 96, W_R3):
                V.tensor_scalar(wp[:, w:w + 1], wp[:, w:w + 1], 0.1 * FS * I3, None, ALU.mult)
                V.tensor_scalar(wp[:, w + 1:w + 65], wp[:, w + 1:w + 65], FS * I3, None, ALU.mult)
            V.memset(tot[1][:, :], 0.0).then_inc(s_wscaled, 1)
            v.wait_ge(s_wscaled, 1)
            V.memset(df1[0][:, :], 0.0).then_inc(e_z, 1)
            v.wait_ge(e_z, 1)

            def dense_stats(u):
                j = u.mod(2)
                v.wait_ge(d_in[j], u.over(2, 16, 16))
                for k in range(GD):
                    ins = V.bn_stats(st1[j][:, k, :], x_in[j][:, k * XW:k * XW + D])
                ins.then_inc(d_ln1, 1)
                moments(st1[j], su1[j], df1[j], sq1[j], m2a[j], neg1[j], var1[j], GD, d_ln1, lambda n: u.times(6, n))
                rest_of(hr[j], x_in[j], neg1[j], GD, d_ln1)

            def dense_scale(u):
                j = u.mod(2)
                v.wait_ge(d_sq1, u.times(1, 1))
                V.reciprocal(inv1[j][:, :], sd1[j][:, :]).then_inc(d_scl, 1)
                v.wait_ge(d_scl, u.times(2, 1))
                V.tensor_tensor(scl1[j][:, :], inv1[j][:, :], x3(x_in[j], XW, GD)[:, :, D], ALU.mult).then_inc(d_scl, 1)
                v.wait_ge(d_scl, u.times(2, 2))
                wait(v, d_y, u.times(1, -1))

            def dense_x1(u, k):
                j, pair = u.mod(2), k // 2
                if k % 2 == 0:
                    v.wait_ge(d_mm, u.times(4, pair + 1))
                ins = V.scalar_tensor_tensor(x1[j][:, k * D:(k + 1) * D], bank[2 + k % 4 // 2][:, k % 2 * D:(k % 2 + 1) * D],
                                             scl1[j][:, k:k + 1], x_in[j][:, k * XW:k * XW + D], ALU.mult, ALU.add)
                if k % 2 == 1:
                    ins.then_inc(d_x1, 1)
                    v.wait_ge(d_x1, u.times(4, pair + 1))
                    for kk in (k - 1, k):
                        ins = V.bn_stats(st2[j][:, kk, :], x1[j][:, kk * D:(kk + 1) * D])
                    if k == GD - 1:
                        ins.then_inc(d_ln2, 1)

            def dense_moments2(u):
                j = u.mod(2)
                moments(st2[j], su2[j], df2[j], sq2[j], m2b[j], neg2[j], var2[j], GD, d_ln2, lambda n: u.times(5, n))

            def dense_norm2(u):
                j = u.mod(2)
                v.wait_ge(d_sq2, u.times(1, 1))
                V.reciprocal(inv2[j][:, :], sd2[j][:, :]).then_inc(d_nmr, 1)
                v.wait_ge(d_nmr, u.times(2, 1))
                V.tensor_tensor(nmr2[j][:, :], neg2[j][:, :], inv2[j][:, :], ALU.mult).then_inc(d_nmr, 1)

            def selectors(j, loaded, value, signal):
                v.wait_ge(loaded, value)
                for t in range(GQ):
                    V.tensor_scalar(same[t][j][:, :], q_row[j][:, t * P:(t + 1) * P], q_key[j][:, t:t + 1], None,
                                    ALU.is_equal)
                    ins = V.tensor_scalar(carry[t][j][:, :], q_row[j][:, t * P:(t + 1) * P],
                                          q_key[j][:, GQ + t:GQ + t + 1], None, ALU.is_equal)
                ins.then_inc(signal, 1)

            def p1_prepare(q):
                j = q.mod(2)
                v.wait_ge(e_g[j], q.over(2, 64, 64))
                for t in range(GQ):
                    ins = V.bn_stats(st_e[j][:, t, :], x_e[j][:, t * XW:t * XW + D])
                ins.then_inc(e_ln, 1)
                moments(st_e[j], su_e[j], df_e[j], sq_e[j], m2_e[j], neg_e[j], var_e[j], GQ, e_ln,
                        lambda n: q.times(6, n))
                rest_of(hr_e[j], x_e[j], neg_e[j], GQ, e_ln)
                selectors(j, e_tb[j], q.over(2, 48, 48), e_sc)

            def p1_scale(q):
                j = q.mod(2)
                v.wait_ge(e_sq, q.times(1, 1))
                V.reciprocal(inv_e[j][:, :], sd_e[j][:, :]).then_inc(e_scl, 1)
                v.wait_ge(e_scl, q.times(2, 1))
                V.tensor_tensor(scl_e[j][:, :], inv_e[j][:, :], x3(x_e[j], XW, GQ)[:, :, D], ALU.mult).then_inc(e_scl, 1)

            def p1_slot(q, k):
                j = q.mod(2)
                if 0 <= k - 2 < GQ:
                    n = k - 2
                    v.wait_ge(e_xb, q.times(GQ, n + 1))
                    x = xr[n % 2]
                    V.tensor_tensor(x[:, 65:161].rearrange("p (u i) -> p u i", i=3), bc_last(bank[7][:, U_C:U_C + DU], 3),
                                    bc_mid(ed(j, n, 1, 4), DU), ALU.mult).then_inc(e_vx, 1)
                    v.wait_ge(e_vx, q.times(GQ, n + 1))
                    wait(v, e_seg, q.times(GQ, n - 1))
                    V.scalar_tensor_tensor(v_e[n % 2][:, :], bank[7][:, U_A:U_A + CW], ed(j, n, 0, 1), x[:, :],
                                           ALU.mult, ALU.add).then_inc(e_v, 1)
                if k < GQ:
                    n = k
                    v.wait_ge(e_gg, q.times(GQ, n + 1))
                    wait(v, e_ftr, q.times(GQ, n - 1))
                    g, w, f = g_e[n % 2], bank[5 + n % 2][:, D:D + 192], feat[n % 2]
                    V.tensor_tensor(f[:, 0:128].rearrange("p (a u) -> p a u", a=2), w[:, 0:128].rearrange("p (a u) -> p a u", a=2),
                                    bc_mid(g[:, 0:DS], 2), ALU.mult)
                    V.tensor_tensor(f[:, 128:320].rearrange("p (a u i) -> p a u i", a=2, i=3),
                                    w[:, 128:192].rearrange("p (a u) -> p a u", a=2).unsqueeze(3).to_broadcast([P, 2, DU, 3]),
                                    g[:, DS:D].rearrange("p (u i) -> p u i", i=3).unsqueeze(1).to_broadcast([P, 2, DU, 3]),
                                    ALU.mult).then_inc(e_fm, 1)
                    v.wait_ge(e_fm, q.times(GQ, n + 1))
                    V.tensor_tensor(f[:, 224:320].rearrange("p (u i) -> p u i", i=3),
                                    f[:, 224:320].rearrange("p (u i) -> p u i", i=3),
                                    bc_mid(ed(j, n, 1, 4), DU), ALU.mult).then_inc(e_ft, 1)

            def step(u, a=True, d=True, quad=True):
                q = At(u.i, u.c // 2, 2)
                odd = u.mod(2) == 1
                if a:
                    dense_stats(u)
                if quad and odd:
                    p1_scale(q)
                if quad and not odd:
                    p1_prepare(q)
                if d:
                    dense_scale(u - 1)
                for k in range(GD):
                    if d:
                        dense_x1(u - 1, k)
                    if quad and odd:
                        p1_slot(q, k)
                if d:
                    dense_moments2(u - 1)
                    dense_norm2(u - 1)

            for u in range(4):
                step(At(0, u), d=u >= 1)
            with v.Fori(1, U // 4) as i:
                for c in range(4):
                    step(At(i, c))
            for u in range(U - 2, U):
                step(At(0, u))
            step(At(0, U), a=False, quad=False)

            PI2 = 6.283185307179586
            CA = 6.28125
            CB = 0.0019350051879882812
            CC = PI2 - CA - CB
            ROUND = 1.5 * 2.0 ** 23
            PI_IN = 3.1415925

            def p2_prepare(q):
                j = q.mod(2)
                v.wait_ge(r_g[j], q.over(2, 64, 64))
                for t in range(GQ):
                    ins = V.bn_stats(st_e[j][:, t, :], x_e[j][:, t * XW:t * XW + D])
                ins.then_inc(r_ln1, 1)
                moments(st_e[j], su_e[j], df_e[j], sq_e[j], m2_e[j], neg_e[j], var_e[j], GQ, r_ln1,
                        lambda n: q.times(6, n))
                rest_of(hr_e[j], x_e[j], neg_e[j], GQ, r_ln1)
                v.wait_ge(r_cv[j], q.over(2, 16, 16))
                ang, turns, rest, arg = (trig[n][j] for n in range(4))

                def link(ins, n):
                    ins.then_inc(r_ang, 1)
                    v.wait_ge(r_ang, q.times(8, n))

                link(V.tensor_tensor(ang[:, 0:GQ], x3(cv[j], CW, GQ)[:, :, 0], x3(x_e[j], XW, GQ)[:, :, D], ALU.mult), 1)
                link(V.tensor_scalar(turns[:, 0:GQ], ang[:, 0:GQ], 1.0 / PI2, ROUND, ALU.mult, ALU.add), 2)
                link(V.tensor_scalar(turns[:, GQ:2 * GQ], turns[:, 0:GQ], -ROUND, None, ALU.add), 3)
                k = turns[:, GQ:2 * GQ]
                link(V.scalar_tensor_tensor(rest[:, 0:GQ], k, -CA, ang[:, 0:GQ], ALU.mult, ALU.add), 4)
                link(V.scalar_tensor_tensor(rest[:, GQ:2 * GQ], k, -CB, rest[:, 0:GQ], ALU.mult, ALU.add), 5)
                link(V.scalar_tensor_tensor(ang[:, GQ:2 * GQ], k, -CC, rest[:, GQ:2 * GQ], ALU.mult, ALU.add), 6)
                link(V.tensor_scalar(arg[:, 0:GQ], ang[:, GQ:2 * GQ], PI_IN, -PI_IN, ALU.min, ALU.max), 7)
                V.tensor_scalar(arg[:, GQ:2 * GQ], arg[:, 0:GQ], 0.5, None, ALU.mult).then_inc(r_ang, 1)

            def p2_x1(q):
                j = q.mod(2)
                sines, half2, scales = trig[4][j], trig[5][j], trig[6][j]
                attr = x3(x_e[j], XW, GQ)[:, :, D]

                def link(ins, n):
                    ins.then_inc(r_scl, 1)
                    v.wait_ge(r_scl, q.times(4, n))

                v.wait_ge(r_sq1, q.times(1, 1))
                v.wait_ge(r_sin, q.times(1, 1))
                V.reciprocal(inv_e[j][:, :], sd_e[j][:, :])
                V.tensor_tensor(scales[:, GQ:2 * GQ], sines[:, 0:GQ], attr, ALU.mult)
                link(V.tensor_tensor(half2[:, 0:GQ], sines[:, GQ:2 * GQ], sines[:, GQ:2 * GQ], ALU.mult), 1)
                V.tensor_tensor(scl_e[j][:, :], inv_e[j][:, :], attr, ALU.mult)
                link(V.tensor_scalar(half2[:, GQ:2 * GQ], half2[:, 0:GQ], -2.0, 1.0, ALU.mult, ALU.add), 2)
                link(V.tensor_tensor(scales[:, 0:GQ], scl_e[j][:, :], half2[:, GQ:2 * GQ], ALU.mult), 3)
                v.wait_ge(r_mm, q.times(1, 1))
                wait(v, r_y, q.times(1, -1))
                part = part2[j]
                for t in range(GQ):
                    ins = V.scalar_tensor_tensor(part[:, t * D:(t + 1) * D], bank[2 + 2 * j + t // 2][:, t % 2 * D:(t % 2 + 1) * D],
                                                 scales[:, t:t + 1], x_e[j][:, t * XW:t * XW + D], ALU.mult, ALU.add)
                link(ins, 4)
                for t in range(GQ):
                    ins = V.scalar_tensor_tensor(x1[j][:, t * D:(t + 1) * D], cv[j][:, t * CW + 1:(t + 1) * CW],
                                                 scales[:, GQ + t:GQ + t + 1], part[:, t * D:(t + 1) * D],
                                                 ALU.mult, ALU.add)
                ins.then_inc(r_x1, 2)
                v.wait_ge(r_x1, q.times(2, 2))
                for t in range(GQ):
                    ins = V.bn_stats(st2[j][:, t, :], x1[j][:, t * D:(t + 1) * D])
                ins.then_inc(r_ln2, 1)
                moments(st2[j], su2[j], df2[j], sq2[j], m2b[j], neg2[j], var2[j], GQ, r_ln2, lambda n: q.times(5, n))

            def p2_norm2(q):
                j = q.mod(2)
                v.wait_ge(r_sq2, q.times(1, 1))
                V.reciprocal(inv2[j][:, 0:GQ], sd2[j][:, 0:GQ]).then_inc(r_nmr, 1)
                v.wait_ge(r_nmr, q.times(2, 1))
                V.tensor_tensor(nmr2[j][:, 0:GQ], neg2[j][:, 0:GQ], inv2[j][:, 0:GQ], ALU.mult).then_inc(r_nmr, 1)

            def p2_y(q):
                j = q.mod(2)
                v.wait_ge(r_h1, q.times(1, 1))
                wait(v, r_sty[j], q.over(2, 16))
                V.tensor_tensor(yo[j][:, 0:GQ * D], x1[j][:, 0:GQ * D], h1[j][:, 0:GQ * D], ALU.add).then_inc(r_y, 1)

            def p2_step(q, a=True, d=True, y=True):
                if a:
                    p2_prepare(q)
                if y:
                    p2_y(q - 2)
                if d:
                    p2_x1(q - 1)
                    p2_norm2(q - 1)

            for j in range(2):
                v.wait_ge(d_sth[j], 16 * (U // 2))
                v.wait_ge(d_sto[j], 16 * (U // 2))
            p2_step(At(0, 0, 2), d=False, y=False)
            p2_step(At(0, 1, 2), y=False)
            with v.Fori(1, (Q - 1) // 2) as i:
                for c in range(2):
                    p2_step(At(i, c, 2))
            p2_step(At(0, Q - 1, 2))
            p2_step(At(0, Q, 2), a=False)
            p2_step(At(0, Q + 1, 2), a=False, d=False)
            for j in range(2):
                v.wait_ge(r_sty[j], 16 * ((Q + 1 - j) // 2))

            V.memset(tot[1][:, :], 0.0).then_inc(m_z, 1)

            def p3_features(n):
                j, t = n.c // 4 % 2, n.mod(4)
                if t == 0:
                    wait(v, m_seg, n.times(1, -GQ))
                    selectors(j, m_tb[j], n.over(8, 48, 48), m_sc)
                    v.wait_ge(m_g[j], n.over(8, 64, 64))
                wait(v, m_ftr, n.times(1, -1))
                f, h = feat[n.mod(2)], h1[j][:, t * D:(t + 1) * D]
                V.tensor_scalar(f[:, 0:D], h, ed(j, t, 0, 1), None, ALU.mult)
                turned = bass.AP(tensor=q_ed[j], offset=t * EW + 1, ap=[[GQ * EW, P], [1, 3], [0, DU], [1, 3]])
                V.tensor_tensor(f[:, D:D + 3 * DV].rearrange("p (s u i) -> p s u i", s=3, i=3),
                                h[:, DS:D].rearrange("p (u i) -> p u i", i=3).unsqueeze(1).to_broadcast([P, 3, DU, 3]),
                                turned, ALU.mult).then_inc(m_ft, 1)

            def p3_message(n):
                j, t = n.c // 4 % 2, n.mod(4)
                b = bank[2 + n.mod(2)]
                v.wait_ge(m_u, n.times(1, 1))
                x = xr[n.mod(2)]
                v.wait_ge(m_cs, n.times(1, 1))
                V.tensor_tensor(x[:, 0:DV].rearrange("p (u i) -> p u i", i=3), bc_last(b[:, D:D + DU], 3),
                                bc_mid(ed(j, t, 1, 4), DU), ALU.mult).then_inc(m_vx, 1)
                v.wait_ge(m_vx, n.times(1, 1))
                wait(v, m_seg, n.times(1, -1))
                V.tensor_tensor(v_e[n.mod(2)][:, DS:D], b[:, DS:D], x[:, 0:DV], ALU.add).then_inc(m_v, 1)

            def p3_out(n):
                j, t = n.c // 4 % 2, n.mod(4)
                if t == 0:
                    v.wait_ge(m_y[j], n.over(8, 16, 16))
                    wait(v, m_put[j], n.over(8, 64))
                v.wait_ge(m_tot, n.times(1, 1))
                V.scalar_tensor_tensor(yo[j][:, t * D:(t + 1) * D], bank[4 + n.mod(2)][:, 0:D], 0.0,
                                       x1[j][:, t * D:(t + 1) * D], ALU.max, ALU.add).then_inc(m_o, 1)

            def p3_slot(n, lo=0, hi=4):
                if lo <= 2 < hi:
                    p3_message(n - 2)
                if lo <= 0 < hi:
                    p3_features(n)
                if lo <= 3 < hi:
                    p3_out(n - 3)

            for n in range(8):
                p3_slot(At(0, n, 8), 0, n + 1)
            with v.Fori(1, (Q - 1) // 2) as i:
                for c in range(8):
                    p3_slot(At(i, c, 8))
            for n in range(T - GQ, T + 3):
                p3_slot(At(0, n, 8), max(0, n - T + 1))


def pack_weights(np, w):
    pack = np.zeros((P, W_END), np.float32)
    u3 = np.arange(DU) * 3

    def kron(a, shift=0):
        k = np.zeros((DV, DV), np.float32)
        for i in range(3):
            k[np.ix_(u3 + i, u3 + (i + shift) % 3)] = a
        return k

    for col, w0, w1 in ((W_SC, "L0_gnn_sc_w0", "L0_gnn_sc_w1"), (W_L1, "L0_gnn_lin1_w0", "L0_gnn_lin1_w1")):
        pack[0:32, col:col + DS] = w[w0][32:64]
        pack[32:128, col + DS:col + D] = kron(w[w1])
        for t in range(4):
            pack[32 * t:32 * t + 32, col + D + t * DS:col + D + (t + 1) * DS] = w[w0][0:32]
    for t in range(4):
        pack[8 * t:8 * t + 8, W_FC1 + 64 * t:W_FC1 + 64 * (t + 1)] = w["L0_gnn_fc_w1"]
    for h in range(2):
        pack[64 * h:64 * h + 64, W_FC2 + 192 * h:W_FC2 + 192 * (h + 1)] = w["L0_gnn_fc_w2"]
    lin2a, lin2b, lin3 = w["L0_gnn_lin2_w0"], w["L0_gnn_lin2_w1"], w["L0_gnn_lin3_w"]
    rest = np.repeat(np.concatenate([lin3[64:], lin2a[64:]], 1), 3, 0)
    pack[64:128, W_R1:W_R1 + 32] = lin2b[0:64]
    pack[0:64, W_R1 + 32:W_R1 + 33] = lin3[0:64]
    pack[0:64, W_R1 + 33:W_R1 + 97] = lin2a[0:64]
    pack[0:96, W_R2:W_R2 + 96] = kron(lin2b[64:])
    pack[96:128, W_R2 + 96:W_R2 + 161] = rest[0:32]
    pack[64:128, W_R3:W_R3 + 65] = rest[32:96]
    pack[0:64, W_W1T:W_W1T + 64] = w["L1_gnn_W1"].T
    pack[0:64, W_W2T:W_W2T + 96] = np.repeat(w["L1_gnn_W2"].T, 3, 1)
    pack[0:32, W_W3T:W_W3T + 64] = w["L1_gnn_W3"].T
    pack[0:96, W_W4T:W_W4T + 96] = kron(w["L1_gnn_W4"].T)
    pack[0:96, W_W5T:W_W5T + 96] = kron(w["L1_gnn_W5"].T)
    pack[0:64, W_WS:W_WS + 64] = w["L1_gnn_Ws"]
    pack[0:96, W_WVK:W_WVK + 96] = kron(w["L1_gnn_Wv"])
    pack[0:32, W_WV:W_WV + 32] = w["L1_gnn_Wv"]
    pack[0:96, W_WVA:W_WVA + 96] = kron(w["L1_gnn_Wv"], 2)
    pack[0:96, W_WVB:W_WVB + 96] = kron(w["L1_gnn_Wv"], 1)
    return pack


def kernel(**inputs):
    import numpy as np
    import concourse.bacc as bacc
    from concourse.bass_utils import run_bass_kernel_spmd as run

    w = {k: np.asarray(v) for k, v in inputs.items()}
    N, E = w["x"].shape[0], w["src"].shape[0]
    T = -(-E // (P * GQ)) * GQ
    pad = T * P - E

    def by_tile(a, fill):
        a = np.concatenate([a, np.full((pad,) + a.shape[1:], fill, a.dtype)])
        return np.ascontiguousarray(np.swapaxes(a.reshape((T, P) + a.shape[1:]), 0, 1))

    y = w["edge_attr_4"]
    arrays = {
        "xa": np.ascontiguousarray(np.concatenate([w["x"], w["node_vec1"]], 1)),
        "src": by_tile(w["src"].astype(np.int32), 0),
        "dst": by_tile(w["dst"].astype(np.int32), N),
        "edges": by_tile(np.concatenate([y, y[:, 1:3]], 1), 0),
        "scalars": by_tile(w["edge_attr_8"], 0),
        "wpack": pack_weights(np, w),
    }
    nc = bacc.Bacc("TRN2", target_bir_lowering=False, num_devices=1)
    aps = {k: nc.dram_tensor(f"in_{k}", a.shape, mybir.dt.from_np(a.dtype), kind="ExternalInput").ap()
           for k, a in arrays.items()}
    out = nc.dram_tensor("out", (N, D), mybir.dt.float32, kind="ExternalOutput").ap()
    gnn_kernel(nc, out=out, **aps)
    r = run(nc, [{f"in_{k}": a for k, a in arrays.items()}], core_ids=[0])
    return r.results[0]["out"]
```

```python
from contextlib import ExitStack

import concourse.bass as bass
from concourse import mybir

P = 128
GD = 8
GQ = 4
D = 160
DS, DU, DV = 64, 32, 96
XW = D + 1
EW = 6
SW = 8
CW = D + 1
EPS = 1e-5
FAR = 1 << 20

W_SC, W_L1, W_FC1, W_FC2, W_R1, W_R2, W_R3 = 0, 416, 832, 1088, 1472, 1569, 1730
W_W1T, W_W2T, W_W3T, W_W4T, W_W5T = 1795, 1859, 1955, 2019, 2115
W_WS, W_WVK, W_WV, W_WVA, W_WVB, W_END = 2211, 2275, 2371, 2403, 2499, 2595

U_C, U_A, U_D, U_B = 0, 32, 97, 193
U_SEG = 2 * P


class At:

    def __init__(self, i, c, period=4):
        self.i, self.c, self.period = i + c // period, c % period, period

    def __add__(self, n):
        return At(self.i, self.c + n, self.period)

    def __sub__(self, n):
        return At(self.i, self.c - n, self.period)

    def times(self, m, plus=0):
        return self.i * (self.period * m) + (self.c * m + plus)

    def over(self, k, m=1, plus=0):
        return self.i * (self.period // k * m) + (self.c // k * m + plus)

    def mod(self, k):
        return self.c % k

    def within(self, count):
        return not isinstance(self.i, int) or 0 <= self.i * self.period + self.c < count


def wait(eng, sem, value):
    if not (isinstance(value, int) and value <= 0):
        eng.wait_ge(sem, value)


def gnn_kernel(nc, xa, src, dst, number, edges_in, scalars_in, scalars_t_in, wpack, out):
    f32, i32 = mybir.dt.float32, mybir.dt.int32
    ALU, ACT, AX = mybir.AluOpType, mybir.ActivationFunctionType, mybir.AxisListType
    N = xa.shape[0]
    T = src.shape[1]
    Q = T // GQ
    UROWS = P * GD
    U = -(-N // UROWS)
    assert U == 2 * Q and Q % 2 == 1 and Q >= 5
    TA = min(T, P)

    def scratch(name, shape, dt=f32):
        return nc.dram_tensor(name, shape, dt).ap()

    src_tab = scratch("src_tab", (Q, P, GQ), i32)
    dst_tab = scratch("dst_tab", (Q, P, GQ), i32)
    put_tab = scratch("put_tab", (Q, P, GQ), i32)
    key_tab = scratch("key_tab", (Q, P, 2 * GQ))
    row_tab = scratch("row_tab", (T, P))
    sum_tab = scratch("sum_tab", (Q, P, GQ * CW))
    y_tab = scratch("y_tab", (Q, P, GQ * D))
    h1_all = scratch("h1_all", (N, D))

    edges = scratch("edges", (P, T, EW))
    scalars_t = scratch("scalars_t", (Q, GQ * SW, P))
    scalars_sorted = scratch("scalars_sorted", (P, T, SW))
    src_sorted = scratch("src_sorted", (P, T), i32)
    dst_sorted = scratch("dst_sorted", (P, T), i32)

    CH = GQ * P
    dst_c = dst.rearrange("p t -> (p t)").rearrange("(b f) -> b f", f=CH)
    number_c = number.rearrange("p t -> (p t)").rearrange("(b f) -> b f", f=CH)

    row_q = row_tab.rearrange("(q c) p -> q (c p)", c=GQ)
    ed_q = edges.rearrange("p (q c) f -> q p (c f)", c=GQ)
    NU = U - 1
    x_u = xa[0:NU * UROWS, :].rearrange("(u p g) f -> u p (g f)", p=P, g=GD)
    o_u = out[0:NU * UROWS, :].rearrange("(u p g) f -> u p (g f)", p=P, g=GD)
    h_u = h1_all[0:NU * UROWS, :].rearrange("(u p g) f -> u p (g f)", p=P, g=GD)
    x_l = xa[N - UROWS:N, :].rearrange("(p g) f -> p (g f)", p=P)
    o_l = out[N - UROWS:N, :].rearrange("(p g) f -> p (g f)", p=P)
    h_l = h1_all[N - UROWS:N, :].rearrange("(p g) f -> p (g f)", p=P)

    with ExitStack() as ctx:
        def sb(name, shape, dt=f32):
            return ctx.enter_context(nc.sbuf_tensor(name, shape, dt))

        def two(name, shape, dt=f32):
            return [sb(f"{name}{i}", shape, dt) for i in range(2)]

        def four(name, shape, dt=f32):
            return [sb(f"{name}{i}", shape, dt) for i in range(4)]

        def sem(name):
            return ctx.enter_context(nc.semaphore(name))

        def sem2(name):
            return [sem(f"{name}{i}") for i in range(2)]

        bank = [ctx.enter_context(nc.psum_tensor(f"bank{i}", [P, 512], f32)) for i in range(8)]

        wp = sb("wp", [P, W_END])
        ident = sb("ident", [P, P])
        msg1 = [sb("msg1a", [P, D]), sb("msg1b", [P, D]), sb("msg1c", [P, DV]), sb("msg1d", [P, DV])]
        msg1s = sb("msg1s", [P, DU])
        t_src = sb("t_src", [P, T], i32)
        t_dst = sb("t_dst", [P, T], i32)
        t_next = sb("t_next", [P, T], i32)
        t_prev = sb("t_prev", [P, T], i32)
        t_gat = sb("t_gat", [P, T], i32)
        t_put = sb("t_put", [P, T], i32)
        f_dst = sb("f_dst", [P, T])
        f_next = sb("f_next", [P, T])
        f_put = sb("f_put", [P, T])
        f_key = sb("f_key", [P, Q, 2 * GQ])
        t_row = two("t_row", [P, P])
        minus_half = sb("minus_half", [P, GD])
        ones = sb("ones", [P, P])
        falls = sb("falls", [P, T])
        fall = sb("fall", [P, 1])
        unsorted = sb("unsorted", [P, 1], i32)
        k_dst = sb("k_dst", [P, GQ], i32)
        k_src = sb("k_src", [P, GQ], i32)
        k_num = sb("k_num", [P, GQ])
        k_ed = sb("k_ed", [P, GQ, EW])
        k_sc = sb("k_sc", [P, GQ, SW])
        k_row = sb("k_row", [P, CH], i32)
        k_rnum = sb("k_rnum", [P, CH])
        k_less = sb("k_less", [P, GQ])
        k_rank = sb("k_rank", [P, GQ])
        k_tile = sb("k_tile", [P, GQ])
        k_pos = sb("k_pos", [P, GQ])
        k_put = sb("k_put", [P, GQ], i32)
        x_all = sb("x_all", [P, 4 * GD * XW])
        x_in = [x_all[:, i * GD * XW:(i + 1) * GD * XW] for i in range(4)]
        k_cmp = x_all[:, 0:GQ * CH].rearrange("p (c f) -> p c f", c=GQ)
        st1, st2 = four("st1", [P, GD, 6]), two("st2", [P, GD, 6])
        su1, su2 = four("su1", [P, GD, 2]), two("su2", [P, GD, 2])
        df1, df2 = four("df1", [P, GD]), two("df2", [P, GD])
        sq1, sq2 = four("sq1", [P, GD]), two("sq2", [P, GD])
        m21, m22 = four("m21", [P, GD]), two("m22", [P, GD])
        neg1, neg2 = four("neg1", [P, GD]), two("neg2", [P, GD])
        var1, var2 = four("var1", [P, GD]), two("var2", [P, GD])
        inv1, inv2 = four("inv1", [P, GD]), two("inv2", [P, GD])
        scl1, nmr2 = four("scl1", [P, GD]), two("nmr2", [P, GD])
        hb = two("hb", [P, GD * P])
        hr = two("hr", [P, GD * 32])
        hT = two("hT", [P, 512])
        hR = two("hR", [P, P])
        x1 = two("x1", [P, GD * D])
        h1 = two("h1", [P, GD * D])
        yo = two("yo", [P, GD * D])
        i_src = two("i_src", [P, GQ], i32)
        i_dst = two("i_dst", [P, GQ], i32)
        i_put = two("i_put", [P, GQ], i32)
        q_key = two("q_key", [P, 2 * GQ])
        q_row = two("q_row", [P, GQ * P])
        q_ed = two("q_ed", [P, GQ * EW])
        q_sct = two("q_sct", [GQ * SW, P])
        q_hid = two("q_hid", [P, 256])
        same = [two(f"same{t}", [P, P]) for t in range(GQ)]
        carry = [two(f"carry{t}", [P, P]) for t in range(GQ)]
        x_e = two("x_e", [P, GQ * XW])
        h_e = sb("h_e", [P, GQ * P])
        hr_e = two("hr_e", [P, GQ * 32])
        part2 = two("part2", [P, GQ * D])
        eT = sb("eT", [P, 512])
        eR = sb("eR", [P, P])
        g_e = two("g_e", [P, D])
        feat = two("feat", [P, 512])
        fT = two("fT", [P, 512])
        xr = two("xr", [P, CW])
        v_e = two("v_e", [P, CW])
        tot = two("tot", [P, GQ * CW])
        cv = two("cv", [P, GQ * CW])
        trig = [two(f"trig{n}", [P, 2 * GQ]) for n in range(8)]

        st_e = two("st_e", [P, GQ, 6])
        su_e = two("su_e", [P, GQ, 2])
        df_e = two("df_e", [P, GQ])
        sq_e = two("sq_e", [P, GQ])
        m2_e = two("m2_e", [P, GQ])
        neg_e = two("neg_e", [P, GQ])
        var_e = two("var_e", [P, GQ])
        inv_e = two("inv_e", [P, GQ])
        scl_e = two("scl_e", [P, GQ])

        s_w = sem("weights_loaded")
        s_tab_in = sem("edge_tables_loaded")
        s_fill = sem("table_edges_filled")
        s_id = sem("identity_built")
        s_tabc = sem("tables_computed")
        s_wscaled = sem("weights_scaled")
        s_rowps = sem("rows_transposed")
        s_rowsb = sem("rows_copied")
        s_tab_out = sem("tables_stored")
        s_turn = sem("indirect_dmas_may_start")
        s_mz = sem("message_weights_cleared")
        s_mp = sem("message_weights_multiplied")
        s_mc = sem("message_weights_copied")

        s_ones = sem("ones_built")
        s_fall = sem("falls_counted")
        s_fallp = sem("falls_summed")
        s_flag = sem("unsorted_known")
        s_rows = sem("edge_rows_copied")
        k_own = sem("sort_keys_loaded")
        k_chunk = sem("sort_chunk_loaded")
        k_z = sem("sort_count_cleared")
        k_step = sem("sort_count_steps")
        k_ps = sem("sort_place_steps")
        k_sct = sem("sort_rows_scattered")
        k_sct2 = sem("sorted_scalars_transposed")
        k_go = sem("sort_quad_may_start")
        k_tab = sem("sorted_tables_loaded")

        block = ctx.enter_context(nc.Block())

        n_in = sem2("net_scalars_loaded")
        n_mm = sem("net_products_done")
        n_act = sem("net_hidden_ready")
        d_in = [sem(f"x_loaded{i}") for i in range(4)]
        d_ln1 = sem("dense_moments1")
        d_relu = sem("dense_h_ready")
        d_tr = sem("dense_h_transposed")
        d_hT = sem("dense_hT_copied")
        d_mm = sem("dense_product_done")
        d_scl = sem("dense_scale_ready")
        d_nmr = sem("dense_norm2_ready")
        d_x1 = sem("dense_x1_ready")
        d_ln2 = sem("dense_moments2")
        d_h1 = sem("dense_h1_ready")
        d_y = sem("dense_y_ready")
        d_sth = sem2("dense_h1_stored")
        d_sto = sem2("dense_out_stored")
        e_ix = sem2("p1_index_loaded")
        e_tb = sem2("p1_tables_loaded")
        e_scl = sem("p1_scale_ready")
        e_g = sem2("p1_source_rows")
        e_ln = sem("p1_moments")
        e_relu = sem("p1_h_ready")
        e_sc = sem("p1_selectors_ready")
        e_tr = sem("p1_h_transposed")
        e_hT = sem("p1_hT_copied")
        e_pw = sem("p1_products_done")
        e_gg = sem("p1_g_ready")
        e_fm = sem("p1_feature_step")
        e_ft = sem("p1_features_ready")
        e_ftr = sem("p1_features_transposed")
        e_fte = sem("p1_featuresT_copied")
        e_u = sem("p1_message_parts_done")
        e_xb = sem("p1_rest_copied")
        e_vx = sem("p1_rest_ready")
        e_v = sem("p1_message_ready")
        e_seg = sem("p1_sum_done")
        e_tot = sem("p1_sum_copied")
        e_st = sem2("p1_sum_stored")
        e_z = sem("p1_first_carry_cleared")
        r_ix = sem2("p2_index_loaded")
        r_px = sem2("p2_put_loaded")
        r_cv = sem2("p2_sums_loaded")
        r_g = sem2("p2_node_rows")
        r_ln1 = sem("p2_moments1")
        r_inv = sem("p2_root1_ready")
        r_nmr = sem("p2_norm2_ready")
        r_ang = sem("p2_angle_steps")
        r_relu = sem("p2_h_ready")
        r_sin = sem("p2_sines_ready")
        r_tr = sem("p2_h_transposed")
        r_hT = sem("p2_hT_copied")
        r_mm = sem("p2_product_done")
        r_scl = sem("p2_scale_steps")
        r_x1 = sem("p2_x1_steps")
        r_ln2 = sem("p2_moments2")
        r_h1 = sem("p2_h1_ready")
        r_y = sem("p2_y_ready")
        r_put = sem2("p2_h1_scattered")
        r_sty = sem2("p2_y_stored")
        m_ix = sem2("p3_index_loaded")
        m_px = sem2("p3_put_loaded")
        m_tb = sem2("p3_tables_loaded")
        m_y = sem2("p3_y_loaded")
        m_g = sem2("p3_h1_rows")
        m_sc = sem("p3_selectors_ready")
        m_ft = sem("p3_features_ready")
        m_ss = sem("p3_scalars_copied")
        m_ftr = sem("p3_features_transposed")
        m_fte = sem("p3_featuresT_copied")
        m_u = sem("p3_message_parts_done")
        m_cs = sem("p3_scalar_message_copied")
        m_vx = sem("p3_outer_part_ready")
        m_v = sem("p3_message_ready")
        m_seg = sem("p3_sum_done")
        m_tot = sem("p3_sum_copied")
        m_o = sem("p3_out_ready")
        m_put = sem2("p3_out_scattered")
        m_z = sem("p3_first_carry_cleared")

        def x3(t, w, g):
            return t[:, :].rearrange("p (g f) -> p g f", g=g, f=w)

        def ed(par, t, a, b):
            return q_ed[par][:, t * EW + a:t * EW + b]

        def bc_mid(ap, n):
            return ap.unsqueeze(1).to_broadcast([P, n, ap.shape[1]])

        def bc_last(ap, n):
            return ap.unsqueeze(2).to_broadcast([P, ap.shape[1], n])

        @block.sync
        def _(sp):
            sp.dma_start(wp[:, :], wpack).then_inc(s_w, 16)
            sp.dma_start(t_src[:, :], src).then_inc(s_tab_in, 16)
            sp.dma_start(t_dst[:, :], dst).then_inc(s_tab_in, 16)
            sp.wait_ge(s_fill, 2)
            sp.dma_start(t_next[0:P - 1, :], dst[1:P, :]).then_inc(s_tab_in, 16)
            sp.dma_start(t_next[P - 1:P, 0:T - 1], dst[0:1, 1:T]).then_inc(s_tab_in, 16)
            sp.dma_start(t_prev[P - 1:P, 1:T], dst[P - 1:P, 0:T - 1]).then_inc(s_tab_in, 16)
            sp.dma_start(edges.rearrange("p t f -> p (t f)"), edges_in.rearrange("p t f -> p (t f)")).then_inc(s_rows, 16)
            sp.dma_start(scalars_t.rearrange("q f p -> (q f) p"), scalars_t_in.rearrange("q f p -> (q f) p")).then_inc(s_rows, 16)
            sp.wait_ge(s_flag, 1)
            with sp.If(sp.value_load(unsorted[0:1, 0:1], min_val=0, max_val=1) > 0):
                sp.wait_ge(s_rows, 32)
                with sp.Fori(0, Q) as a:
                    sp.wait_ge(k_go, a + 1)
                    sp.dma_start(k_dst[:, :], dst.rearrange("p (q c) -> q p c", c=GQ)[a]).then_inc(k_own, 16)
                    sp.dma_start(k_src[:, :], src.rearrange("p (q c) -> q p c", c=GQ)[a]).then_inc(k_own, 16)
                    sp.dma_start(k_num[:, :], number.rearrange("p (q c) -> q p c", c=GQ)[a]).then_inc(k_own, 16)
                    sp.dma_start(k_ed[:, :, :], edges_in.rearrange("p (q c) f -> q p c f", c=GQ)[a]).then_inc(k_own, 16)
                    sp.dma_start(k_sc[:, :, :], scalars_in.rearrange("p (q c) f -> q p c f", c=GQ)[a]).then_inc(k_own, 16)
                    with sp.Fori(0, Q) as b:
                        sp.wait_ge(k_step, a * (Q * 6) + b * 6 + 1)
                        sp.dma_start(k_row[:, :], dst_c[b].partition_broadcast(P)).then_inc(k_chunk, 16)
                        sp.dma_start(k_rnum[:, :], number_c[b].partition_broadcast(P)).then_inc(k_chunk, 16)
                sp.wait_ge(k_go, Q + 1)
                sp.dma_start(t_src[:, :], src_sorted).then_inc(k_tab, 16)
                sp.dma_start(t_dst[:, :], dst_sorted).then_inc(k_tab, 16)
                sp.dma_start(t_next[0:P - 1, :], dst_sorted[1:P, :]).then_inc(k_tab, 16)
                sp.dma_start(t_next[P - 1:P, 0:T - 1], dst_sorted[0:1, 1:T]).then_inc(k_tab, 16)
                sp.dma_start(t_prev[P - 1:P, 1:T], dst_sorted[P - 1:P, 0:T - 1]).then_inc(k_tab, 16)
                with sp.Fori(0, Q) as a:
                    for t in range(GQ):
                        sp.dma_start(scalars_t.rearrange("q (c f) p -> q c f p", c=GQ)[a, t],
                                     scalars_sorted.rearrange("p (q c) f -> q c f p", c=GQ)[a, t],
                                     allow_slow_non_contiguous=True).then_inc(k_sct2, 16)
                sp.wait_ge(k_sct2, 16 * T)
            sp.wait_ge(s_tabc, 6)
            sp.dma_start(src_tab.rearrange("q p c -> p q c"), t_src[:, :].rearrange("p (q c) -> p q c", c=GQ)).then_inc(s_tab_out, 16)
            sp.dma_start(dst_tab.rearrange("q p c -> p q c"), t_gat[:, :].rearrange("p (q c) -> p q c", c=GQ)).then_inc(s_tab_out, 16)
            sp.dma_start(put_tab.rearrange("q p c -> p q c"), t_put[:, :].rearrange("p (q c) -> p q c", c=GQ)).then_inc(s_tab_out, 16)
            sp.dma_start(key_tab.rearrange("q p c -> p q c"), f_key[:, :, :]).then_inc(s_tab_out, 16)
            sp.wait_ge(s_rowsb, 1)
            sp.dma_start(row_tab[0:TA, :], t_row[0][0:TA, :]).then_inc(s_tab_out, 16)
            n_out = 5
            if T > P:
                sp.wait_ge(s_rowsb, 2)
                sp.dma_start(row_tab[P:T, :], t_row[1][0:T - P, :]).then_inc(s_tab_out, 16)
                n_out = 6

            sp.wait_ge(s_rows, 32)
            sp.wait_ge(s_tab_out, 16 * n_out)

            def x_load(u, last=False):
                wait(sp, d_x1, u.times(4, -12))
                sp.dma_start(x_in[u.mod(4)], x_l if last else x_u[u.times(1)]).then_inc(d_in[u.mod(4)], 16)

            def dense_store(u, last=False):
                j = u.mod(2)
                if last:
                    sp.wait_ge(d_sth[1 - j], 16 * (U // 2))
                    sp.wait_ge(d_sto[1 - j], 16 * (U // 2))
                sp.wait_ge(d_h1, u.times(2, 2))
                sp.dma_start(h_l if last else h_u[u.times(1)], h1[j][:, :]).then_inc(d_sth[j], 16)
                sp.wait_ge(d_y, u.times(2, 2))
                sp.dma_start(o_l if last else o_u[u.times(1)], yo[j][:, :]).then_inc(d_sto[j], 16)

            def p1_load(q):
                j = q.mod(2)
                wait(sp, e_g[j], q.over(2, 64))
                sp.dma_start(i_src[j][:, :], src_tab[q.times(1)]).then_inc(e_ix[j], 16)
                wait(sp, n_mm, q.times(1, -1))
                sp.dma_start(q_sct[j][:, :], scalars_t[q.times(1)]).then_inc(n_in[j], 16)

            def p1_tables(q):
                j = q.mod(2)
                wait(sp, e_v, q.times(GQ, -GQ))
                sp.dma_start(q_key[j][:, :], key_tab[q.times(1)]).then_inc(e_tb[j], 16)
                sp.dma_start(q_ed[j][:, :], ed_q[q.times(1)]).then_inc(e_tb[j], 16)
                sp.dma_start(q_row[j][:, :], row_q[q.times(1)].partition_broadcast(P)).then_inc(e_tb[j], 16)

            def p1_store(q):
                sp.wait_ge(e_tot, q.times(GQ, GQ))
                sp.dma_start(sum_tab[q.times(1)], tot[q.mod(2)][:, :]).then_inc(e_st[q.mod(2)], 16)

            def step(v, last=False, laststore=False):
                q = At(v.i, v.c // 2, 2)
                if v.within(U):
                    x_load(v, last)
                if v.mod(2) == 0 and (q + 1).within(Q):
                    p1_load(q + 1)
                if v.mod(2) == 1 and q.within(Q):
                    p1_tables(q)
                if (v - 4).within(U):
                    dense_store(v - 4, laststore)
                if v.mod(2) == 1 and (q - 2).within(Q):
                    p1_store(q - 2)

            p1_load(At(0, 0, 2))
            for v in range(4):
                step(At(0, v))
            with sp.Fori(1, U // 4) as i:
                for c in range(4):
                    step(At(i, c))
            for v in range(U - 2, U + 4):
                step(At(0, v), last=v == U - 1, laststore=v == U + 3)
            for j in range(2):
                sp.wait_ge(e_st[j], 16 * ((Q + 1 - j) // 2))

            def p2_load(q):
                j = q.mod(2)
                wait(sp, r_g[j], q.over(2, 64))
                sp.dma_start(i_dst[j][:, :], dst_tab[q.times(1)]).then_inc(r_ix[j], 16)
                wait(sp, r_x1, q.times(2, -2))
                sp.dma_start(cv[j][:, :], sum_tab[q.times(1)]).then_inc(r_cv[j], 16)

            def p2_put(q):
                j = q.mod(2)
                wait(sp, r_put[j], q.over(2, 64))
                sp.dma_start(i_put[j][:, :], put_tab[q.times(1)]).then_inc(r_px[j], 16)

            def p2_store(q):
                sp.wait_ge(r_y, q.times(1, 1))
                sp.dma_start(y_tab[q.times(1)], yo[q.mod(2)][:, 0:GQ * D]).then_inc(r_sty[q.mod(2)], 16)

            def p2_step(q, load=True, put=True, store=True):
                if load:
                    p2_load(q + 1)
                if put:
                    p2_put(q - 1)
                if store:
                    p2_store(q - 2)

            p2_load(At(0, 0, 2))
            p2_step(At(0, 0, 2), put=False, store=False)
            p2_step(At(0, 1, 2), store=False)
            with sp.Fori(1, (Q - 1) // 2) as i:
                for c in range(2):
                    p2_step(At(i, c, 2))
            p2_step(At(0, Q - 1, 2), load=False)
            p2_step(At(0, Q, 2), load=False)
            p2_step(At(0, Q + 1, 2), load=False, put=False)
            for j in range(2):
                sp.wait_ge(r_sty[j], 16 * ((Q + 1 - j) // 2))
                sp.wait_ge(r_put[j], 64 * ((Q + 1 - j) // 2))

            def p3_load(q):
                j = q.mod(2)
                wait(sp, m_g[j], q.over(2, 64))
                sp.dma_start(i_src[j][:, :], src_tab[q.times(1)]).then_inc(m_ix[j], 16)
                wait(sp, m_o, q.times(GQ, -GQ))
                sp.dma_start(q_key[j][:, :], key_tab[q.times(1)]).then_inc(m_tb[j], 16)
                sp.dma_start(q_ed[j][:, :], ed_q[q.times(1)]).then_inc(m_tb[j], 16)
                sp.dma_start(q_row[j][:, :], row_q[q.times(1)].partition_broadcast(P)).then_inc(m_tb[j], 16)
                sp.dma_start(x1[j][:, 0:GQ * D], y_tab[q.times(1)]).then_inc(m_y[j], 16)
                wait(sp, m_put[j], q.over(2, 64))
                sp.dma_start(i_put[j][:, :], put_tab[q.times(1)]).then_inc(m_px[j], 16)

            p3_load(At(0, 0, 2))
            p3_load(At(0, 1, 2))
            with sp.Fori(1, (Q - 1) // 2) as i:
                for c in range(2):
                    p3_load(At(i, c, 2))
            p3_load(At(0, Q - 1, 2))
            for j in range(2):
                sp.wait_ge(m_put[j], 64 * ((Q + 1 - j) // 2))

        @block.gpsimd
        def _(pool):
            nc.gpsimd.memset(t_next[:, :], N + 5).then_inc(s_fill, 1)
            nc.gpsimd.memset(t_prev[:, :], -1).then_inc(s_fill, 1)
            nc.gpsimd.memset(minus_half[:, :], -0.5)
            nc.gpsimd.memset(ones[:, :], 1.0).then_inc(s_ones, 1)
            pool.wait_ge(s_ones, 1)
            nc.gpsimd.memset(ident[:, :], 0.0).then_inc(s_id, 1)
            pool.wait_ge(s_id, 1)
            nc.gpsimd.affine_select(out=ident[:, :], in_=ident[:, :], compare_op=ALU.not_equal, fill=1.0, base=0,
                                    pattern=[[-1, P]], channel_multiplier=1).then_inc(s_id, 1)

            def gather(rows, into, width, index, signal):
                pool.sem_inc(s_turn, 1)
                for t in range(GQ):
                    nc.gpsimd.indirect_dma_start(
                        into[:, t * width:(t + 1) * width], None, rows,
                        bass.IndirectOffsetOnAxis(ap=index[:, t:t + 1], axis=0)).then_inc(signal, 16)

            def scatter_tile(rows, tile, index, t, signal):
                pool.sem_inc(s_turn, 1)
                nc.gpsimd.indirect_dma_start(
                    rows, bass.IndirectOffsetOnAxis(ap=index[:, t:t + 1], axis=0), tile, None,
                    bounds_check=N - 1, oob_is_err=False).then_inc(signal, 16)

            pool.wait_ge(s_flag, 1)
            with pool.If(pool.value_load(unsorted[0:1, 0:1], min_val=0, max_val=1) > 0):
                pool.sem_inc(k_go, 1)
                with pool.Fori(0, Q) as a:
                    pool.wait_ge(k_ps, a * 7 + 7)
                    pool.sem_inc(s_turn, 1)
                    for t in range(GQ):
                        for rows, tile in ((src_sorted.rearrange("p (t o) -> (p t) o", o=1), k_src[:, t:t + 1]),
                                           (dst_sorted.rearrange("p (t o) -> (p t) o", o=1), k_dst[:, t:t + 1]),
                                           (edges.rearrange("p t f -> (p t) f"), k_ed[:, t, :]),
                                           (scalars_sorted.rearrange("p t f -> (p t) f"), k_sc[:, t, :])):
                            nc.gpsimd.indirect_dma_start(
                                rows, bass.IndirectOffsetOnAxis(ap=k_put[:, t:t + 1], axis=0), tile, None) \
                                .then_inc(k_sct, 16)
                    pool.wait_ge(k_sct, a * 256 + 256)
                    pool.sem_inc(k_go, 1)

            def p1_gather(q):
                j = q.mod(2)
                pool.wait_ge(e_ix[j], q.over(2, 16, 16))
                wait(pool, e_relu, q.times(1, -1))
                wait(pool, e_scl, q.times(2, -2))
                gather(xa, x_e[j], XW, i_src[j], e_g[j])

            def dense_y(u):
                j = u.mod(2)
                for h in range(2):
                    pool.wait_ge(d_h1, u.times(2, h + 1))
                    if h == 0:
                        wait(pool, d_sto[j], u.over(2, 16))
                    a, b = h * GQ * D, (h + 1) * GQ * D
                    nc.gpsimd.tensor_tensor(yo[j][:, a:b], x1[j][:, a:b], h1[j][:, a:b], ALU.add).then_inc(d_y, 1)

            def inverse_root(inv, var, n, signal):
                nc.gpsimd.tensor_tensor(inv[:, 0:n], var[:, 0:n], minus_half[:, 0:n], ALU.pow).then_inc(signal, 1)

            def dense_scale(u):
                j = u.mod(4)
                pool.wait_ge(d_ln1, u.times(5, 4))
                inverse_root(inv1[j], var1[j], GD, d_scl)
                pool.wait_ge(d_scl, u.times(2, 1))
                nc.gpsimd.tensor_tensor(scl1[j][:, :], inv1[j][:, :], x3(x_in[j], XW, GD)[:, :, D], ALU.mult).then_inc(d_scl, 1)

            def dense_norm2(u):
                j = u.mod(2)
                pool.wait_ge(d_ln2, u.times(4, 4))
                inverse_root(inv2[j], var2[j], GD, d_nmr)
                pool.wait_ge(d_nmr, u.times(2, 1))
                nc.gpsimd.tensor_tensor(nmr2[j][:, :], neg2[j][:, :], inv2[j][:, :], ALU.mult).then_inc(d_nmr, 1)

            def p1_scale(q):
                j = q.mod(2)
                pool.wait_ge(e_ln, q.times(5, 4))
                inverse_root(inv_e[j], var_e[j], GQ, e_scl)
                pool.wait_ge(e_scl, q.times(2, 1))
                nc.gpsimd.tensor_tensor(scl_e[j][:, :], inv_e[j][:, :], x3(x_e[j], XW, GQ)[:, :, D], ALU.mult).then_inc(e_scl, 1)

            def step(w):
                q = At(w.i, w.c // 2, 2)
                if w.mod(2) == 1 and (q + 1).within(Q):
                    p1_gather(q + 1)
                if (w - 1).within(U):
                    dense_scale(w - 1)
                if (w - 4).within(U):
                    dense_y(w - 4)
                if (w - 3).within(U):
                    dense_norm2(w - 3)
                if w.mod(2) == 0 and q.within(Q):
                    p1_scale(q)

            p1_gather(At(0, 0, 2))
            for w in range(4):
                step(At(0, w))
            with pool.Fori(1, U // 4) as i:
                for c in range(4):
                    step(At(i, c))
            for w in range(U - 2, U + 4):
                step(At(0, w))
            for j in range(2):
                pool.wait_ge(d_sth[j], 16 * (U // 2))
                pool.wait_ge(d_sto[j], 16 * (U // 2))

            def p2_gather(q):
                j = q.mod(2)
                pool.wait_ge(r_ix[j], q.over(2, 16, 16))
                wait(pool, r_x1, q.times(2, -2))
                gather(xa, x_e[j], XW, i_dst[j], r_g[j])

            def p2_scatter(q):
                j = q.mod(2)
                pool.wait_ge(r_px[j], q.over(2, 16, 16))
                pool.wait_ge(r_h1, q.times(1, 1))
                for t in range(GQ):
                    scatter_tile(h1_all, h1[j][:, t * D:(t + 1) * D], i_put[j], t, r_put[j])

            def p2_root1(q):
                pool.wait_ge(r_ln1, q.times(5, 4))
                inverse_root(inv_e[q.mod(2)], var_e[q.mod(2)], GQ, r_inv)

            def p2_norm2(q):
                j = q.mod(2)
                pool.wait_ge(r_ln2, q.times(4, 4))
                inverse_root(inv2[j], var2[j], GQ, r_nmr)
                pool.wait_ge(r_nmr, q.times(2, 1))
                nc.gpsimd.tensor_tensor(nmr2[j][:, 0:GQ], neg2[j][:, 0:GQ], inv2[j][:, 0:GQ], ALU.mult).then_inc(r_nmr, 1)

            def p2_step(q):
                if (q - 3).within(Q):
                    p2_scatter(q - 3)
                if q.within(Q):
                    p2_gather(q)
                if (q - 1).within(Q):
                    p2_root1(q - 1)
                if (q - 2).within(Q):
                    p2_norm2(q - 2)

            pool.wait_ge(e_tot, Q * GQ)
            for q in range(4):
                p2_step(At(0, q, 2))
            with pool.Fori(2, (Q - 1) // 2) as i:
                for c in range(2):
                    p2_step(At(i, c, 2))
            for q in range(Q - 1, Q + 3):
                p2_step(At(0, q, 2))
            for j in range(2):
                pool.wait_ge(r_put[j], 64 * ((Q + 1 - j) // 2))
            pool.wait_ge(r_y, Q)

            def p3_gather(q):
                j = q.mod(2)
                pool.wait_ge(m_ix[j], q.over(2, 16, 16))
                wait(pool, m_ft, q.times(GQ, -GQ))
                wait(pool, m_ss, q.times(GQ, -GQ))
                gather(h1_all, h1[j], D, i_src[j], m_g[j])

            def p3_scatter(q):
                j = q.mod(2)
                pool.wait_ge(m_px[j], q.over(2, 16, 16))
                for t in range(GQ):
                    pool.wait_ge(m_o, q.times(GQ, t + 1))
                    scatter_tile(out, yo[j][:, t * D:(t + 1) * D], i_put[j], t, m_put[j])

            p3_gather(At(0, 0, 2))
            p3_gather(At(0, 1, 2))
            p3_scatter(At(0, 0, 2))
            with pool.Fori(0, (Q - 3) // 2) as i:
                for c in (2, 3):
                    p3_gather(At(i, c, 2))
                    p3_scatter(At(i, c, 2) - 1)
            p3_gather(At(0, Q - 1, 2))
            p3_scatter(At(0, Q - 2, 2))
            p3_scatter(At(0, Q - 1, 2))

        @block.scalar
        def _(act):
            def dense_h1(u, h):
                j = u.mod(2)
                act.wait_ge(d_nmr, u.times(2, 2))
                wait(act, d_y, u.times(2, h - 3))
                wait(act, d_sth[j], u.over(2, 16))
                for k in range(h * GQ, (h + 1) * GQ):
                    ins = nc.scalar.activation(h1[j][:, k * D:(k + 1) * D], x1[j][:, k * D:(k + 1) * D], ACT.Relu,
                                               bias=nmr2[j][:, k:k + 1], scale=inv2[j][:, k:k + 1])
                ins.then_inc(d_h1, 1)

            def dense_relu(u, h):
                act.wait_ge(d_ln1, u.times(5, 3))
                x, hh = x_in[u.mod(4)], hb[u.mod(2)]
                for k in range(h * GQ, (h + 1) * GQ):
                    ins = nc.scalar.activation(hh[:, k * P:(k + 1) * P], x[:, k * XW + 32:k * XW + D], ACT.Relu,
                                               bias=neg1[u.mod(4)][:, k:k + 1])
                ins.then_inc(d_relu, 1)

            def dense_copy(u, h):
                act.wait_ge(d_tr, u.times(2, h + 1))
                wait(act, d_mm, u.times(4, 2 * h - 2))
                nc.scalar.activation(hT[h][:, :], bank[0][:, :], ACT.Copy)
                nc.scalar.activation(hR[h][:, :], bank[1][:, 0:P], ACT.Relu).then_inc(d_hT, 1)

            def net_silu(q):
                act.wait_ge(n_mm, q.times(1, 1))
                nc.scalar.activation(q_hid[q.mod(2)][:, :], bank[4][:, 0:2 * P], ACT.Silu,
                                     scale=8.0 ** -0.5).then_inc(n_act, 1)

            def p1_relu(q):
                j = q.mod(2)
                act.wait_ge(e_ln, q.times(5, 3))
                for t in range(GQ):
                    ins = nc.scalar.activation(h_e[:, t * P:(t + 1) * P], x_e[j][:, t * XW + 32:t * XW + D], ACT.Relu,
                                               bias=neg_e[j][:, t:t + 1])
                ins.then_inc(e_relu, 1)

            def p1_copy(q):
                act.wait_ge(e_tr, q.times(1, 1))
                wait(act, e_pw, q.times(GQ))
                nc.scalar.activation(eT[:, :], bank[4][:, :], ACT.Copy)
                nc.scalar.activation(eR[:, :], bank[1][:, P:2 * P], ACT.Relu).then_inc(e_hT, 1)

            def p1_rest(n):
                act.wait_ge(e_u, n.times(1, 1))
                wait(act, e_v, n.times(1, -1))
                nc.scalar.activation(xr[n.mod(2)][:, 0:65], bank[7][:, U_B:U_B + 65], ACT.Copy).then_inc(e_xb, 1)

            def p1_source(n):
                act.wait_ge(e_pw, n.times(1, 1))
                j, t = n.c // GQ % 2, n.mod(4)
                act.wait_ge(e_scl, n.over(4, 2, 2))
                wait(act, e_ft, n.times(1, -1))
                nc.scalar.activation(g_e[n.mod(2)][:, :], bank[5 + n.mod(2)][:, 0:D], ACT.Copy,
                                     scale=scl_e[j][:, t:t + 1]).then_inc(e_gg, 1)

            def p1_total(n):
                act.wait_ge(e_seg, n.times(1, 1))
                j, t = n.c // GQ % 2, n.mod(4)
                if t == 0:
                    wait(act, e_st[j], n.over(8, 16))
                nc.scalar.activation(tot[j][:, t * CW:(t + 1) * CW], bank[1][:, U_SEG:U_SEG + CW],
                                     ACT.Copy).then_inc(e_tot, 1)

            def p1_feat_t(n):
                act.wait_ge(e_ftr, n.times(1, 1))
                wait(act, e_u, n.times(1, -1))
                nc.scalar.activation(fT[n.mod(2)][:, 0:384], bank[4][:, 0:384], ACT.Copy).then_inc(e_fte, 1)

            def slot(u, h):
                s = At(u.i, 2 * u.c + h, 8)
                if (s - 2).within(T):
                    p1_rest(s - 2)
                if s.within(T):
                    p1_source(s)
                if (s - 3).within(T):
                    p1_total(s - 3)
                if (u - 2).within(U):
                    dense_h1(u - 2, h)
                if (s - 1).within(T):
                    p1_feat_t(s - 1)

            def step(u):
                q = At(u.i, u.c // 2, 2)
                odd = u.mod(2) == 1
                if u.within(U):
                    dense_relu(u, 0)
                slot(u, 0)
                if not odd and (q + 1).within(Q):
                    net_silu(q + 1)
                if u.within(U):
                    dense_copy(u, 0)
                    dense_relu(u, 1)
                if odd and (q + 1).within(Q):
                    p1_relu(q + 1)
                slot(u, 1)
                if odd and (q + 1).within(Q):
                    p1_copy(q + 1)
                if u.within(U):
                    dense_copy(u, 1)

            net_silu(At(0, 0, 2))
            p1_relu(At(0, 0, 2))
            p1_copy(At(0, 0, 2))
            for u in range(4):
                step(At(0, u))
            with act.Fori(1, U // 4) as i:
                for c in range(4):
                    step(At(i, c))
            for u in range(U - 2, U + 2):
                step(At(0, u))

            def p2_h1(q):
                j = q.mod(2)
                act.wait_ge(r_nmr, q.times(2, 2))
                wait(act, r_y, q.times(1, -1))
                wait(act, r_put[j], q.over(2, 64))
                for t in range(GQ):
                    ins = nc.scalar.activation(h1[j][:, t * D:(t + 1) * D], x1[j][:, t * D:(t + 1) * D], ACT.Relu,
                                               bias=nmr2[j][:, t:t + 1], scale=inv2[j][:, t:t + 1])
                ins.then_inc(r_h1, 1)

            def p2_relu(q):
                j = q.mod(2)
                act.wait_ge(r_ln1, q.times(5, 3))
                for t in range(GQ):
                    ins = nc.scalar.activation(h_e[:, t * P:(t + 1) * P], x_e[j][:, t * XW + 32:t * XW + D], ACT.Relu,
                                               bias=neg_e[j][:, t:t + 1])
                ins.then_inc(r_relu, 1)

            def p2_copy(q):
                act.wait_ge(r_tr, q.times(1, 1))
                wait(act, r_mm, q.times(1))
                nc.scalar.activation(eT[:, :], bank[0][:, :], ACT.Copy)
                nc.scalar.activation(eR[:, :], bank[1][:, 0:P], ACT.Relu).then_inc(r_hT, 1)

            def p2_sines(q):
                j = q.mod(2)
                act.wait_ge(r_ang, q.times(8, 8))
                nc.scalar.activation(trig[4][j][:, :], trig[3][j][:, :], ACT.Sin).then_inc(r_sin, 1)

            def p2_step(q, a=True, h=True):
                if h:
                    p2_h1(q - 2)
                if a:
                    p2_relu(q)
                    p2_copy(q)
                    p2_sines(q)

            p2_step(At(0, 0, 2), h=False)
            p2_step(At(0, 1, 2), h=False)
            p2_step(At(0, 2, 2))
            p2_step(At(0, 3, 2))
            with act.Fori(2, (Q - 1) // 2) as i:
                for c in range(2):
                    p2_step(At(i, c, 2))
            p2_step(At(0, Q - 1, 2))
            p2_step(At(0, Q, 2), a=False)
            p2_step(At(0, Q + 1, 2), a=False)

            def p3_scalars(n):
                if n.mod(4) == 0:
                    act.wait_ge(m_g[n.c // 4 % 2], n.over(8, 64, 64))
                wait(act, m_ftr, n.times(1, -1))
                j = n.c // 4 % 2
                t = n.mod(4)
                nc.scalar.activation(feat[n.mod(2)][:, 448:512], h1[j][:, t * D:t * D + DS], ACT.Copy).then_inc(m_ss, 1)

            def p3_featT(n):
                act.wait_ge(m_ftr, n.times(1, 1))
                wait(act, m_u, n.times(1, -1))
                nc.scalar.activation(fT[n.mod(2)][:, :], bank[n.mod(2)][:, :], ACT.Copy).then_inc(m_fte, 1)

            def p3_smsg(n):
                act.wait_ge(m_u, n.times(1, 1))
                wait(act, m_seg, n.times(1, -1))
                nc.scalar.activation(v_e[n.mod(2)][:, 0:DS], bank[2 + n.mod(2)][:, 0:DS], ACT.Copy).then_inc(m_cs, 1)

            def p3_total(n):
                act.wait_ge(m_seg, n.times(1, 1))
                nc.scalar.activation(tot[n.mod(2)][:, 0:D], bank[4 + n.mod(2)][:, 0:D], ACT.Copy).then_inc(m_tot, 1)

            def p3_slot(n, lo=0, hi=4):
                if hi > 0 and lo <= 0:
                    p3_scalars(n)
                if lo <= 2 < hi:
                    p3_smsg(n - 2)
                if lo <= 1 < hi:
                    p3_featT(n - 1)
                if lo <= 3 < hi:
                    p3_total(n - 3)

            for n in range(8):
                p3_slot(At(0, n, 8), 0, n + 1)
            with act.Fori(1, (Q - 1) // 2) as i:
                for c in range(8):
                    p3_slot(At(i, c, 8))
            for n in range(T - GQ, T + 3):
                p3_slot(At(0, n, 8), max(0, n - T + 1))

        @block.tensor
        def _(pe):
            def transpose_rows(main, rest, ps_main, ps_rest, tr_sem):
                for t in range(GQ):
                    nc.tensor.transpose(ps_main[:, t * P:(t + 1) * P], main[:, t * P:(t + 1) * P], ident[:, :])
                nc.tensor.transpose(ps_rest, rest, ident[:, :]).then_inc(tr_sem, 1)

            def linear(dst_ps, main, rest, w, t):
                nc.tensor.matmul(dst_ps, main[:, t * P:(t + 1) * P], wp[:, w:w + D], start=True, stop=False)
                return nc.tensor.matmul(dst_ps[:, 0:DS], rest[:, :], wp[:, w + D + t * DS:w + D + (t + 1) * DS],
                                        start=False, stop=True)

            pe.wait_ge(s_ones, 1)
            pe.wait_ge(s_fall, 2)
            nc.tensor.matmul(bank[7][:, 0:1], ones[:, :], fall[:, :], start=True, stop=True).then_inc(s_fallp, 1)

            pe.wait_ge(s_id, 2)
            pe.wait_ge(s_tabc, 1)
            nc.tensor.transpose(bank[6][0:TA, 0:P], f_dst[:, 0:TA], ident[:, :]).then_inc(s_rowps, 1)
            if T > P:
                nc.tensor.transpose(bank[7][0:T - P, 0:P], f_dst[:, P:T], ident[:, :]).then_inc(s_rowps, 1)

            pe.wait_ge(s_w, 16)
            pieces = [(b, W_W1T, 64, b, W_WS, 64) for b in (0, 1)] \
                + [(2 + b, W_W4T, 96, b, W_WVK, 96) for b in range(3)] \
                + [(5 + b, W_W2T, 64, b, W_WS, 64) for b in range(3)] \
                + [(8 + b, W_W5T, 96, b, W_WVA, 96) for b in range(3)] \
                + [(11 + b, W_W5T, 96, b, W_WVB, 96) for b in range(3)] \
                + [(14 + b, W_W3T, 32, b, W_WV, 32) for b in (0, 1)]
            for r, wl, kk, b, wr, cols in pieces:
                where = 32 * (r % 4)
                nc.tensor.matmul(bank[r // 4][where:where + 32, 0:cols],
                                 wp[0:kk, wl + 32 * b:wl + 32 * (b + 1)], wp[0:kk, wr:wr + cols],
                                 start=True, stop=True).then_inc(s_mp, 1)
            pe.wait_ge(s_mc, 1)
            pe.wait_ge(s_wscaled, 1)

            def dense_mm(u, h):
                pe.wait_ge(d_hT, u.times(2, h + 1))
                for k in range(GQ):
                    if k % 2 == 0:
                        wait(pe, d_x1, u.times(4, 2 * h + k // 2 - 1))
                    ins = linear(bank[2 + k // 2][:, k % 2 * D:(k % 2 + 1) * D], hT[h], hR[h], W_SC, k)
                    if k % 2 == 1:
                        ins.then_inc(d_mm, 1)

            def dense_tr(u, h):
                pe.wait_ge(d_relu, u.times(2, h + 1))
                pe.wait_ge(d_ln1, u.times(5, 5))
                wait(pe, d_hT, u.times(2, h))
                wait(pe, e_tot, u.times(2, h - 2))
                if h == 1 and u.mod(2) == 1:
                    q1 = At(u.i, u.c // 2, 2) + 1
                    if q1.within(Q):
                        pe.wait_ge(e_hT, q1.times(1, 1))
                elif h == 0 and not isinstance(u.i, int) or h == 0:
                    wait(pe, e_hT, At(u.i, u.c // 2, 2).times(1, 1))
                transpose_rows(hb[u.mod(2)][:, h * 4 * P:(h + 1) * 4 * P], hr[u.mod(2)][:, h * P:(h + 1) * P], bank[0],
                               bank[1][:, 0:P], d_tr)

            def net_mm(q):
                pe.wait_ge(n_in[q.mod(2)], q.over(2, 16, 16))
                wait(pe, e_fte, q.times(GQ, -GQ))
                for h in range(2):
                    ins = nc.tensor.matmul(bank[4][:, h * P:(h + 1) * P],
                                           wp[0:32, W_FC1 + h * P:W_FC1 + (h + 1) * P], q_sct[q.mod(2)][:, :],
                                           start=True, stop=True)
                ins.then_inc(n_mm, 1)

            def p1_tr(q):
                pe.wait_ge(e_relu, q.times(1, 1))
                pe.wait_ge(e_ln, q.times(5, 5))
                wait(pe, e_fte, q.times(GQ, -1))
                pe.wait_ge(n_act, q.times(1, 1))
                wait(pe, d_hT, q.times(4, -1))
                wait(pe, e_tot, q.times(4, -3))
                transpose_rows(h_e[:, :], hr_e[q.mod(2)][:, :], bank[4], bank[1][:, P:2 * P], e_tr)

            def p1_parts(n):
                pe.wait_ge(e_fte, n.times(1, 1))
                wait(pe, e_v, n.times(1))
                f = fT[n.mod(2)]
                nc.tensor.matmul(bank[7][:, U_C:U_C + 97], f[:, 0:P], wp[:, W_R1:W_R1 + 97], start=True, stop=True)
                nc.tensor.matmul(bank[7][:, U_D:U_D + 161], f[:, P:2 * P], wp[:, W_R2:W_R2 + 161],
                                 start=True, stop=False)
                nc.tensor.matmul(bank[7][:, U_B:U_B + 65], f[:, 2 * P:3 * P], wp[:, W_R3:W_R3 + 65],
                                 start=False, stop=True).then_inc(e_u, 1)

            def p1_source(n):
                j, t = n.c // GQ % 2, n.mod(4)
                if t == 0:
                    pe.wait_ge(e_hT, n.over(4, 1, 1))
                    pe.wait_ge(n_act, n.over(4, 1, 1))
                wait(pe, e_ft, n.times(1, -1))
                b = bank[5 + n.mod(2)]
                linear(b[:, 0:D], eT, eR, W_L1, t)
                nc.tensor.matmul(b[:, D:D + 192], q_hid[j][:, t // 2 * P:(t // 2 + 1) * P],
                                 wp[:, W_FC2 + t % 2 * 192:W_FC2 + (t % 2 + 1) * 192],
                                 start=True, stop=True).then_inc(e_pw, 1)

            def p1_sum(n, dense_copied):
                j, t = n.c // GQ % 2, n.mod(4)
                if t == 0:
                    pe.wait_ge(e_sc, n.over(4, 1, 1))
                pe.wait_ge(e_v, n.times(1, 1))
                wait(pe, e_tot, n.times(1))
                wait(pe, d_hT, dense_copied)
                before = tot[j][:, (t - 1) * CW:t * CW] if t else tot[1 - j][:, (GQ - 1) * CW:GQ * CW]
                nc.tensor.matmul(bank[1][:, U_SEG:U_SEG + CW], same[t][j][:, :], v_e[n.mod(2)][:, :],
                                 start=True, stop=False)
                nc.tensor.matmul(bank[1][:, U_SEG:U_SEG + CW], carry[t][j][:, :], before,
                                 start=False, stop=True).then_inc(e_seg, 1)

            def p1_feat_t(n, q1):
                pe.wait_ge(e_ft, n.times(1, 1))
                wait(pe, e_fte, n.times(1))
                if q1 is not None:
                    pe.wait_ge(n_act, q1.times(1, 1))
                f = feat[n.mod(2)]
                for c, at in enumerate((0, 128, 192)):
                    ins = nc.tensor.transpose(bank[4][:, c * P:(c + 1) * P], f[:, at:at + P], ident[:, :])
                ins.then_inc(e_ftr, 1)

            def slot(u, h):
                s = At(u.i, 2 * u.c + h, 8)
                q1 = At(u.i, u.c // 2, 2) + 1
                if (s - 2).within(T):
                    p1_parts(s - 2)
                if s.within(T):
                    p1_source(s)
                if (s - 3).within(T):
                    p1_sum(s - 3, u.times(2, h) if u.within(U) else 2 * U)
                if (u - 1).within(U):
                    dense_mm(u - 1, h)
                if (s - 1).within(T):
                    p1_feat_t(s - 1, q1 if u.mod(2) == 0 and h == 1 and q1.within(Q) else None)

            def step(u):
                q = At(u.i, u.c // 2, 2)
                odd = u.mod(2) == 1
                slot(u, 0)
                if not odd and (q + 1).within(Q):
                    net_mm(q + 1)
                if u.within(U):
                    dense_tr(u, 0)
                slot(u, 1)
                if odd and (q + 1).within(Q):
                    p1_tr(q + 1)
                if u.within(U):
                    dense_tr(u, 1)

            pe.wait_ge(e_z, 1)
            net_mm(At(0, 0, 2))
            p1_tr(At(0, 0, 2))
            for u in range(4):
                step(At(0, u))
            with pe.Fori(1, U // 4) as i:
                for c in range(4):
                    step(At(i, c))
            for u in range(U - 2, U + 2):
                step(At(0, u))

            def p2_step(q):
                j = q.mod(2)
                pe.wait_ge(r_relu, q.times(1, 1))
                wait(pe, r_hT, q.times(1))
                pe.wait_ge(r_ln1, q.times(5, 5))
                transpose_rows(h_e[:, :], hr_e[j][:, :], bank[0], bank[1][:, 0:P], r_tr)
                pe.wait_ge(r_hT, q.times(1, 1))
                wait(pe, r_x1, q.times(2, -2))
                for t in range(GQ):
                    ins = linear(bank[2 + 2 * j + t // 2][:, t % 2 * D:(t % 2 + 1) * D], eT, eR, W_SC, t)
                ins.then_inc(r_mm, 1)

            pe.wait_ge(d_x1, 4 * U)
            for q in range(2):
                p2_step(At(0, q, 2))
            with pe.Fori(1, (Q - 1) // 2) as i:
                for c in range(2):
                    p2_step(At(i, c, 2))
            p2_step(At(0, Q - 1, 2))
            pe.wait_ge(r_x1, 2 * Q)
            pe.wait_ge(m_z, 1)

            def p3_tr(n):
                pe.wait_ge(m_ft, n.times(1, 1))
                pe.wait_ge(m_ss, n.times(1, 1))
                wait(pe, m_fte, n.times(1, -1))
                for c in range(4):
                    ins = nc.tensor.transpose(bank[n.mod(2)][:, c * P:(c + 1) * P],
                                              feat[n.mod(2)][:, c * P:(c + 1) * P], ident[:, :])
                ins.then_inc(m_ftr, 1)

            def p3_parts(n):
                pe.wait_ge(m_fte, n.times(1, 1))
                wait(pe, m_v, n.times(1, -1))
                f, b = fT[n.mod(2)], bank[2 + n.mod(2)]
                nc.tensor.matmul(b[:, D:D + DU], f[:, 3 * P:4 * P], msg1s[:, :], start=True, stop=True)
                nc.tensor.matmul(b[:, 0:D], f[:, 0:P], msg1[0][:, :], start=True, stop=False)
                nc.tensor.matmul(b[:, 0:D], f[:, P:2 * P], msg1[1][:, :], start=False, stop=False)
                nc.tensor.matmul(b[:, DS:D], f[:, 2 * P:3 * P], msg1[2][:, :], start=False, stop=False)
                nc.tensor.matmul(b[:, DS:D], f[:, 3 * P:4 * P], msg1[3][:, :], start=False, stop=True).then_inc(m_u, 1)

            def p3_sum(n):
                j, t = n.c // 4 % 2, n.mod(4)
                if t == 0:
                    pe.wait_ge(m_sc, n.over(4, 1, 1))
                pe.wait_ge(m_v, n.times(1, 1))
                wait(pe, m_tot, n.times(1))
                wait(pe, m_o, n.times(1, -1))
                b = bank[4 + n.mod(2)]
                nc.tensor.matmul(b[:, 0:D], same[t][j][:, :], v_e[n.mod(2)][:, 0:D], start=True, stop=False)
                nc.tensor.matmul(b[:, 0:D], carry[t][j][:, :], tot[1 - n.mod(2)][:, 0:D],
                                 start=False, stop=True).then_inc(m_seg, 1)

            def p3_slot(n, lo=0, hi=4):
                if lo <= 2 < hi:
                    p3_parts(n - 2)
                if lo <= 1 < hi:
                    p3_tr(n - 1)
                if lo <= 3 < hi:
                    p3_sum(n - 3)

            for n in range(8):
                p3_slot(At(0, n, 8), 0, n + 1)
            with pe.Fori(1, (Q - 1) // 2) as i:
                for c in range(8):
                    p3_slot(At(i, c, 8))
            for n in range(T - GQ, T + 3):
                p3_slot(At(0, n, 8), max(0, n - T + 1))

        @block.vector
        def _(v):
            V = nc.vector

            def moments(st, su, df, sq, m2, neg, var, n, signal, base):
                v.wait_ge(signal, base(1))
                V.tensor_tensor(su[:, 0:n, :], st[:, 0:n, 1:3], st[:, 0:n, 4:6], ALU.add)
                V.tensor_tensor(df[:, 0:n], st[:, 0:n, 1], st[:, 0:n, 4], ALU.subtract).then_inc(signal, 1)
                v.wait_ge(signal, base(2))
                V.tensor_scalar(neg[:, 0:n], su[:, 0:n, 0], -0.5, None, ALU.mult)
                V.scalar_tensor_tensor(sq[:, 0:n], df[:, 0:n], 0.25, df[:, 0:n], ALU.mult, ALU.mult)
                V.tensor_scalar(m2[:, 0:n], su[:, 0:n, 1], 1.0 / D, EPS, ALU.mult, ALU.add).then_inc(signal, 1)
                v.wait_ge(signal, base(3))
                V.tensor_tensor(var[:, 0:n], m2[:, 0:n], sq[:, 0:n], ALU.add).then_inc(signal, 1)

            def rest_of(into, rows, neg, n, signal):
                V.tensor_tensor(x3(into, 32, n), x3(rows, XW, n)[:, :, 0:32], bc_last(neg[:, 0:n], 32), ALU.add) \
                    .then_inc(signal, 1)

            v.wait_ge(s_tab_in, 80)
            V.tensor_tensor(falls[:, :], t_next[:, :], t_dst[:, :], ALU.is_lt).then_inc(s_fall, 1)
            v.wait_ge(s_fall, 1)
            V.tensor_reduce(fall[:, :], falls[:, :], AX.X, ALU.add).then_inc(s_fall, 1)
            v.wait_ge(s_fallp, 1)
            V.tensor_scalar(unsorted[:, :], bank[7][:, 0:1], 1.0, None, ALU.min).then_inc(s_flag, 1)
            v.wait_ge(s_flag, 1)
            with v.If(v.value_load(unsorted[0:1, 0:1], min_val=0, max_val=1) > 0):
                V.memset(k_tile[:, :], 0.0).then_inc(k_step, 1)
                with v.Fori(0, Q) as a:
                    v.wait_ge(k_own, a * 80 + 80)
                    V.memset(k_rank[:, :], 0.0).then_inc(k_z, 1)
                    with v.Fori(0, Q) as b:
                        def counted(ins, n):
                            ins.then_inc(k_step, 1)
                            v.wait_ge(k_step, a * (Q * 6) + b * 6 + (n + 1))

                        v.wait_ge(k_z, a + 1)
                        v.wait_ge(k_chunk, a * (Q * 32) + b * 32 + 32)
                        counted(V.tensor_tensor(k_cmp, bc_mid(k_row[:, :], GQ), bc_last(k_dst[:, :], CH), ALU.subtract), 1)
                        counted(V.tensor_scalar(k_cmp, k_cmp, -1.0, 1.0, ALU.max, ALU.min), 2)
                        counted(V.scalar_tensor_tensor(k_cmp, k_cmp, float(FAR), bc_mid(k_rnum[:, :], GQ),
                                                       ALU.mult, ALU.add), 3)
                        counted(V.tensor_tensor(k_cmp, k_cmp, bc_last(k_num[:, :], CH), ALU.is_lt), 4)
                        counted(V.tensor_reduce(k_less[:, :], k_cmp, AX.X, ALU.add), 5)
                        counted(V.tensor_tensor(k_rank[:, :], k_rank[:, :], k_less[:, :], ALU.add), 6)

                    def placed(ins, n):
                        ins.then_inc(k_ps, 1)
                        v.wait_ge(k_ps, a * 7 + n)

                    placed(V.tensor_scalar(k_tile[:, :], k_rank[:, :], 1.0 / P, -(P - 1) / (2.0 * P), ALU.mult, ALU.add), 1)
                    placed(V.tensor_scalar(k_tile[:, :], k_tile[:, :], 1.5 * 2.0 ** 23, None, ALU.add), 2)
                    placed(V.tensor_scalar(k_tile[:, :], k_tile[:, :], -1.5 * 2.0 ** 23, None, ALU.add), 3)
                    placed(V.scalar_tensor_tensor(k_rank[:, :], k_tile[:, :], -float(P), k_rank[:, :], ALU.mult, ALU.add), 4)
                    placed(V.scalar_tensor_tensor(k_pos[:, :], k_rank[:, :], float(T), k_tile[:, :], ALU.mult, ALU.add), 5)
                    placed(V.tensor_copy(k_put[:, :], k_pos[:, :]), 6)
                    V.memset(k_less[:, :], 0.0).then_inc(k_ps, 1)
                v.wait_ge(k_tab, 80)
            V.tensor_copy(f_dst[:, :], t_dst[:, :]).then_inc(s_tabc, 1)
            V.tensor_copy(f_next[:, :], t_next[:, :])
            V.tensor_copy(f_key[:, :, GQ:2 * GQ], t_prev[:, :].rearrange("p (q c) -> p q c", c=GQ)).then_inc(s_tabc, 1)
            v.wait_ge(s_tabc, 2)
            V.tensor_copy(f_key[:, :, 0:GQ], f_dst[:, :].rearrange("p (q c) -> p q c", c=GQ))
            V.tensor_scalar(t_gat[:, :], f_dst[:, :], float(N - 1), None, ALU.min)
            V.tensor_tensor(f_put[:, :], f_dst[:, :], f_next[:, :], ALU.is_equal).then_inc(s_tabc, 1)
            v.wait_ge(s_tabc, 3)
            V.scalar_tensor_tensor(f_next[:, :], f_put[:, :], float(FAR), f_dst[:, :], ALU.mult, ALU.add) \
                .then_inc(s_tabc, 1)
            v.wait_ge(s_tabc, 4)
            V.tensor_copy(t_put[:, :], f_next[:, :]).then_inc(s_tabc, 2)
            v.wait_ge(s_rowps, 1)
            V.tensor_copy(t_row[0][0:TA, :], bank[6][0:TA, 0:P]).then_inc(s_rowsb, 1)
            if T > P:
                v.wait_ge(s_rowps, 2)
                V.tensor_copy(t_row[1][0:T - P, :], bank[7][0:T - P, 0:P]).then_inc(s_rowsb, 1)

            v.wait_ge(s_w, 16)
            V.memset(msg1[0][:, :], 0.0)
            V.memset(msg1[1][:, :], 0.0)
            V.memset(msg1s[:, :], 0.0).then_inc(s_mz, 1)
            LS, LV, I3, I6 = DS ** -0.5, DU ** -0.5, 3.0 ** -0.5, 6.0 ** -0.5
            C0, C1 = (DS + DU) ** -0.5, (3.0 / (DS + 2 * DU)) ** 0.5
            v.wait_ge(s_mz, 1)
            v.wait_ge(s_mp, 16)

            def piece(r, cols, into, at, factor):
                w = 32 * (r % 4)
                return V.tensor_scalar(into[w:w + 32, at:at + cols], bank[r // 4][w:w + 32, 0:cols], factor, None, ALU.mult)

            for r in range(16):
                if r < 2:
                    ins = piece(r, DS, msg1[0], 0, C0 * LS)
                elif r < 4:
                    ins = piece(r, DV, msg1[0], DS, C1 * I3 * LV)
                elif r < 5:
                    ins = piece(r, DV, msg1[1], DS, C1 * I3 * LV)
                elif r < 8:
                    ins = piece(r, DS, msg1[1], 0, C0 * I3 * LS)
                elif r < 11:
                    ins = piece(r, DV, msg1[2], 0, C1 * I6 * LV)
                elif r < 12:
                    ins = piece(r, DV, msg1[2], 0, -C1 * I6 * LV)
                elif r < 14:
                    ins = piece(r, DV, msg1[3], 0, -C1 * I6 * LV)
                else:
                    ins = piece(r, DU, msg1s, 0, C1 * I3 * LV)
            V.memset(msg1[3][DS:P, :], 0.0).then_inc(s_mc, 1)
            for w in (W_SC, W_L1):
                V.tensor_scalar(wp[:, w:w + DS], wp[:, w:w + DS], LS, None, ALU.mult)
                V.tensor_scalar(wp[:, w + DS:w + D], wp[:, w + DS:w + D], LV, None, ALU.mult)
                V.tensor_scalar(wp[:, w + D:w + D + 4 * DS], wp[:, w + D:w + D + 4 * DS], LS, None, ALU.mult)
            V.tensor_scalar(wp[:, W_FC2:W_FC2 + 384], wp[:, W_FC2:W_FC2 + 384], DS ** -0.5, None, ALU.mult)
            FS = 0.25 * float(DV) ** -0.5
            V.tensor_scalar(wp[:, W_R1:W_R1 + 32], wp[:, W_R1:W_R1 + 32], FS, None, ALU.mult)
            V.tensor_scalar(wp[:, W_R1 + 32:W_R1 + 33], wp[:, W_R1 + 32:W_R1 + 33], 0.1 * FS, None, ALU.mult)
            V.tensor_scalar(wp[:, W_R1 + 33:W_R1 + 97], wp[:, W_R1 + 33:W_R1 + 97], FS, None, ALU.mult)
            V.tensor_scalar(wp[:, W_R2:W_R2 + 96], wp[:, W_R2:W_R2 + 96], FS, None, ALU.mult)
            for w in (W_R2 + 96, W_R3):
                V.tensor_scalar(wp[:, w:w + 1], wp[:, w:w + 1], 0.1 * FS * I3, None, ALU.mult)
                V.tensor_scalar(wp[:, w + 1:w + 65], wp[:, w + 1:w + 65], FS * I3, None, ALU.mult)
            V.memset(tot[1][:, :], 0.0).then_inc(s_wscaled, 1)
            v.wait_ge(s_wscaled, 1)
            V.memset(df1[0][:, :], 0.0).then_inc(e_z, 1)
            v.wait_ge(e_z, 1)

            def dense_stats(u):
                j = u.mod(4)
                v.wait_ge(d_in[j], u.over(4, 16, 16))
                for k in range(GD):
                    ins = V.bn_stats(st1[j][:, k, :], x_in[j][:, k * XW:k * XW + D])
                ins.then_inc(d_ln1, 1)
                moments(st1[j], su1[j], df1[j], sq1[j], m21[j], neg1[j], var1[j], GD, d_ln1, lambda n: u.times(5, n))
                rest_of(hr[u.mod(2)], x_in[j], neg1[j], GD, d_ln1)

            def dense_x1(u, h):
                j = u.mod(2)
                v.wait_ge(d_scl, u.times(2, 2))
                wait(v, d_y, u.times(2, h - 3))
                x, scl = x_in[u.mod(4)], scl1[u.mod(4)]
                for pair in range(2 * h, 2 * h + 2):
                    v.wait_ge(d_mm, u.times(4, pair + 1))
                    for k in (2 * pair, 2 * pair + 1):
                        ins = V.scalar_tensor_tensor(x1[j][:, k * D:(k + 1) * D], bank[2 + pair % 2][:, k % 2 * D:(k % 2 + 1) * D],
                                                     scl[:, k:k + 1], x[:, k * XW:k * XW + D], ALU.mult, ALU.add)
                    ins.then_inc(d_x1, 1)
                for pair in range(2 * h, 2 * h + 2):
                    v.wait_ge(d_x1, u.times(4, pair + 1))
                    for k in (2 * pair, 2 * pair + 1):
                        ins = V.bn_stats(st2[j][:, k, :], x1[j][:, k * D:(k + 1) * D])
                if h == 1:
                    ins.then_inc(d_ln2, 1)

            def dense_moments2(u):
                j = u.mod(2)
                moments(st2[j], su2[j], df2[j], sq2[j], m22[j], neg2[j], var2[j], GD, d_ln2, lambda n: u.times(4, n))

            def selectors(j, loaded, value, signal):
                v.wait_ge(loaded, value)
                for t in range(GQ):
                    V.tensor_scalar(same[t][j][:, :], q_row[j][:, t * P:(t + 1) * P], q_key[j][:, t:t + 1], None,
                                    ALU.is_equal)
                    ins = V.tensor_scalar(carry[t][j][:, :], q_row[j][:, t * P:(t + 1) * P],
                                          q_key[j][:, GQ + t:GQ + t + 1], None, ALU.is_equal)
                ins.then_inc(signal, 1)

            def p1_prepare(q):
                j = q.mod(2)
                v.wait_ge(e_g[j], q.over(2, 64, 64))
                for t in range(GQ):
                    ins = V.bn_stats(st_e[j][:, t, :], x_e[j][:, t * XW:t * XW + D])
                ins.then_inc(e_ln, 1)
                moments(st_e[j], su_e[j], df_e[j], sq_e[j], m2_e[j], neg_e[j], var_e[j], GQ, e_ln,
                        lambda n: q.times(5, n))
                rest_of(hr_e[j], x_e[j], neg_e[j], GQ, e_ln)

            def p1_selectors(q):
                wait(v, e_seg, q.times(GQ, -GQ))
                selectors(q.mod(2), e_tb[q.mod(2)], q.over(2, 48, 48), e_sc)

            def p1_message(n):
                j, t = n.c // GQ % 2, n.mod(4)
                v.wait_ge(e_xb, n.times(1, 1))
                x = xr[n.mod(2)]
                V.tensor_tensor(x[:, 65:161].rearrange("p (u i) -> p u i", i=3), bc_last(bank[7][:, U_C:U_C + DU], 3),
                                bc_mid(ed(j, t, 1, 4), DU), ALU.mult).then_inc(e_vx, 1)
                v.wait_ge(e_vx, n.times(1, 1))
                wait(v, e_seg, n.times(1, -1))
                V.scalar_tensor_tensor(v_e[n.mod(2)][:, :], bank[7][:, U_A:U_A + CW], ed(j, t, 0, 1), x[:, :],
                                       ALU.mult, ALU.add).then_inc(e_v, 1)

            def p1_features(n):
                j, t = n.c // GQ % 2, n.mod(4)
                v.wait_ge(e_gg, n.times(1, 1))
                wait(v, e_ftr, n.times(1, -1))
                g, w, f = g_e[n.mod(2)], bank[5 + n.mod(2)][:, D:D + 192], feat[n.mod(2)]
                V.tensor_tensor(f[:, 128:320].rearrange("p (a u i) -> p a u i", a=2, i=3),
                                w[:, 128:192].rearrange("p (a u) -> p a u", a=2).unsqueeze(3).to_broadcast([P, 2, DU, 3]),
                                g[:, DS:D].rearrange("p (u i) -> p u i", i=3).unsqueeze(1).to_broadcast([P, 2, DU, 3]),
                                ALU.mult).then_inc(e_fm, 1)
                V.tensor_tensor(f[:, 0:128].rearrange("p (a u) -> p a u", a=2), w[:, 0:128].rearrange("p (a u) -> p a u", a=2),
                                bc_mid(g[:, 0:DS], 2), ALU.mult)
                v.wait_ge(e_fm, n.times(1, 1))
                V.tensor_tensor(f[:, 224:320].rearrange("p (u i) -> p u i", i=3),
                                f[:, 224:320].rearrange("p (u i) -> p u i", i=3),
                                bc_mid(ed(j, t, 1, 4), DU), ALU.mult).then_inc(e_ft, 1)

            def slot(u, h):
                s = At(u.i, 2 * u.c + h, 8)
                if (u - 1).within(U):
                    dense_x1(u - 1, h)
                if (s - 2).within(T):
                    p1_message(s - 2)
                if s.within(T):
                    if s.mod(4) == 0:
                        v.wait_ge(e_sc, s.over(4, 1, 1))
                    p1_features(s)

            def step(u):
                q = At(u.i, u.c // 2, 2)
                odd = u.mod(2) == 1
                slot(u, 0)
                if (u + 1).within(U):
                    dense_stats(u + 1)
                slot(u, 1)
                if (u - 1).within(U):
                    dense_moments2(u - 1)
                if not odd and (q + 1).within(Q):
                    p1_prepare(q + 1)
                if odd and (q + 1).within(Q):
                    p1_selectors(q + 1)

            dense_stats(At(0, 0))
            p1_prepare(At(0, 0, 2))
            p1_selectors(At(0, 0, 2))
            for u in range(4):
                step(At(0, u))
            with v.Fori(1, U // 4) as i:
                for c in range(4):
                    step(At(i, c))
            for u in range(U - 2, U + 2):
                step(At(0, u))

            PI2 = 6.283185307179586
            CA = 6.28125
            CB = 0.0019350051879882812
            CC = PI2 - CA - CB
            ROUND = 1.5 * 2.0 ** 23
            PI_IN = 3.1415925

            def p2_prepare(q):
                j = q.mod(2)
                v.wait_ge(r_g[j], q.over(2, 64, 64))
                for t in range(GQ):
                    ins = V.bn_stats(st_e[j][:, t, :], x_e[j][:, t * XW:t * XW + D])
                ins.then_inc(r_ln1, 1)
                moments(st_e[j], su_e[j], df_e[j], sq_e[j], m2_e[j], neg_e[j], var_e[j], GQ, r_ln1,
                        lambda n: q.times(5, n))
                rest_of(hr_e[j], x_e[j], neg_e[j], GQ, r_ln1)
                v.wait_ge(r_cv[j], q.over(2, 16, 16))
                ang, turns, rest, arg = (trig[n][j] for n in range(4))

                def link(ins, n):
                    ins.then_inc(r_ang, 1)
                    v.wait_ge(r_ang, q.times(8, n))

                link(V.tensor_tensor(ang[:, 0:GQ], x3(cv[j], CW, GQ)[:, :, 0], x3(x_e[j], XW, GQ)[:, :, D], ALU.mult), 1)
                link(V.tensor_scalar(turns[:, 0:GQ], ang[:, 0:GQ], 1.0 / PI2, ROUND, ALU.mult, ALU.add), 2)
                link(V.tensor_scalar(turns[:, GQ:2 * GQ], turns[:, 0:GQ], -ROUND, None, ALU.add), 3)
                k = turns[:, GQ:2 * GQ]
                link(V.scalar_tensor_tensor(rest[:, 0:GQ], k, -CA, ang[:, 0:GQ], ALU.mult, ALU.add), 4)
                link(V.scalar_tensor_tensor(rest[:, GQ:2 * GQ], k, -CB, rest[:, 0:GQ], ALU.mult, ALU.add), 5)
                link(V.scalar_tensor_tensor(ang[:, GQ:2 * GQ], k, -CC, rest[:, GQ:2 * GQ], ALU.mult, ALU.add), 6)
                link(V.tensor_scalar(arg[:, 0:GQ], ang[:, GQ:2 * GQ], PI_IN, -PI_IN, ALU.min, ALU.max), 7)
                V.tensor_scalar(arg[:, GQ:2 * GQ], arg[:, 0:GQ], 0.5, None, ALU.mult).then_inc(r_ang, 1)

            def p2_x1(q):
                j = q.mod(2)
                sines, half2, scales = trig[4][j], trig[5][j], trig[6][j]
                attr = x3(x_e[j], XW, GQ)[:, :, D]

                def link(ins, n):
                    ins.then_inc(r_scl, 1)
                    v.wait_ge(r_scl, q.times(4, n))

                v.wait_ge(r_inv, q.times(1, 1))
                v.wait_ge(r_sin, q.times(1, 1))
                V.tensor_tensor(scales[:, GQ:2 * GQ], sines[:, 0:GQ], attr, ALU.mult)
                link(V.tensor_tensor(half2[:, 0:GQ], sines[:, GQ:2 * GQ], sines[:, GQ:2 * GQ], ALU.mult), 1)
                V.tensor_tensor(scl_e[j][:, :], inv_e[j][:, :], attr, ALU.mult)
                link(V.tensor_scalar(half2[:, GQ:2 * GQ], half2[:, 0:GQ], -2.0, 1.0, ALU.mult, ALU.add), 2)
                link(V.tensor_tensor(scales[:, 0:GQ], scl_e[j][:, :], half2[:, GQ:2 * GQ], ALU.mult), 3)
                v.wait_ge(r_mm, q.times(1, 1))
                wait(v, r_y, q.times(1, -1))
                part = part2[j]
                for t in range(GQ):
                    ins = V.scalar_tensor_tensor(part[:, t * D:(t + 1) * D], bank[2 + 2 * j + t // 2][:, t % 2 * D:(t % 2 + 1) * D],
                                                 scales[:, t:t + 1], x_e[j][:, t * XW:t * XW + D], ALU.mult, ALU.add)
                link(ins, 4)
                for t in range(GQ):
                    ins = V.scalar_tensor_tensor(x1[j][:, t * D:(t + 1) * D], cv[j][:, t * CW + 1:(t + 1) * CW],
                                                 scales[:, GQ + t:GQ + t + 1], part[:, t * D:(t + 1) * D],
                                                 ALU.mult, ALU.add)
                ins.then_inc(r_x1, 2)
                v.wait_ge(r_x1, q.times(2, 2))
                for t in range(GQ):
                    ins = V.bn_stats(st2[j][:, t, :], x1[j][:, t * D:(t + 1) * D])
                ins.then_inc(r_ln2, 1)
                moments(st2[j], su2[j], df2[j], sq2[j], m22[j], neg2[j], var2[j], GQ, r_ln2, lambda n: q.times(4, n))

            def p2_y(q):
                j = q.mod(2)
                v.wait_ge(r_h1, q.times(1, 1))
                wait(v, r_sty[j], q.over(2, 16))
                V.tensor_tensor(yo[j][:, 0:GQ * D], x1[j][:, 0:GQ * D], h1[j][:, 0:GQ * D], ALU.add).then_inc(r_y, 1)

            def p2_step(q, a=True, d=True, y=True):
                if a:
                    p2_prepare(q)
                if y:
                    p2_y(q - 2)
                if d:
                    p2_x1(q - 1)

            for j in range(2):
                v.wait_ge(d_sth[j], 16 * (U // 2))
                v.wait_ge(d_sto[j], 16 * (U // 2))
            p2_step(At(0, 0, 2), d=False, y=False)
            p2_step(At(0, 1, 2), y=False)
            with v.Fori(1, (Q - 1) // 2) as i:
                for c in range(2):
                    p2_step(At(i, c, 2))
            p2_step(At(0, Q - 1, 2))
            p2_step(At(0, Q, 2), a=False)
            p2_step(At(0, Q + 1, 2), a=False, d=False)
            for j in range(2):
                v.wait_ge(r_sty[j], 16 * ((Q + 1 - j) // 2))

            V.memset(tot[1][:, :], 0.0).then_inc(m_z, 1)

            def p3_features(n):
                j, t = n.c // 4 % 2, n.mod(4)
                if t == 0:
                    wait(v, m_seg, n.times(1, -GQ))
                    selectors(j, m_tb[j], n.over(8, 48, 48), m_sc)
                    v.wait_ge(m_g[j], n.over(8, 64, 64))
                wait(v, m_ftr, n.times(1, -1))
                f, h = feat[n.mod(2)], h1[j][:, t * D:(t + 1) * D]
                V.tensor_scalar(f[:, 0:D], h, ed(j, t, 0, 1), None, ALU.mult)
                turned = bass.AP(tensor=q_ed[j], offset=t * EW + 1, ap=[[GQ * EW, P], [1, 3], [0, DU], [1, 3]])
                V.tensor_tensor(f[:, D:D + 3 * DV].rearrange("p (s u i) -> p s u i", s=3, i=3),
                                h[:, DS:D].rearrange("p (u i) -> p u i", i=3).unsqueeze(1).to_broadcast([P, 3, DU, 3]),
                                turned, ALU.mult).then_inc(m_ft, 1)

            def p3_message(n):
                j, t = n.c // 4 % 2, n.mod(4)
                b = bank[2 + n.mod(2)]
                v.wait_ge(m_u, n.times(1, 1))
                x = xr[n.mod(2)]
                v.wait_ge(m_cs, n.times(1, 1))
                V.tensor_tensor(x[:, 0:DV].rearrange("p (u i) -> p u i", i=3), bc_last(b[:, D:D + DU], 3),
                                bc_mid(ed(j, t, 1, 4), DU), ALU.mult).then_inc(m_vx, 1)
                v.wait_ge(m_vx, n.times(1, 1))
                wait(v, m_seg, n.times(1, -1))
                V.tensor_tensor(v_e[n.mod(2)][:, DS:D], b[:, DS:D], x[:, 0:DV], ALU.add).then_inc(m_v, 1)

            def p3_out(n):
                j, t = n.c // 4 % 2, n.mod(4)
                if t == 0:
                    v.wait_ge(m_y[j], n.over(8, 16, 16))
                    wait(v, m_put[j], n.over(8, 64))
                v.wait_ge(m_tot, n.times(1, 1))
                V.scalar_tensor_tensor(yo[j][:, t * D:(t + 1) * D], bank[4 + n.mod(2)][:, 0:D], 0.0,
                                       x1[j][:, t * D:(t + 1) * D], ALU.max, ALU.add).then_inc(m_o, 1)

            def p3_slot(n, lo=0, hi=4):
                if lo <= 2 < hi:
                    p3_message(n - 2)
                if lo <= 0 < hi:
                    p3_features(n)
                if lo <= 3 < hi:
                    p3_out(n - 3)

            for n in range(8):
                p3_slot(At(0, n, 8), 0, n + 1)
            with v.Fori(1, (Q - 1) // 2) as i:
                for c in range(8):
                    p3_slot(At(i, c, 8))
            for n in range(T - GQ, T + 3):
                p3_slot(At(0, n, 8), max(0, n - T + 1))


def pack_weights(np, w):
    pack = np.zeros((P, W_END), np.float32)
    u3 = np.arange(DU) * 3

    def kron(a, shift=0):
        k = np.zeros((DV, DV), np.float32)
        for i in range(3):
            k[np.ix_(u3 + i, u3 + (i + shift) % 3)] = a
        return k

    for col, w0, w1 in ((W_SC, "L0_gnn_sc_w0", "L0_gnn_sc_w1"), (W_L1, "L0_gnn_lin1_w0", "L0_gnn_lin1_w1")):
        pack[0:32, col:col + DS] = w[w0][32:64]
        pack[32:128, col + DS:col + D] = kron(w[w1])
        for t in range(4):
            pack[32 * t:32 * t + 32, col + D + t * DS:col + D + (t + 1) * DS] = w[w0][0:32]
    for t in range(4):
        pack[8 * t:8 * t + 8, W_FC1 + 64 * t:W_FC1 + 64 * (t + 1)] = w["L0_gnn_fc_w1"]
    for h in range(2):
        pack[64 * h:64 * h + 64, W_FC2 + 192 * h:W_FC2 + 192 * (h + 1)] = w["L0_gnn_fc_w2"]
    lin2a, lin2b, lin3 = w["L0_gnn_lin2_w0"], w["L0_gnn_lin2_w1"], w["L0_gnn_lin3_w"]
    rest = np.repeat(np.concatenate([lin3[64:], lin2a[64:]], 1), 3, 0)
    pack[64:128, W_R1:W_R1 + 32] = lin2b[0:64]
    pack[0:64, W_R1 + 32:W_R1 + 33] = lin3[0:64]
    pack[0:64, W_R1 + 33:W_R1 + 97] = lin2a[0:64]
    pack[0:96, W_R2:W_R2 + 96] = kron(lin2b[64:])
    pack[96:128, W_R2 + 96:W_R2 + 161] = rest[0:32]
    pack[64:128, W_R3:W_R3 + 65] = rest[32:96]
    pack[0:64, W_W1T:W_W1T + 64] = w["L1_gnn_W1"].T
    pack[0:64, W_W2T:W_W2T + 96] = np.repeat(w["L1_gnn_W2"].T, 3, 1)
    pack[0:32, W_W3T:W_W3T + 64] = w["L1_gnn_W3"].T
    pack[0:96, W_W4T:W_W4T + 96] = kron(w["L1_gnn_W4"].T)
    pack[0:96, W_W5T:W_W5T + 96] = kron(w["L1_gnn_W5"].T)
    pack[0:64, W_WS:W_WS + 64] = w["L1_gnn_Ws"]
    pack[0:96, W_WVK:W_WVK + 96] = kron(w["L1_gnn_Wv"])
    pack[0:32, W_WV:W_WV + 32] = w["L1_gnn_Wv"]
    pack[0:96, W_WVA:W_WVA + 96] = kron(w["L1_gnn_Wv"], 2)
    pack[0:96, W_WVB:W_WVB + 96] = kron(w["L1_gnn_Wv"], 1)
    return pack


def kernel(**inputs):
    import numpy as np
    import concourse.bacc as bacc
    from concourse.bass_utils import run_bass_kernel_spmd as run

    w = {k: np.asarray(v) for k, v in inputs.items()}
    N, E = w["x"].shape[0], w["src"].shape[0]
    T = -(-E // (P * GQ)) * GQ
    pad = T * P - E

    def by_tile(a, fill):
        a = np.concatenate([a, np.full((pad,) + a.shape[1:], fill, a.dtype)])
        return np.ascontiguousarray(np.swapaxes(a.reshape((T, P) + a.shape[1:]), 0, 1))

    y, rows = w["edge_attr_4"], by_tile(w["edge_attr_8"], 0)
    arrays = {
        "xa": np.ascontiguousarray(np.concatenate([w["x"], w["node_vec1"]], 1)),
        "src": by_tile(w["src"].astype(np.int32), 0),
        "dst": by_tile(w["dst"].astype(np.int32), N),
        "number": np.ascontiguousarray(np.arange(T * P, dtype=np.float32).reshape(T, P).T),
        "edges_in": by_tile(np.concatenate([y, y[:, 1:3]], 1), 0),
        "scalars_in": rows,
        "scalars_t_in": np.ascontiguousarray(rows.reshape(P, T // GQ, GQ * SW).transpose(1, 2, 0)),
        "wpack": pack_weights(np, w),
    }
    nc = bacc.Bacc("TRN2", target_bir_lowering=False, num_devices=1)
    aps = {k: nc.dram_tensor(f"in_{k}", a.shape, mybir.dt.from_np(a.dtype), kind="ExternalInput").ap()
           for k, a in arrays.items()}
    out = nc.dram_tensor("out", (N, D), mybir.dt.float32, kind="ExternalOutput").ap()
    gnn_kernel(nc, out=out, **aps)
    r = run(nc, [{f"in_{k}": a for k, a in arrays.items()}], core_ids=[0])
    return r.results[0]["out"]
```

```python
from contextlib import ExitStack

import concourse.bass as bass
from concourse import mybir

P = 128
GD = 8
GQ = 4
D = 160
DS, DU, DV = 64, 32, 96
XW = D + 1
EW = 6
SW = 8
CW = D + 1
EPS = 1e-5
FAR = 1 << 20

W_SC, W_L1, W_FC1, W_FC2, W_R1, W_R2, W_R3 = 0, 416, 832, 1088, 1472, 1569, 1730
W_W1T, W_W2T, W_W3T, W_W4T, W_W5T = 1795, 1859, 1955, 2019, 2115
W_WS, W_WVK, W_WV, W_WVA, W_WVB, W_END = 2211, 2275, 2371, 2403, 2499, 2595

U_C, U_A, U_D, U_B = 0, 32, 97, 193
U_SEG = 2 * P


class At:

    def __init__(self, i, c, period=4):
        self.i, self.c, self.period = i + c // period, c % period, period

    def __add__(self, n):
        return At(self.i, self.c + n, self.period)

    def __sub__(self, n):
        return At(self.i, self.c - n, self.period)

    def times(self, m, plus=0):
        return self.i * (self.period * m) + (self.c * m + plus)

    def over(self, k, m=1, plus=0):
        return self.i * (self.period // k * m) + (self.c // k * m + plus)

    def mod(self, k):
        return self.c % k

    def within(self, count):
        return not isinstance(self.i, int) or 0 <= self.i * self.period + self.c < count


def wait(eng, sem, value):
    if not (isinstance(value, int) and value <= 0):
        eng.wait_ge(sem, value)


def gnn_kernel(nc, xa, src, dst, number, edges_in, scalars_in, scalars_t_in, wpack, out):
    f32, i32 = mybir.dt.float32, mybir.dt.int32
    ALU, ACT, AX = mybir.AluOpType, mybir.ActivationFunctionType, mybir.AxisListType
    N = xa.shape[0]
    T = src.shape[1]
    Q = T // GQ
    UROWS = P * GD
    U = -(-N // UROWS)
    assert U == 2 * Q and Q % 4 == 1 and Q >= 13
    TA = min(T, P)

    def scratch(name, shape, dt=f32):
        return nc.dram_tensor(name, shape, dt).ap()

    src_tab = scratch("src_tab", (Q, P, GQ), i32)
    dst_tab = scratch("dst_tab", (Q, P, GQ), i32)
    put_tab = scratch("put_tab", (Q, P, GQ), i32)
    key_tab = scratch("key_tab", (Q, P, 2 * GQ))
    row_tab = scratch("row_tab", (T, P))
    sum_tab = scratch("sum_tab", (Q, P, GQ * CW))
    y_tab = scratch("y_tab", (Q, P, GQ * D))
    h1_all = scratch("h1_all", (N, D))

    edges = scratch("edges", (P, T, EW))
    scalars_t = scratch("scalars_t", (Q, GQ * SW, P))
    scalars_sorted = scratch("scalars_sorted", (P, T, SW))
    src_sorted = scratch("src_sorted", (P, T), i32)
    dst_sorted = scratch("dst_sorted", (P, T), i32)

    CH = GQ * P
    dst_c = dst.rearrange("p t -> (p t)").rearrange("(b f) -> b f", f=CH)
    number_c = number.rearrange("p t -> (p t)").rearrange("(b f) -> b f", f=CH)

    row_q = row_tab.rearrange("(q c) p -> q (c p)", c=GQ)
    ed_q = edges.rearrange("p (q c) f -> q p (c f)", c=GQ)
    NU = U - 1
    x_u = xa[0:NU * UROWS, :].rearrange("(u p g) f -> u p (g f)", p=P, g=GD)
    o_u = out[0:NU * UROWS, :].rearrange("(u p g) f -> u p (g f)", p=P, g=GD)
    h_u = h1_all[0:NU * UROWS, :].rearrange("(u p g) f -> u p (g f)", p=P, g=GD)
    x_l = xa[N - UROWS:N, :].rearrange("(p g) f -> p (g f)", p=P)
    o_l = out[N - UROWS:N, :].rearrange("(p g) f -> p (g f)", p=P)
    h_l = h1_all[N - UROWS:N, :].rearrange("(p g) f -> p (g f)", p=P)

    with ExitStack() as ctx:
        def sb(name, shape, dt=f32):
            return ctx.enter_context(nc.sbuf_tensor(name, shape, dt))

        def two(name, shape, dt=f32):
            return [sb(f"{name}{i}", shape, dt) for i in range(2)]

        def four(name, shape, dt=f32):
            return [sb(f"{name}{i}", shape, dt) for i in range(4)]

        def sem(name):
            return ctx.enter_context(nc.semaphore(name))

        def sem2(name):
            return [sem(f"{name}{i}") for i in range(2)]

        bank = [ctx.enter_context(nc.psum_tensor(f"bank{i}", [P, 512], f32)) for i in range(8)]

        wp = sb("wp", [P, W_END])
        ident = sb("ident", [P, P])
        msg1 = [sb("msg1a", [P, D]), sb("msg1b", [P, D]), sb("msg1c", [P, DV]), sb("msg1d", [P, DV])]
        msg1s = sb("msg1s", [P, DU])
        t_src = sb("t_src", [P, T], i32)
        t_dst = sb("t_dst", [P, T], i32)
        t_next = sb("t_next", [P, T], i32)
        t_prev = sb("t_prev", [P, T], i32)
        t_gat = sb("t_gat", [P, T], i32)
        t_put = sb("t_put", [P, T], i32)
        f_dst = sb("f_dst", [P, T])
        f_next = sb("f_next", [P, T])
        f_put = sb("f_put", [P, T])
        f_key = sb("f_key", [P, Q, 2 * GQ])
        t_row = two("t_row", [P, P])
        minus_half = sb("minus_half", [P, GD])
        ones = sb("ones", [P, P])
        falls = sb("falls", [P, T])
        fall = sb("fall", [P, 1])
        unsorted = sb("unsorted", [P, 1], i32)
        k_dst = sb("k_dst", [P, GQ], i32)
        k_src = sb("k_src", [P, GQ], i32)
        k_num = sb("k_num", [P, GQ])
        k_ed = sb("k_ed", [P, GQ, EW])
        k_sc = sb("k_sc", [P, GQ, SW])
        k_row = sb("k_row", [P, CH], i32)
        k_rnum = sb("k_rnum", [P, CH])
        k_less = sb("k_less", [P, GQ])
        k_rank = sb("k_rank", [P, GQ])
        k_tile = sb("k_tile", [P, GQ])
        k_pos = sb("k_pos", [P, GQ])
        k_put = sb("k_put", [P, GQ], i32)
        x_all = sb("x_all", [P, 4 * GD * XW])
        x_in = [x_all[:, i * GD * XW:(i + 1) * GD * XW] for i in range(4)]
        k_cmp = x_all[:, 2 * GD * XW:2 * GD * XW + GQ * CH].rearrange("p (c f) -> p c f", c=GQ)
        st1, st2 = four("st1", [P, GD, 6]), two("st2", [P, GD, 6])
        su1, su2 = four("su1", [P, GD, 2]), two("su2", [P, GD, 2])
        df1, df2 = four("df1", [P, GD]), two("df2", [P, GD])
        sq1, sq2 = four("sq1", [P, GD]), two("sq2", [P, GD])
        m21, m22 = four("m21", [P, GD]), two("m22", [P, GD])
        neg1, neg2 = four("neg1", [P, GD]), two("neg2", [P, GD])
        var1, var2 = four("var1", [P, GD]), two("var2", [P, GD])
        inv1, inv2 = four("inv1", [P, GD]), two("inv2", [P, GD])
        scl1, nmr2 = four("scl1", [P, GD]), two("nmr2", [P, GD])
        hb = two("hb", [P, GD * P])
        hr = two("hr", [P, GD * 32])
        hT = two("hT", [P, 512])
        hR = two("hR", [P, P])
        x1 = two("x1", [P, GD * D])
        h1 = two("h1", [P, GD * D])
        yo = two("yo", [P, GD * D])
        i_src = two("i_src", [P, GQ], i32)
        i_dst = four("i_dst", [P, GQ], i32)
        i_put = two("i_put", [P, GQ], i32)
        q_key = two("q_key", [P, 2 * GQ])
        q_row = two("q_row", [P, GQ * P])
        q_ed = two("q_ed", [P, GQ * EW])
        q_sct = two("q_sct", [GQ * SW, P])
        q_hid = two("q_hid", [P, 256])
        same = two("same", [P, GQ * P])
        carry = two("carry", [P, GQ * P])
        x_e = two("x_e", [P, GQ * XW])
        h_e = sb("h_e", [P, GQ * P])
        hr_e = two("hr_e", [P, GQ * 32])
        part2 = two("part2", [P, GQ * D])
        eT = two("eT", [P, 512])
        eR = two("eR", [P, P])
        g_e = two("g_e", [P, D])
        feat = two("feat", [P, 512])
        fT = two("fT", [P, 512])
        xr = two("xr", [P, CW])
        v_e = two("v_e", [P, CW])
        tot = two("tot", [P, GQ * CW])
        x_q = [x_all[:, i * GQ * XW:(i + 1) * GQ * XW] for i in range(4)]
        cv = [c[:, :] for c in two("cv", [P, GQ * CW])] + [hb[i][:, 0:GQ * CW] for i in range(2)]
        trig = [two(f"trig{n}", [P, 2 * GQ]) for n in range(8)]

        st_e = two("st_e", [P, GQ, 6])
        su_e = two("su_e", [P, GQ, 2])
        df_e = two("df_e", [P, GQ])
        sq_e = two("sq_e", [P, GQ])
        m2_e = two("m2_e", [P, GQ])
        neg_e = two("neg_e", [P, GQ])
        var_e = two("var_e", [P, GQ])
        sd_e = two("sd_e", [P, GQ])
        sd2 = two("sd2", [P, GQ])
        inv_e = two("inv_e", [P, GQ])
        scl_e = two("scl_e", [P, GQ])

        s_w = sem("weights_loaded")
        s_tab_in = sem("edge_tables_loaded")
        s_fill = sem("table_edges_filled")
        s_id = sem("identity_built")
        s_tabc = sem("tables_computed")
        s_wscaled = sem("weights_scaled")
        s_rowps = sem("rows_transposed")
        s_rowsb = sem("rows_copied")
        s_tab_out = sem("tables_stored")
        s_turn = sem("indirect_dmas_may_start")
        s_mz = sem("message_weights_cleared")
        s_mp = sem("message_weights_multiplied")
        s_mc = sem("message_weights_copied")

        s_ones = sem("ones_built")
        s_fall = sem("falls_counted")
        s_fallp = sem("falls_summed")
        s_flag = sem("unsorted_known")
        s_rows = sem("edge_rows_copied")
        k_own = sem("sort_keys_loaded")
        k_chunk = sem("sort_chunk_loaded")
        k_z = sem("sort_count_cleared")
        k_step = sem("sort_count_steps")
        k_ps = sem("sort_place_steps")
        k_sct = sem("sort_rows_scattered")
        k_sct2 = sem("sorted_scalars_transposed")
        k_go = sem("sort_quad_may_start")
        k_tab = sem("sorted_tables_loaded")

        block = ctx.enter_context(nc.Block())

        n_in = sem2("net_scalars_loaded")
        n_mm = sem("net_products_done")
        n_act = sem("net_hidden_ready")
        d_in = [sem(f"x_loaded{i}") for i in range(4)]
        d_ln1 = sem("dense_moments1")
        d_relu = sem("dense_h_ready")
        d_tr = sem("dense_h_transposed")
        d_hT = sem("dense_hT_copied")
        d_mm = sem("dense_product_done")
        d_scl = sem("dense_scale_ready")
        d_nmr = sem("dense_norm2_ready")
        d_x1 = sem("dense_x1_ready")
        d_ln2 = sem("dense_moments2")
        d_h1 = sem("dense_h1_ready")
        d_y = sem("dense_y_ready")
        d_sth = sem2("dense_h1_stored")
        d_sto = sem2("dense_out_stored")
        e_ix = sem2("p1_index_loaded")
        e_tb = sem2("p1_tables_loaded")
        e_scl = sem("p1_scale_ready")
        e_g = sem2("p1_source_rows")
        e_ln = sem("p1_moments")
        e_relu = sem("p1_h_ready")
        e_sc = sem("p1_selectors_ready")
        e_tr = sem("p1_h_transposed")
        e_hT = sem("p1_hT_copied")
        e_pw = sem("p1_products_done")
        e_gg = sem("p1_g_ready")
        e_fm = sem("p1_feature_step")
        e_ft = sem("p1_features_ready")
        e_ftr = sem("p1_features_transposed")
        e_fte = sem("p1_featuresT_copied")
        e_u = sem("p1_message_parts_done")
        e_xb = sem("p1_rest_copied")
        e_vx = sem("p1_rest_ready")
        e_v = sem("p1_message_ready")
        e_seg = sem("p1_sum_done")
        e_tot = sem("p1_sum_copied")
        e_st = sem2("p1_sum_stored")
        e_z = sem("p1_first_carry_cleared")
        r_ix = [sem(f"p2_index_loaded{i}") for i in range(4)]
        r_px = sem2("p2_put_loaded")
        r_cv = [sem(f"p2_sums_loaded{i}") for i in range(4)]
        r_g = [sem(f"p2_node_rows{i}") for i in range(4)]
        r_ln1 = sem("p2_moments1")
        r_sq1 = sem("p2_root1_ready")
        r_sq2 = sem("p2_root2_ready")
        r_nmr = sem("p2_norm2_ready")
        r_ang = sem("p2_angle_steps")
        r_relu = sem("p2_h_ready")
        r_sin = sem("p2_sines_ready")
        r_tr = sem("p2_h_transposed")
        r_hT = sem("p2_hT_copied")
        r_mm = sem("p2_product_done")
        r_scl = sem("p2_scale_steps")
        r_x1 = sem("p2_x1_steps")
        r_ln2 = sem("p2_moments2")
        r_h1 = sem("p2_h1_ready")
        r_y = sem("p2_y_ready")
        r_put = sem2("p2_h1_scattered")
        r_sty = sem2("p2_y_stored")
        m_ix = sem2("p3_index_loaded")
        m_px = sem2("p3_put_loaded")
        m_tb = sem2("p3_tables_loaded")
        m_y = sem2("p3_y_loaded")
        m_g = sem2("p3_h1_rows")
        m_sc = sem("p3_selectors_ready")
        m_ft = sem("p3_features_ready")
        m_ss = sem("p3_scalars_copied")
        m_ftr = sem("p3_features_transposed")
        m_fte = sem("p3_featuresT_copied")
        m_u = sem("p3_message_parts_done")
        m_vx = sem("p3_outer_part_ready")
        m_v = sem("p3_message_ready")
        m_seg = sem("p3_sum_done")
        m_tot = sem("p3_sum_copied")
        m_o = sem("p3_out_ready")
        m_put = sem2("p3_out_scattered")
        m_z = sem("p3_first_carry_cleared")

        def x3(t, w, g):
            return t[:, :].rearrange("p (g f) -> p g f", g=g, f=w)

        def ed(par, t, a, b):
            return q_ed[par][:, t * EW + a:t * EW + b]

        def bc_mid(ap, n):
            return ap.unsqueeze(1).to_broadcast([P, n, ap.shape[1]])

        def bc_last(ap, n):
            return ap.unsqueeze(2).to_broadcast([P, ap.shape[1], n])

        @block.sync
        def _(sp):
            sp.dma_start(t_src[:, :], src).then_inc(s_tab_in, 16)
            sp.dma_start(t_dst[:, :], dst).then_inc(s_tab_in, 16)
            sp.dma_start(wp[:, :], wpack).then_inc(s_w, 16)
            sp.wait_ge(s_fill, 2)
            sp.dma_start(t_next[0:P - 1, :], dst[1:P, :]).then_inc(s_tab_in, 16)
            sp.dma_start(t_next[P - 1:P, 0:T - 1], dst[0:1, 1:T]).then_inc(s_tab_in, 16)
            sp.dma_start(t_prev[P - 1:P, 1:T], dst[P - 1:P, 0:T - 1]).then_inc(s_tab_in, 16)
            for u in range(2):
                sp.dma_start(x_in[u], x_u[u]).then_inc(d_in[u], 16)
            sp.dma_start(edges.rearrange("p t f -> p (t f)"), edges_in.rearrange("p t f -> p (t f)")).then_inc(s_rows, 16)
            sp.dma_start(scalars_t.rearrange("q f p -> (q f) p"), scalars_t_in.rearrange("q f p -> (q f) p")).then_inc(s_rows, 16)
            sp.wait_ge(s_flag, 1)
            with sp.If(sp.value_load(unsorted[0:1, 0:1], min_val=0, max_val=1) > 0):
                sp.wait_ge(s_rows, 32)
                with sp.Fori(0, Q) as a:
                    sp.wait_ge(k_go, a + 1)
                    sp.dma_start(k_dst[:, :], dst.rearrange("p (q c) -> q p c", c=GQ)[a]).then_inc(k_own, 16)
                    sp.dma_start(k_src[:, :], src.rearrange("p (q c) -> q p c", c=GQ)[a]).then_inc(k_own, 16)
                    sp.dma_start(k_num[:, :], number.rearrange("p (q c) -> q p c", c=GQ)[a]).then_inc(k_own, 16)
                    sp.dma_start(k_ed[:, :, :], edges_in.rearrange("p (q c) f -> q p c f", c=GQ)[a]).then_inc(k_own, 16)
                    sp.dma_start(k_sc[:, :, :], scalars_in.rearrange("p (q c) f -> q p c f", c=GQ)[a]).then_inc(k_own, 16)
                    with sp.Fori(0, Q) as b:
                        sp.wait_ge(k_step, a * (Q * 6) + b * 6 + 1)
                        sp.dma_start(k_row[:, :], dst_c[b].partition_broadcast(P)).then_inc(k_chunk, 16)
                        sp.dma_start(k_rnum[:, :], number_c[b].partition_broadcast(P)).then_inc(k_chunk, 16)
                sp.wait_ge(k_go, Q + 1)
                sp.dma_start(t_src[:, :], src_sorted).then_inc(k_tab, 16)
                sp.dma_start(t_dst[:, :], dst_sorted).then_inc(k_tab, 16)
                sp.dma_start(t_next[0:P - 1, :], dst_sorted[1:P, :]).then_inc(k_tab, 16)
                sp.dma_start(t_next[P - 1:P, 0:T - 1], dst_sorted[0:1, 1:T]).then_inc(k_tab, 16)
                sp.dma_start(t_prev[P - 1:P, 1:T], dst_sorted[P - 1:P, 0:T - 1]).then_inc(k_tab, 16)
                with sp.Fori(0, Q) as a:
                    for t in range(GQ):
                        sp.dma_start(scalars_t.rearrange("q (c f) p -> q c f p", c=GQ)[a, t],
                                     scalars_sorted.rearrange("p (q c) f -> q c f p", c=GQ)[a, t],
                                     allow_slow_non_contiguous=True).then_inc(k_sct2, 16)
                sp.wait_ge(k_sct2, 16 * T)
            sp.wait_ge(s_tabc, 6)
            sp.dma_start(src_tab.rearrange("q p c -> p q c"), t_src[:, :].rearrange("p (q c) -> p q c", c=GQ)).then_inc(s_tab_out, 16)
            sp.dma_start(dst_tab.rearrange("q p c -> p q c"), t_gat[:, :].rearrange("p (q c) -> p q c", c=GQ)).then_inc(s_tab_out, 16)
            sp.dma_start(put_tab.rearrange("q p c -> p q c"), t_put[:, :].rearrange("p (q c) -> p q c", c=GQ)).then_inc(s_tab_out, 16)
            sp.dma_start(key_tab.rearrange("q p c -> p q c"), f_key[:, :, :]).then_inc(s_tab_out, 16)
            sp.wait_ge(s_rowsb, 1)
            sp.dma_start(row_tab[0:TA, :], t_row[0][0:TA, :]).then_inc(s_tab_out, 16)
            n_out = 5
            if T > P:
                sp.wait_ge(s_rowsb, 2)
                sp.dma_start(row_tab[P:T, :], t_row[1][0:T - P, :]).then_inc(s_tab_out, 16)
                n_out = 6

            sp.wait_ge(s_rows, 32)
            sp.wait_ge(s_tab_out, 16 * n_out)

            def x_load(u, last=False):
                wait(sp, d_x1, u.times(4, -12))
                sp.dma_start(x_in[u.mod(4)], x_l if last else x_u[u.times(1)]).then_inc(d_in[u.mod(4)], 16)

            def dense_store(u, last=False):
                j = u.mod(2)
                if last:
                    sp.wait_ge(d_sth[1 - j], 16 * (U // 2))
                    sp.wait_ge(d_sto[1 - j], 16 * (U // 2))
                sp.wait_ge(d_h1, u.times(2, 2))
                sp.dma_start(h_l if last else h_u[u.times(1)], h1[j][:, :]).then_inc(d_sth[j], 16)
                sp.wait_ge(d_y, u.times(2, 2))
                sp.dma_start(o_l if last else o_u[u.times(1)], yo[j][:, :]).then_inc(d_sto[j], 16)

            def p1_load(q):
                j = q.mod(2)
                wait(sp, e_g[j], q.over(2, 64))
                sp.dma_start(i_src[j][:, :], src_tab[q.times(1)]).then_inc(e_ix[j], 16)
                wait(sp, n_mm, q.times(1, -1))
                sp.dma_start(q_sct[j][:, :], scalars_t[q.times(1)]).then_inc(n_in[j], 16)

            def p1_tables(q):
                j = q.mod(2)
                wait(sp, e_v, q.times(GQ, -GQ))
                sp.dma_start(q_key[j][:, :], key_tab[q.times(1)]).then_inc(e_tb[j], 16)
                sp.dma_start(q_ed[j][:, :], ed_q[q.times(1)]).then_inc(e_tb[j], 16)
                sp.dma_start(q_row[j][:, :], row_q[q.times(1)].partition_broadcast(P)).then_inc(e_tb[j], 16)

            def p1_store(q):
                sp.wait_ge(e_tot, q.times(GQ, GQ))
                sp.dma_start(sum_tab[q.times(1)], tot[q.mod(2)][:, :]).then_inc(e_st[q.mod(2)], 16)

            def p2_index(q):
                wait(sp, r_g[q.mod(4)], q.over(4, 64))
                sp.dma_start(i_dst[q.mod(4)][:, :], dst_tab[q.times(1)]).then_inc(r_ix[q.mod(4)], 16)

            def step(v, last=False, laststore=False):
                q = At(v.i, v.c // 2, 2)
                if (v - 2).within(U - 2):
                    x_load(v, last)
                if v.mod(2) == 0 and (q + 1).within(Q):
                    p1_load(q + 1)
                if v.mod(2) == 1 and q.within(Q):
                    p1_tables(q)
                if (v - 4).within(U):
                    dense_store(v - 4, laststore)
                if v.mod(2) == 1 and (q - 2).within(Q):
                    p1_store(q - 2)

            p1_load(At(0, 0, 2))
            for v in range(4):
                if v == 2:
                    sp.wait_ge(e_ix[0], 16)
                step(At(0, v))
            with sp.Fori(1, U // 4) as i:
                for c in range(4):
                    step(At(i, c))
            for v in range(U - 2, U + 3):
                step(At(0, v), last=v == U - 1)
            for q in range(4):
                p2_index(At(0, q))
            step(At(0, U + 3), laststore=True)
            for j in range(2):
                sp.wait_ge(e_st[j], 16 * ((Q + 1 - j) // 2))

            def p2_sums(q):
                wait(sp, r_x1, q.times(2, -6))
                sp.dma_start(cv[q.mod(4)], sum_tab[q.times(1)]).then_inc(r_cv[q.mod(4)], 16)

            def p2_put(q):
                j = q.mod(2)
                wait(sp, r_put[j], q.over(2, 64))
                sp.dma_start(i_put[j][:, :], put_tab[q.times(1)]).then_inc(r_px[j], 16)

            def p2_store(q):
                sp.wait_ge(r_y, q.times(1, 1))
                sp.dma_start(y_tab[q.times(1)], yo[q.mod(2)][:, 0:GQ * D]).then_inc(r_sty[q.mod(2)], 16)

            def p2_step(v):
                if (v - 4).within(Q - 4):
                    p2_index(v)
                if (v - 1).within(Q):
                    p2_sums(v - 1)
                if (v - 5).within(Q):
                    p2_put(v - 5)
                if (v - 6).within(Q):
                    p2_store(v - 6)

            for v in range(8):
                p2_step(At(0, v))
            with sp.Fori(2, Q // 4) as i:
                for c in range(4):
                    p2_step(At(i, c))
            for v in range(Q - 1, Q + 6):
                p2_step(At(0, v))
            def p3_load(q):
                j = q.mod(2)
                wait(sp, m_g[j], q.over(2, 64))
                sp.dma_start(i_src[j][:, :], src_tab[q.times(1)]).then_inc(m_ix[j], 16)

            def p3_tables(q):
                j = q.mod(2)
                wait(sp, m_v, q.times(GQ, -GQ))
                sp.dma_start(q_key[j][:, :], key_tab[q.times(1)]).then_inc(m_tb[j], 16)
                sp.dma_start(q_ed[j][:, :], ed_q[q.times(1)]).then_inc(m_tb[j], 16)
                sp.dma_start(q_row[j][:, :], row_q[q.times(1)].partition_broadcast(P)).then_inc(m_tb[j], 16)

            def p3_y(q):
                j = q.mod(2)
                wait(sp, m_o, q.times(GQ, -GQ))
                sp.dma_start(x1[j][:, 0:GQ * D], y_tab[q.times(1)]).then_inc(m_y[j], 16)
                wait(sp, m_put[j], q.over(2, 64))
                sp.dma_start(i_put[j][:, :], put_tab[q.times(1)]).then_inc(m_px[j], 16)

            p3_load(At(0, 0, 2))
            p3_load(At(0, 1, 2))
            p3_tables(At(0, 0, 2))
            for j in range(2):
                sp.wait_ge(r_sty[j], 16 * ((Q + 1 - j) // 2))
                sp.wait_ge(r_put[j], 64 * ((Q + 1 - j) // 2))
            p3_y(At(0, 0, 2))
            p3_load(At(0, 2, 2))
            p3_tables(At(0, 1, 2))
            p3_y(At(0, 1, 2))
            with sp.Fori(1, (Q - 1) // 2) as i:
                for c in range(2):
                    p3_load(At(i, c, 2) + 1)
                    p3_tables(At(i, c, 2))
                    p3_y(At(i, c, 2))
            p3_tables(At(0, Q - 1, 2))
            p3_y(At(0, Q - 1, 2))
            for j in range(2):
                sp.wait_ge(m_put[j], 64 * ((Q + 1 - j) // 2))

        @block.gpsimd
        def _(pool):
            nc.gpsimd.memset(t_next[:, :], N + 5).then_inc(s_fill, 1)
            nc.gpsimd.memset(t_prev[:, :], -1).then_inc(s_fill, 1)
            nc.gpsimd.memset(minus_half[:, :], -0.5)
            nc.gpsimd.memset(ones[:, :], 1.0).then_inc(s_ones, 1)
            pool.wait_ge(s_ones, 1)
            nc.gpsimd.memset(ident[:, :], 0.0).then_inc(s_id, 1)
            pool.wait_ge(s_id, 1)
            nc.gpsimd.affine_select(out=ident[:, :], in_=ident[:, :], compare_op=ALU.not_equal, fill=1.0, base=0,
                                    pattern=[[-1, P]], channel_multiplier=1).then_inc(s_id, 1)

            def gather(rows, into, width, index, signal):
                pool.sem_inc(s_turn, 1)
                for t in range(GQ):
                    nc.gpsimd.indirect_dma_start(
                        into[:, t * width:(t + 1) * width], None, rows,
                        bass.IndirectOffsetOnAxis(ap=index[:, t:t + 1], axis=0)).then_inc(signal, 16)

            def scatter_tile(rows, tile, index, t, signal):
                pool.sem_inc(s_turn, 1)
                nc.gpsimd.indirect_dma_start(
                    rows, bass.IndirectOffsetOnAxis(ap=index[:, t:t + 1], axis=0), tile, None,
                    bounds_check=N - 1, oob_is_err=False).then_inc(signal, 16)

            pool.wait_ge(s_flag, 1)
            with pool.If(pool.value_load(unsorted[0:1, 0:1], min_val=0, max_val=1) > 0):
                pool.sem_inc(k_go, 1)
                with pool.Fori(0, Q) as a:
                    pool.wait_ge(k_ps, a * 7 + 7)
                    pool.sem_inc(s_turn, 1)
                    for t in range(GQ):
                        for rows, tile in ((src_sorted.rearrange("p (t o) -> (p t) o", o=1), k_src[:, t:t + 1]),
                                           (dst_sorted.rearrange("p (t o) -> (p t) o", o=1), k_dst[:, t:t + 1]),
                                           (edges.rearrange("p t f -> (p t) f"), k_ed[:, t, :]),
                                           (scalars_sorted.rearrange("p t f -> (p t) f"), k_sc[:, t, :])):
                            nc.gpsimd.indirect_dma_start(
                                rows, bass.IndirectOffsetOnAxis(ap=k_put[:, t:t + 1], axis=0), tile, None) \
                                .then_inc(k_sct, 16)
                    pool.wait_ge(k_sct, a * 256 + 256)
                    pool.sem_inc(k_go, 1)
                pool.wait_ge(k_tab, 80)

            def p1_gather(q):
                j = q.mod(2)
                pool.wait_ge(e_ix[j], q.over(2, 16, 16))
                wait(pool, e_relu, q.times(1, -1))
                wait(pool, e_scl, q.times(2, -2))
                gather(xa, x_e[j], XW, i_src[j], e_g[j])

            def dense_y(u):
                j = u.mod(2)
                for h in range(2):
                    pool.wait_ge(d_h1, u.times(2, h + 1))
                    if h == 0:
                        wait(pool, d_sto[j], u.over(2, 16))
                    a, b = h * GQ * D, (h + 1) * GQ * D
                    nc.gpsimd.tensor_tensor(yo[j][:, a:b], x1[j][:, a:b], h1[j][:, a:b], ALU.add).then_inc(d_y, 1)

            def inverse_root(inv, var, n, signal):
                nc.gpsimd.tensor_tensor(inv[:, 0:n], var[:, 0:n], minus_half[:, 0:n], ALU.pow).then_inc(signal, 1)

            def dense_scale(u):
                j = u.mod(4)
                pool.wait_ge(d_ln1, u.times(5, 4))
                inverse_root(inv1[j], var1[j], GD, d_scl)
                pool.wait_ge(d_scl, u.times(2, 1))
                nc.gpsimd.tensor_tensor(scl1[j][:, :], inv1[j][:, :], x3(x_in[j], XW, GD)[:, :, D], ALU.mult).then_inc(d_scl, 1)

            def dense_norm2(u):
                j = u.mod(2)
                pool.wait_ge(d_ln2, u.times(4, 4))
                inverse_root(inv2[j], var2[j], GD, d_nmr)
                pool.wait_ge(d_nmr, u.times(2, 1))
                nc.gpsimd.tensor_tensor(nmr2[j][:, :], neg2[j][:, :], inv2[j][:, :], ALU.mult).then_inc(d_nmr, 1)

            def p1_scale(q):
                j = q.mod(2)
                pool.wait_ge(e_ln, q.times(5, 4))
                inverse_root(inv_e[j], var_e[j], GQ, e_scl)
                pool.wait_ge(e_scl, q.times(2, 1))
                nc.gpsimd.tensor_tensor(scl_e[j][:, :], inv_e[j][:, :], x3(x_e[j], XW, GQ)[:, :, D], ALU.mult).then_inc(e_scl, 1)

            def step(w):
                q = At(w.i, w.c // 2, 2)
                if w.mod(2) == 1 and (q + 1).within(Q):
                    p1_gather(q + 1)
                if (w - 1).within(U):
                    dense_scale(w - 1)
                if (w - 4).within(U):
                    dense_y(w - 4)
                if (w - 3).within(U):
                    dense_norm2(w - 3)
                if w.mod(2) == 0 and q.within(Q):
                    p1_scale(q)

            pool.wait_ge(s_tab_in, 80)
            gather(xa, x_e[0], XW, t_src, e_g[0])
            for w in range(8):
                step(At(0, w))
            with pool.Fori(2, U // 4) as i:
                for c in range(4):
                    step(At(i, c))
            for w in range(U - 2, U + 4):
                step(At(0, w))

            def p2_gather(q):
                k = q.mod(4)
                pool.wait_ge(r_ix[k], q.over(4, 16, 16))
                wait(pool, r_x1, q.times(2, -6))
                gather(xa, x_q[k], XW, i_dst[k], r_g[k])

            def p2_scatter(q):
                j = q.mod(2)
                pool.wait_ge(r_px[j], q.over(2, 16, 16))
                pool.wait_ge(r_h1, q.times(1, 1))
                for t in range(GQ):
                    scatter_tile(h1_all, h1[j][:, t * D:(t + 1) * D], i_put[j], t, r_put[j])

            def p2_step(w):
                if w.within(Q):
                    p2_gather(w)
                if (w - 4).within(Q):
                    p2_scatter(w - 4)

            pool.wait_ge(d_x1, 4 * U)
            for w in range(4):
                p2_step(At(0, w))
            for j in range(2):
                pool.wait_ge(d_sth[j], 16 * (U // 2))
                pool.wait_ge(d_sto[j], 16 * (U // 2))
            with pool.Fori(1, Q // 4) as i:
                for c in range(4):
                    p2_step(At(i, c))
            for w in range(Q - 1, Q + 4):
                p2_step(At(0, w))
            for j in range(2):
                pool.wait_ge(r_put[j], 64 * ((Q + 1 - j) // 2))
            pool.wait_ge(r_y, Q)

            def p3_gather(n):
                j, t = n.c // GQ % 2, n.mod(4)
                if t == 0:
                    pool.wait_ge(m_ix[j], n.over(8, 16, 16))
                wait(pool, m_ft, n.times(1, -7))
                wait(pool, m_ss, n.times(1, -7))
                pool.sem_inc(s_turn, 1)
                nc.gpsimd.indirect_dma_start(
                    h1[j][:, t * D:(t + 1) * D], None, h1_all,
                    bass.IndirectOffsetOnAxis(ap=i_src[j][:, t:t + 1], axis=0)).then_inc(m_g[j], 16)

            def p3_scatter(n):
                j, t = n.c // GQ % 2, n.mod(4)
                if t == 0:
                    pool.wait_ge(m_px[j], n.over(8, 16, 16))
                pool.wait_ge(m_o, n.times(1, 1))
                scatter_tile(out, yo[j][:, t * D:(t + 1) * D], i_put[j], t, m_put[j])

            for n in range(7):
                p3_gather(At(0, n, 8))
            for n in range(8):
                if n >= 4:
                    p3_scatter(At(0, n - 4, 8))
                p3_gather(At(0, n + 7, 8))
            with pool.Fori(1, (Q - 3) // 2) as i:
                for c in range(8):
                    p3_scatter(At(i, c, 8) - 4)
                    p3_gather(At(i, c, 8) + 7)
            for n in range(T - 3 * GQ, T + 4):
                p3_scatter(At(0, n - 4, 8))
                if n + 7 < T:
                    p3_gather(At(0, n + 7, 8))

        @block.scalar
        def _(act):
            def dense_h1(u, h):
                j = u.mod(2)
                act.wait_ge(d_nmr, u.times(2, 2))
                wait(act, d_y, u.times(2, h - 3))
                wait(act, d_sth[j], u.over(2, 16))
                for k in range(h * GQ, (h + 1) * GQ):
                    ins = nc.scalar.activation(h1[j][:, k * D:(k + 1) * D], x1[j][:, k * D:(k + 1) * D], ACT.Relu,
                                               bias=nmr2[j][:, k:k + 1], scale=inv2[j][:, k:k + 1])
                ins.then_inc(d_h1, 1)

            def dense_relu(u, h):
                act.wait_ge(d_ln1, u.times(5, 3))
                x, hh = x_in[u.mod(4)], hb[u.mod(2)]
                for k in range(h * GQ, (h + 1) * GQ):
                    ins = nc.scalar.activation(hh[:, k * P:(k + 1) * P], x[:, k * XW + 32:k * XW + D], ACT.Relu,
                                               bias=neg1[u.mod(4)][:, k:k + 1])
                ins.then_inc(d_relu, 1)

            def dense_copy(u, h):
                act.wait_ge(d_tr, u.times(2, h + 1))
                wait(act, d_mm, u.times(4, 2 * h - 2))
                nc.scalar.activation(hT[h][:, :], bank[0][:, :], ACT.Copy)
                nc.scalar.activation(hR[h][:, :], bank[1][:, 0:P], ACT.Relu).then_inc(d_hT, 1)

            def net_silu(q):
                act.wait_ge(n_mm, q.times(1, 1))
                nc.scalar.activation(q_hid[q.mod(2)][:, :], bank[4][:, 0:2 * P], ACT.Silu,
                                     scale=8.0 ** -0.5).then_inc(n_act, 1)

            def p1_relu(q):
                j = q.mod(2)
                act.wait_ge(e_ln, q.times(5, 3))
                for t in range(GQ):
                    ins = nc.scalar.activation(h_e[:, t * P:(t + 1) * P], x_e[j][:, t * XW + 32:t * XW + D], ACT.Relu,
                                               bias=neg_e[j][:, t:t + 1])
                ins.then_inc(e_relu, 1)

            def p1_copy(q):
                act.wait_ge(e_tr, q.times(1, 1))
                wait(act, e_pw, q.times(GQ, -GQ))
                nc.scalar.activation(eT[q.mod(2)][:, :], bank[4][:, :], ACT.Copy)
                nc.scalar.activation(eR[q.mod(2)][:, :], bank[1][:, P:2 * P], ACT.Relu).then_inc(e_hT, 1)

            def p1_rest(n):
                act.wait_ge(e_u, n.times(1, 1))
                wait(act, e_v, n.times(1, -1))
                nc.scalar.activation(xr[n.mod(2)][:, 0:65], bank[7][:, U_B:U_B + 65], ACT.Copy).then_inc(e_xb, 1)

            def p1_source(n):
                act.wait_ge(e_pw, n.times(1, 1))
                j, t = n.c // GQ % 2, n.mod(4)
                act.wait_ge(e_scl, n.over(4, 2, 2))
                wait(act, e_ft, n.times(1, -1))
                nc.scalar.activation(g_e[n.mod(2)][:, :], bank[5 + n.mod(2)][:, 0:D], ACT.Copy,
                                     scale=scl_e[j][:, t:t + 1]).then_inc(e_gg, 1)

            def p1_total(n):
                act.wait_ge(e_seg, n.times(1, 1))
                j, t = n.c // GQ % 2, n.mod(4)
                if t == 0:
                    wait(act, e_st[j], n.over(8, 16))
                nc.scalar.activation(tot[j][:, t * CW:(t + 1) * CW], bank[1][:, U_SEG:U_SEG + CW],
                                     ACT.Copy).then_inc(e_tot, 1)

            def p1_feat_t(n):
                act.wait_ge(e_ftr, n.times(1, 1))
                wait(act, e_u, n.times(1, -1))
                nc.scalar.activation(fT[n.mod(2)][:, 0:384], bank[4][:, 0:384], ACT.Copy).then_inc(e_fte, 1)

            def slot(u, h):
                s = At(u.i, 2 * u.c + h, 8)
                if (s - 1).within(T):
                    p1_feat_t(s - 1)
                if (s - 2).within(T):
                    p1_rest(s - 2)
                if s.within(T):
                    p1_source(s)
                if (s - 3).within(T):
                    p1_total(s - 3)

            def step(u):
                q = At(u.i, u.c // 2, 2)
                odd = u.mod(2) == 1
                if u.within(U):
                    dense_relu(u, 0)
                slot(u, 0)
                if not odd and (q + 1).within(Q):
                    net_silu(q + 1)
                if odd and (q + 1).within(Q):
                    p1_relu(q + 1)
                if u.within(U):
                    dense_copy(u, 0)
                if (u - 2).within(U):
                    dense_h1(u - 2, 0)
                if odd and (q + 1).within(Q):
                    p1_copy(q + 1)
                if u.within(U):
                    dense_relu(u, 1)
                slot(u, 1)
                if u.within(U):
                    dense_copy(u, 1)
                if (u - 2).within(U):
                    dense_h1(u - 2, 1)

            net_silu(At(0, 0, 2))
            p1_relu(At(0, 0, 2))
            p1_copy(At(0, 0, 2))
            for u in range(4):
                step(At(0, u))
            with act.Fori(1, U // 4) as i:
                for c in range(4):
                    step(At(i, c))
            for u in range(U - 2, U + 2):
                step(At(0, u))

            def p2_h1(q):
                j = q.mod(2)
                act.wait_ge(r_nmr, q.times(2, 2))
                wait(act, r_y, q.times(1, -1))
                wait(act, r_put[j], q.over(2, 64))
                for t in range(GQ):
                    ins = nc.scalar.activation(h1[j][:, t * D:(t + 1) * D], x1[j][:, t * D:(t + 1) * D], ACT.Relu,
                                               bias=nmr2[j][:, t:t + 1], scale=inv2[j][:, t:t + 1])
                ins.then_inc(r_h1, 1)

            def p2_relu(q):
                act.wait_ge(r_ln1, q.times(5, 3))
                for t in range(GQ):
                    ins = nc.scalar.activation(h_e[:, t * P:(t + 1) * P], x_q[q.mod(4)][:, t * XW + 32:t * XW + D],
                                               ACT.Relu, bias=neg_e[q.mod(2)][:, t:t + 1])
                ins.then_inc(r_relu, 1)

            def p2_copy(q):
                act.wait_ge(r_tr, q.times(1, 1))
                wait(act, r_mm, q.times(1))
                nc.scalar.activation(eT[0][:, :], bank[0][:, :], ACT.Copy)
                nc.scalar.activation(eR[0][:, :], bank[1][:, 0:P], ACT.Relu).then_inc(r_hT, 1)

            def p2_sines(q):
                j = q.mod(2)
                act.wait_ge(r_ang, q.times(8, 8))
                nc.scalar.activation(trig[4][j][:, :], trig[3][j][:, :], ACT.Sin).then_inc(r_sin, 1)

            def p2_root1(q):
                j = q.mod(2)
                act.wait_ge(r_ln1, q.times(5, 4))
                nc.scalar.activation(sd_e[j][:, :], var_e[j][:, :], ACT.Sqrt).then_inc(r_sq1, 1)

            def p2_root2(q):
                j = q.mod(2)
                act.wait_ge(r_ln2, q.times(4, 4))
                nc.scalar.activation(sd2[j][:, :], var2[j][:, 0:GQ], ACT.Sqrt).then_inc(r_sq2, 1)

            def p2_step(q):
                if (q - 2).within(Q):
                    p2_root2(q - 2)
                if q.within(Q):
                    p2_relu(q)
                    p2_root1(q)
                    p2_copy(q)
                if (q - 2).within(Q):
                    p2_h1(q - 2)
                if q.within(Q):
                    p2_sines(q)

            for q in range(4):
                p2_step(At(0, q))
            with act.Fori(1, Q // 4) as i:
                for c in range(4):
                    p2_step(At(i, c))
            for q in range(Q - 1, Q + 2):
                p2_step(At(0, q))

            def p3_scalars(n):
                j, t = n.c // GQ % 2, n.mod(4)
                if t == 0:
                    act.wait_ge(m_g[j], n.over(8, 64, 64))
                wait(act, m_ftr, n.times(1, -1))
                nc.scalar.activation(feat[n.mod(2)][:, 448:512], h1[j][:, t * D:t * D + DS], ACT.Copy).then_inc(m_ss, 1)

            def p3_total(n):
                j, t = n.c // GQ % 2, n.mod(4)
                act.wait_ge(m_seg, n.times(1, 1))
                nc.scalar.activation(tot[j][:, t * CW:t * CW + D], bank[4 + n.mod(2)][:, 0:D], ACT.Copy).then_inc(m_tot, 1)

            def p3_feat_t(n):
                act.wait_ge(m_ftr, n.times(1, 1))
                wait(act, m_u, n.times(1, -1))
                nc.scalar.activation(fT[n.mod(2)][:, :], bank[n.mod(2)][:, :], ACT.Copy).then_inc(m_fte, 1)

            def p3_slot(n):
                if n.within(T):
                    p3_scalars(n)
                if (n - 4).within(T):
                    p3_total(n - 4)
                if (n - 1).within(T):
                    p3_feat_t(n - 1)

            act.wait_ge(m_z, 1)
            for n in range(8):
                p3_slot(At(0, n, 8))
            with act.Fori(1, (Q - 1) // 2) as i:
                for c in range(8):
                    p3_slot(At(i, c, 8))
            for n in range(T - GQ, T + 4):
                p3_slot(At(0, n, 8))

        @block.tensor
        def _(pe):
            def transpose_rows(main, rest, ps_main, ps_rest, tr_sem):
                for t in range(GQ):
                    nc.tensor.transpose(ps_main[:, t * P:(t + 1) * P], main[:, t * P:(t + 1) * P], ident[:, :])
                nc.tensor.transpose(ps_rest, rest, ident[:, :]).then_inc(tr_sem, 1)

            def linear(dst_ps, main, rest, w, t):
                nc.tensor.matmul(dst_ps, main[:, t * P:(t + 1) * P], wp[:, w:w + D], start=True, stop=False)
                return nc.tensor.matmul(dst_ps[:, 0:DS], rest[:, :], wp[:, w + D + t * DS:w + D + (t + 1) * DS],
                                        start=False, stop=True)

            pe.wait_ge(s_ones, 1)
            pe.wait_ge(s_fall, 2)
            nc.tensor.matmul(bank[7][:, 0:1], ones[:, :], fall[:, :], start=True, stop=True).then_inc(s_fallp, 1)

            pe.wait_ge(s_id, 2)
            pe.wait_ge(s_tabc, 1)
            nc.tensor.transpose(bank[6][0:TA, 0:P], f_dst[:, 0:TA], ident[:, :]).then_inc(s_rowps, 1)
            if T > P:
                nc.tensor.transpose(bank[7][0:T - P, 0:P], f_dst[:, P:T], ident[:, :]).then_inc(s_rowps, 1)

            pe.wait_ge(s_w, 16)
            pieces = [(b, W_W1T, 64, b, W_WS, 64) for b in (0, 1)] \
                + [(2 + b, W_W4T, 96, b, W_WVK, 96) for b in range(3)] \
                + [(5 + b, W_W2T, 64, b, W_WS, 64) for b in range(3)] \
                + [(8 + b, W_W5T, 96, b, W_WVA, 96) for b in range(3)] \
                + [(11 + b, W_W5T, 96, b, W_WVB, 96) for b in range(3)] \
                + [(14 + b, W_W3T, 32, b, W_WV, 32) for b in (0, 1)]
            for r, wl, kk, b, wr, cols in pieces:
                where = 32 * (r % 4)
                nc.tensor.matmul(bank[r // 4][where:where + 32, 0:cols],
                                 wp[0:kk, wl + 32 * b:wl + 32 * (b + 1)], wp[0:kk, wr:wr + cols],
                                 start=True, stop=True).then_inc(s_mp, 1)
            pe.wait_ge(s_mc, 1)
            pe.wait_ge(s_wscaled, 1)

            def dense_mm(u, h):
                pe.wait_ge(d_hT, u.times(2, h + 1))
                for k in range(GQ):
                    if k % 2 == 0:
                        wait(pe, d_x1, u.times(4, 2 * h + k // 2 - 1))
                    ins = linear(bank[2 + k // 2][:, k % 2 * D:(k % 2 + 1) * D], hT[h], hR[h], W_SC, k)
                    if k % 2 == 1:
                        ins.then_inc(d_mm, 1)

            def dense_tr(u, h):
                pe.wait_ge(d_relu, u.times(2, h + 1))
                pe.wait_ge(d_ln1, u.times(5, 5))
                wait(pe, d_hT, u.times(2, h))
                wait(pe, e_tot, u.times(2, h - 2))
                q = At(u.i, u.c // 2, 2) + u.c % 2 * h
                pe.wait_ge(e_hT, q.times(1, 1) if q.within(Q) else Q)
                transpose_rows(hb[u.mod(2)][:, h * 4 * P:(h + 1) * 4 * P], hr[u.mod(2)][:, h * P:(h + 1) * P], bank[0],
                               bank[1][:, 0:P], d_tr)

            def net_mm(q):
                pe.wait_ge(n_in[q.mod(2)], q.over(2, 16, 16))
                wait(pe, e_fte, q.times(GQ, -GQ))
                for h in range(2):
                    ins = nc.tensor.matmul(bank[4][:, h * P:(h + 1) * P],
                                           wp[0:32, W_FC1 + h * P:W_FC1 + (h + 1) * P], q_sct[q.mod(2)][:, :],
                                           start=True, stop=True)
                ins.then_inc(n_mm, 1)

            def p1_tr(q):
                pe.wait_ge(e_relu, q.times(1, 1))
                pe.wait_ge(e_ln, q.times(5, 5))
                wait(pe, e_fte, q.times(GQ, -2))
                pe.wait_ge(n_act, q.times(1, 1))
                wait(pe, d_hT, q.times(4, -1))
                wait(pe, e_tot, q.times(4, -4))
                transpose_rows(h_e[:, :], hr_e[q.mod(2)][:, :], bank[4], bank[1][:, P:2 * P], e_tr)

            def p1_parts(n):
                pe.wait_ge(e_fte, n.times(1, 1))
                wait(pe, e_v, n.times(1))
                f = fT[n.mod(2)]
                nc.tensor.matmul(bank[7][:, U_C:U_C + 97], f[:, 0:P], wp[:, W_R1:W_R1 + 97], start=True, stop=True)
                nc.tensor.matmul(bank[7][:, U_D:U_D + 161], f[:, P:2 * P], wp[:, W_R2:W_R2 + 161],
                                 start=True, stop=False)
                nc.tensor.matmul(bank[7][:, U_B:U_B + 65], f[:, 2 * P:3 * P], wp[:, W_R3:W_R3 + 65],
                                 start=False, stop=True).then_inc(e_u, 1)

            def p1_source(n):
                j, t = n.c // GQ % 2, n.mod(4)
                if t == 0:
                    pe.wait_ge(e_hT, n.over(4, 1, 1))
                    pe.wait_ge(n_act, n.over(4, 1, 1))
                wait(pe, e_ft, n.times(1, -1))
                b = bank[5 + n.mod(2)]
                linear(b[:, 0:D], eT[j], eR[j], W_L1, t)
                nc.tensor.matmul(b[:, D:D + 192], q_hid[j][:, t // 2 * P:(t // 2 + 1) * P],
                                 wp[:, W_FC2 + t % 2 * 192:W_FC2 + (t % 2 + 1) * 192],
                                 start=True, stop=True).then_inc(e_pw, 1)

            def p1_sum(n, dense_copied):
                j, t = n.c // GQ % 2, n.mod(4)
                if t == 0:
                    pe.wait_ge(e_sc, n.over(4, 1, 1))
                pe.wait_ge(e_v, n.times(1, 1))
                wait(pe, e_tot, n.times(1))
                wait(pe, d_hT, dense_copied)
                before = tot[j][:, (t - 1) * CW:t * CW] if t else tot[1 - j][:, (GQ - 1) * CW:GQ * CW]
                nc.tensor.matmul(bank[1][:, U_SEG:U_SEG + CW], same[j][:, t * P:(t + 1) * P], v_e[n.mod(2)][:, :],
                                 start=True, stop=False)
                nc.tensor.matmul(bank[1][:, U_SEG:U_SEG + CW], carry[j][:, t * P:(t + 1) * P], before,
                                 start=False, stop=True).then_inc(e_seg, 1)

            def p1_feat_t(n, q1):
                pe.wait_ge(e_ft, n.times(1, 1))
                wait(pe, e_fte, n.times(1))
                if n.mod(4) == 2 and (n + 2).within(T):
                    pe.wait_ge(e_hT, (n + 2).over(4, 1, 1))
                if q1 is not None:
                    pe.wait_ge(n_act, q1.times(1, 1))
                f = feat[n.mod(2)]
                for c, at in enumerate((0, 128, 192)):
                    ins = nc.tensor.transpose(bank[4][:, c * P:(c + 1) * P], f[:, at:at + P], ident[:, :])
                ins.then_inc(e_ftr, 1)

            def slot(u, h):
                s = At(u.i, 2 * u.c + h, 8)
                q1 = At(u.i, u.c // 2, 2) + 1
                if (u - 1).within(U):
                    dense_mm(u - 1, h)
                if h == 1 and u.mod(2) == 1 and q1.within(Q):
                    p1_tr(q1)
                if (s - 1).within(T):
                    p1_feat_t(s - 1, q1 if u.mod(2) == 0 and h == 1 and q1.within(Q) else None)
                if (s - 2).within(T):
                    p1_parts(s - 2)
                if s.within(T):
                    p1_source(s)
                if (s - 3).within(T):
                    p1_sum(s - 3, u.times(2, h) if u.within(U) else 2 * U)

            def step(u):
                q = At(u.i, u.c // 2, 2)
                odd = u.mod(2) == 1
                slot(u, 0)
                if not odd and (q + 1).within(Q):
                    net_mm(q + 1)
                if u.within(U):
                    dense_tr(u, 0)
                slot(u, 1)
                if u.within(U):
                    dense_tr(u, 1)

            pe.wait_ge(e_z, 1)
            net_mm(At(0, 0, 2))
            p1_tr(At(0, 0, 2))
            for u in range(4):
                step(At(0, u))
            with pe.Fori(1, U // 4) as i:
                for c in range(4):
                    step(At(i, c))
            for u in range(U - 2, U + 2):
                step(At(0, u))

            def p2_step(q):
                j = q.mod(2)
                pe.wait_ge(r_relu, q.times(1, 1))
                wait(pe, r_hT, q.times(1))
                pe.wait_ge(r_ln1, q.times(5, 5))
                transpose_rows(h_e[:, :], hr_e[j][:, :], bank[0], bank[1][:, 0:P], r_tr)
                pe.wait_ge(r_hT, q.times(1, 1))
                wait(pe, r_x1, q.times(2, -2))
                for t in range(GQ):
                    ins = linear(bank[2 + 2 * j + t // 2][:, t % 2 * D:(t % 2 + 1) * D], eT[0], eR[0], W_SC, t)
                ins.then_inc(r_mm, 1)

            pe.wait_ge(d_x1, 4 * U)
            for q in range(2):
                p2_step(At(0, q, 2))
            with pe.Fori(1, (Q - 1) // 2) as i:
                for c in range(2):
                    p2_step(At(i, c, 2))
            p2_step(At(0, Q - 1, 2))
            pe.wait_ge(r_x1, 2 * Q)
            pe.wait_ge(m_z, 1)

            def p3_tr(n):
                pe.wait_ge(m_ft, n.times(1, 1))
                pe.wait_ge(m_ss, n.times(1, 1))
                wait(pe, m_fte, n.times(1, -1))
                for c in range(4):
                    ins = nc.tensor.transpose(bank[n.mod(2)][:, c * P:(c + 1) * P],
                                              feat[n.mod(2)][:, c * P:(c + 1) * P], ident[:, :])
                ins.then_inc(m_ftr, 1)

            def p3_parts(n):
                pe.wait_ge(m_fte, n.times(1, 1))
                wait(pe, m_v, n.times(1, -1))
                f, b = fT[n.mod(2)], bank[2 + n.mod(2)]
                nc.tensor.matmul(b[:, D:D + DU], f[:, 3 * P:4 * P], msg1s[:, :], start=True, stop=True)
                nc.tensor.matmul(b[:, 0:D], f[:, 0:P], msg1[0][:, :], start=True, stop=False)
                nc.tensor.matmul(b[:, 0:D], f[:, P:2 * P], msg1[1][:, :], start=False, stop=False)
                nc.tensor.matmul(b[:, DS:D], f[:, 2 * P:3 * P], msg1[2][:, :], start=False, stop=False)
                nc.tensor.matmul(b[:, DS:D], f[:, 3 * P:4 * P], msg1[3][:, :], start=False, stop=True).then_inc(m_u, 1)

            def p3_sum(n):
                j, t = n.c // GQ % 2, n.mod(4)
                if t == 0:
                    pe.wait_ge(m_sc, n.over(4, 1, 1))
                pe.wait_ge(m_v, n.times(1, 1))
                wait(pe, m_tot, n.times(1))
                b = bank[4 + n.mod(2)]
                before = tot[j][:, (t - 1) * CW:(t - 1) * CW + D] if t else tot[1 - j][:, (GQ - 1) * CW:(GQ - 1) * CW + D]
                nc.tensor.matmul(b[:, 0:D], same[j][:, t * P:(t + 1) * P], v_e[n.mod(2)][:, 0:D], start=True, stop=False)
                nc.tensor.matmul(b[:, 0:D], carry[j][:, t * P:(t + 1) * P], before, start=False, stop=True).then_inc(m_seg, 1)

            def p3_slot(n):
                if (n - 1).within(T):
                    p3_tr(n - 1)
                if (n - 4).within(T):
                    p3_sum(n - 4)
                if (n - 2).within(T):
                    p3_parts(n - 2)

            for n in range(8):
                p3_slot(At(0, n, 8))
            with pe.Fori(1, (Q - 1) // 2) as i:
                for c in range(8):
                    p3_slot(At(i, c, 8))
            for n in range(T - GQ, T + 4):
                p3_slot(At(0, n, 8))

        @block.vector
        def _(v):
            V = nc.vector

            def moment_part(part, st, su, df, sq, m2, neg, var, n, signal):
                if part == 1:
                    V.tensor_tensor(su[:, 0:n, :], st[:, 0:n, 1:3], st[:, 0:n, 4:6], ALU.add)
                    ins = V.tensor_tensor(df[:, 0:n], st[:, 0:n, 1], st[:, 0:n, 4], ALU.subtract)
                elif part == 2:
                    V.tensor_scalar(neg[:, 0:n], su[:, 0:n, 0], -0.5, None, ALU.mult)
                    V.scalar_tensor_tensor(sq[:, 0:n], df[:, 0:n], 0.25, df[:, 0:n], ALU.mult, ALU.mult)
                    ins = V.tensor_scalar(m2[:, 0:n], su[:, 0:n, 1], 1.0 / D, EPS, ALU.mult, ALU.add)
                else:
                    ins = V.tensor_tensor(var[:, 0:n], m2[:, 0:n], sq[:, 0:n], ALU.add)
                ins.then_inc(signal, 1)

            def rest_of(into, rows, neg, n, signal):
                V.tensor_tensor(x3(into, 32, n), x3(rows, XW, n)[:, :, 0:32], bc_last(neg[:, 0:n], 32), ALU.add) \
                    .then_inc(signal, 1)

            v.wait_ge(s_tab_in, 80)
            V.tensor_tensor(falls[:, :], t_next[:, :], t_dst[:, :], ALU.is_lt).then_inc(s_fall, 1)
            v.wait_ge(s_fall, 1)
            V.tensor_reduce(fall[:, :], falls[:, :], AX.X, ALU.add).then_inc(s_fall, 1)
            v.wait_ge(s_fallp, 1)
            V.tensor_scalar(unsorted[:, :], bank[7][:, 0:1], 1.0, None, ALU.min).then_inc(s_flag, 1)
            v.wait_ge(s_flag, 1)
            with v.If(v.value_load(unsorted[0:1, 0:1], min_val=0, max_val=1) > 0):
                V.memset(k_tile[:, :], 0.0).then_inc(k_step, 1)
                with v.Fori(0, Q) as a:
                    v.wait_ge(k_own, a * 80 + 80)
                    V.memset(k_rank[:, :], 0.0).then_inc(k_z, 1)
                    with v.Fori(0, Q) as b:
                        def counted(ins, n):
                            ins.then_inc(k_step, 1)
                            v.wait_ge(k_step, a * (Q * 6) + b * 6 + (n + 1))

                        v.wait_ge(k_z, a + 1)
                        v.wait_ge(k_chunk, a * (Q * 32) + b * 32 + 32)
                        counted(V.tensor_tensor(k_cmp, bc_mid(k_row[:, :], GQ), bc_last(k_dst[:, :], CH), ALU.subtract), 1)
                        counted(V.tensor_scalar(k_cmp, k_cmp, -1.0, 1.0, ALU.max, ALU.min), 2)
                        counted(V.scalar_tensor_tensor(k_cmp, k_cmp, float(FAR), bc_mid(k_rnum[:, :], GQ),
                                                       ALU.mult, ALU.add), 3)
                        counted(V.tensor_tensor(k_cmp, k_cmp, bc_last(k_num[:, :], CH), ALU.is_lt), 4)
                        counted(V.tensor_reduce(k_less[:, :], k_cmp, AX.X, ALU.add), 5)
                        counted(V.tensor_tensor(k_rank[:, :], k_rank[:, :], k_less[:, :], ALU.add), 6)

                    def placed(ins, n):
                        ins.then_inc(k_ps, 1)
                        v.wait_ge(k_ps, a * 7 + n)

                    placed(V.tensor_scalar(k_tile[:, :], k_rank[:, :], 1.0 / P, -(P - 1) / (2.0 * P), ALU.mult, ALU.add), 1)
                    placed(V.tensor_scalar(k_tile[:, :], k_tile[:, :], 1.5 * 2.0 ** 23, None, ALU.add), 2)
                    placed(V.tensor_scalar(k_tile[:, :], k_tile[:, :], -1.5 * 2.0 ** 23, None, ALU.add), 3)
                    placed(V.scalar_tensor_tensor(k_rank[:, :], k_tile[:, :], -float(P), k_rank[:, :], ALU.mult, ALU.add), 4)
                    placed(V.scalar_tensor_tensor(k_pos[:, :], k_rank[:, :], float(T), k_tile[:, :], ALU.mult, ALU.add), 5)
                    placed(V.tensor_copy(k_put[:, :], k_pos[:, :]), 6)
                    V.memset(k_less[:, :], 0.0).then_inc(k_ps, 1)
                v.wait_ge(k_tab, 80)
            V.tensor_copy(f_dst[:, :], t_dst[:, :]).then_inc(s_tabc, 1)
            V.tensor_copy(f_next[:, :], t_next[:, :])
            V.tensor_copy(f_key[:, :, GQ:2 * GQ], t_prev[:, :].rearrange("p (q c) -> p q c", c=GQ)).then_inc(s_tabc, 1)
            v.wait_ge(s_tabc, 2)
            V.tensor_copy(f_key[:, :, 0:GQ], f_dst[:, :].rearrange("p (q c) -> p q c", c=GQ))
            V.tensor_scalar(t_gat[:, :], f_dst[:, :], float(N - 1), None, ALU.min)
            V.tensor_tensor(f_put[:, :], f_dst[:, :], f_next[:, :], ALU.is_equal).then_inc(s_tabc, 1)
            v.wait_ge(s_tabc, 3)
            V.scalar_tensor_tensor(f_next[:, :], f_put[:, :], float(FAR), f_dst[:, :], ALU.mult, ALU.add) \
                .then_inc(s_tabc, 1)
            v.wait_ge(s_tabc, 4)
            V.tensor_copy(t_put[:, :], f_next[:, :]).then_inc(s_tabc, 2)
            v.wait_ge(s_rowps, 1)
            V.tensor_copy(t_row[0][0:TA, :], bank[6][0:TA, 0:P]).then_inc(s_rowsb, 1)
            if T > P:
                v.wait_ge(s_rowps, 2)
                V.tensor_copy(t_row[1][0:T - P, :], bank[7][0:T - P, 0:P]).then_inc(s_rowsb, 1)

            v.wait_ge(s_w, 16)
            V.memset(msg1[0][:, :], 0.0)
            V.memset(msg1[1][:, :], 0.0)
            V.memset(msg1s[:, :], 0.0).then_inc(s_mz, 1)
            LS, LV, I3, I6 = DS ** -0.5, DU ** -0.5, 3.0 ** -0.5, 6.0 ** -0.5
            C0, C1 = (DS + DU) ** -0.5, (3.0 / (DS + 2 * DU)) ** 0.5
            v.wait_ge(s_mz, 1)
            v.wait_ge(s_mp, 16)

            def piece(r, cols, into, at, factor):
                w = 32 * (r % 4)
                return V.tensor_scalar(into[w:w + 32, at:at + cols], bank[r // 4][w:w + 32, 0:cols], factor, None, ALU.mult)

            for r in range(16):
                if r < 2:
                    ins = piece(r, DS, msg1[0], 0, C0 * LS)
                elif r < 4:
                    ins = piece(r, DV, msg1[0], DS, C1 * I3 * LV)
                elif r < 5:
                    ins = piece(r, DV, msg1[1], DS, C1 * I3 * LV)
                elif r < 8:
                    ins = piece(r, DS, msg1[1], 0, C0 * I3 * LS)
                elif r < 11:
                    ins = piece(r, DV, msg1[2], 0, C1 * I6 * LV)
                elif r < 12:
                    ins = piece(r, DV, msg1[2], 0, -C1 * I6 * LV)
                elif r < 14:
                    ins = piece(r, DV, msg1[3], 0, -C1 * I6 * LV)
                else:
                    ins = piece(r, DU, msg1s, 0, C1 * I3 * LV)
            V.memset(msg1[3][DS:P, :], 0.0).then_inc(s_mc, 1)
            for w in (W_SC, W_L1):
                V.tensor_scalar(wp[:, w:w + DS], wp[:, w:w + DS], LS, None, ALU.mult)
                V.tensor_scalar(wp[:, w + DS:w + D], wp[:, w + DS:w + D], LV, None, ALU.mult)
                V.tensor_scalar(wp[:, w + D:w + D + 4 * DS], wp[:, w + D:w + D + 4 * DS], LS, None, ALU.mult)
            V.tensor_scalar(wp[:, W_FC2:W_FC2 + 384], wp[:, W_FC2:W_FC2 + 384], DS ** -0.5, None, ALU.mult)
            FS = 0.25 * float(DV) ** -0.5
            V.tensor_scalar(wp[:, W_R1:W_R1 + 32], wp[:, W_R1:W_R1 + 32], FS, None, ALU.mult)
            V.tensor_scalar(wp[:, W_R1 + 32:W_R1 + 33], wp[:, W_R1 + 32:W_R1 + 33], 0.1 * FS, None, ALU.mult)
            V.tensor_scalar(wp[:, W_R1 + 33:W_R1 + 97], wp[:, W_R1 + 33:W_R1 + 97], FS, None, ALU.mult)
            V.tensor_scalar(wp[:, W_R2:W_R2 + 96], wp[:, W_R2:W_R2 + 96], FS, None, ALU.mult)
            for w in (W_R2 + 96, W_R3):
                V.tensor_scalar(wp[:, w:w + 1], wp[:, w:w + 1], 0.1 * FS * I3, None, ALU.mult)
                V.tensor_scalar(wp[:, w + 1:w + 65], wp[:, w + 1:w + 65], FS * I3, None, ALU.mult)
            V.memset(tot[1][:, :], 0.0).then_inc(s_wscaled, 1)
            v.wait_ge(s_wscaled, 1)
            V.memset(df1[0][:, :], 0.0).then_inc(e_z, 1)
            v.wait_ge(e_z, 1)

            def dense_stats(u):
                j = u.mod(4)
                v.wait_ge(d_in[j], u.over(4, 16, 16))
                for k in range(GD):
                    ins = V.bn_stats(st1[j][:, k, :], x_in[j][:, k * XW:k * XW + D])
                ins.then_inc(d_ln1, 1)

            def dense_moments(u, part):
                j = u.mod(4)
                v.wait_ge(d_ln1, u.times(5, part))
                moment_part(part, st1[j], su1[j], df1[j], sq1[j], m21[j], neg1[j], var1[j], GD, d_ln1)

            def dense_rest(u):
                rest_of(hr[u.mod(2)], x_in[u.mod(4)], neg1[u.mod(4)], GD, d_ln1)

            def dense_x1(u, pair):
                j, h = u.mod(2), pair // 2
                if pair == 0:
                    v.wait_ge(d_scl, u.times(2, 2))
                if pair % 2 == 0:
                    wait(v, d_y, u.times(2, h - 3))
                v.wait_ge(d_mm, u.times(4, pair + 1))
                for k in (2 * pair, 2 * pair + 1):
                    ins = V.scalar_tensor_tensor(x1[j][:, k * D:(k + 1) * D], bank[2 + pair % 2][:, k % 2 * D:(k % 2 + 1) * D],
                                                 scl1[u.mod(4)][:, k:k + 1], x_in[u.mod(4)][:, k * XW:k * XW + D],
                                                 ALU.mult, ALU.add)
                ins.then_inc(d_x1, 1)

            def dense_stats2(u, pair):
                j = u.mod(2)
                v.wait_ge(d_x1, u.times(4, pair + 1))
                for k in (2 * pair, 2 * pair + 1):
                    ins = V.bn_stats(st2[j][:, k, :], x1[j][:, k * D:(k + 1) * D])
                if pair == 3:
                    ins.then_inc(d_ln2, 1)

            def dense_moments2(u, part):
                j = u.mod(2)
                v.wait_ge(d_ln2, u.times(4, part))
                moment_part(part, st2[j], su2[j], df2[j], sq2[j], m22[j], neg2[j], var2[j], GD, d_ln2)

            def selector(into, j, key):
                return V.tensor_tensor(x3(into[j], P, GQ), x3(q_row[j], P, GQ),
                                       bc_last(q_key[j][:, key * GQ:(key + 1) * GQ], P), ALU.is_equal)

            def p1_stats(q):
                j = q.mod(2)
                v.wait_ge(e_g[j], q.over(2, 64, 64))
                for t in range(GQ):
                    ins = V.bn_stats(st_e[j][:, t, :], x_e[j][:, t * XW:t * XW + D])
                ins.then_inc(e_ln, 1)

            def p1_moments(q, part):
                j = q.mod(2)
                v.wait_ge(e_ln, q.times(5, part))
                moment_part(part, st_e[j], su_e[j], df_e[j], sq_e[j], m2_e[j], neg_e[j], var_e[j], GQ, e_ln)

            def p1_rest_rows(q):
                rest_of(hr_e[q.mod(2)], x_e[q.mod(2)], neg_e[q.mod(2)], GQ, e_ln)

            def p1_selectors(q):
                wait(v, e_seg, q.times(GQ, -GQ))
                v.wait_ge(e_tb[q.mod(2)], q.over(2, 48, 48))
                selector(same, q.mod(2), 0)
                selector(carry, q.mod(2), 1).then_inc(e_sc, 1)

            def p1_outer(n):
                j, t = n.c // GQ % 2, n.mod(4)
                v.wait_ge(e_xb, n.times(1, 1))
                V.tensor_tensor(xr[n.mod(2)][:, 65:161].rearrange("p (u i) -> p u i", i=3), bc_last(bank[7][:, U_C:U_C + DU], 3),
                                bc_mid(ed(j, t, 1, 4), DU), ALU.mult).then_inc(e_vx, 1)

            def p1_message(n):
                j, t = n.c // GQ % 2, n.mod(4)
                v.wait_ge(e_vx, n.times(1, 1))
                wait(v, e_seg, n.times(1, -1))
                V.scalar_tensor_tensor(v_e[n.mod(2)][:, :], bank[7][:, U_A:U_A + CW], ed(j, t, 0, 1), xr[n.mod(2)][:, :],
                                       ALU.mult, ALU.add).then_inc(e_v, 1)

            def p1_features(n, part):
                j, t = n.c // GQ % 2, n.mod(4)
                g, w, f = g_e[n.mod(2)], bank[5 + n.mod(2)][:, D:D + 192], feat[n.mod(2)]
                if part == 0:
                    if t == 0:
                        v.wait_ge(e_sc, n.over(4, 1, 1))
                    v.wait_ge(e_gg, n.times(1, 1))
                    wait(v, e_ftr, n.times(1, -1))
                    V.tensor_tensor(f[:, 128:320].rearrange("p (a u i) -> p a u i", a=2, i=3),
                                    w[:, 128:192].rearrange("p (a u) -> p a u", a=2).unsqueeze(3).to_broadcast([P, 2, DU, 3]),
                                    g[:, DS:D].rearrange("p (u i) -> p u i", i=3).unsqueeze(1).to_broadcast([P, 2, DU, 3]),
                                    ALU.mult).then_inc(e_fm, 1)
                elif part == 1:
                    V.tensor_tensor(f[:, 0:128].rearrange("p (a u) -> p a u", a=2), w[:, 0:128].rearrange("p (a u) -> p a u", a=2),
                                    bc_mid(g[:, 0:DS], 2), ALU.mult)
                else:
                    v.wait_ge(e_fm, n.times(1, 1))
                    V.tensor_tensor(f[:, 224:320].rearrange("p (u i) -> p u i", i=3),
                                    f[:, 224:320].rearrange("p (u i) -> p u i", i=3),
                                    bc_mid(ed(j, t, 1, 4), DU), ALU.mult).then_inc(e_ft, 1)

            def step(u):
                s0, s1 = At(u.i, 2 * u.c, 8), At(u.i, 2 * u.c + 1, 8)
                q1 = At(u.i, u.c // 2, 2) + 1
                now, ahead, tile = (u - 1).within(U), (u + 1).within(U), s0.within(T)
                rows = u.mod(2) == 0 and q1.within(Q)
                if now:
                    dense_x1(u - 1, 0)
                    dense_x1(u - 1, 1)
                    dense_stats2(u - 1, 0)
                    dense_stats2(u - 1, 1)
                if (s0 - 2).within(T):
                    p1_outer(s0 - 2)
                if tile:
                    p1_features(s0, 0)
                    p1_features(s0, 1)
                if (s0 - 2).within(T):
                    p1_message(s0 - 2)
                if tile:
                    p1_features(s0, 2)
                if ahead:
                    dense_stats(u + 1)
                if now:
                    dense_x1(u - 1, 2)
                if ahead:
                    dense_moments(u + 1, 1)
                if now:
                    dense_x1(u - 1, 3)
                if ahead:
                    dense_moments(u + 1, 2)
                if now:
                    dense_stats2(u - 1, 2)
                if ahead:
                    dense_moments(u + 1, 3)
                if now:
                    dense_stats2(u - 1, 3)
                if rows:
                    p1_stats(q1)
                if (s1 - 2).within(T):
                    p1_outer(s1 - 2)
                if ahead:
                    dense_rest(u + 1)
                if now:
                    dense_moments2(u - 1, 1)
                if tile:
                    p1_features(s1, 0)
                if rows:
                    p1_moments(q1, 1)
                if tile:
                    p1_features(s1, 1)
                if now:
                    dense_moments2(u - 1, 2)
                if (s1 - 2).within(T):
                    p1_message(s1 - 2)
                if rows:
                    p1_moments(q1, 2)
                if tile:
                    p1_features(s1, 2)
                if now:
                    dense_moments2(u - 1, 3)
                if rows:
                    p1_moments(q1, 3)
                    p1_rest_rows(q1)
                if u.mod(2) == 1 and q1.within(Q):
                    p1_selectors(q1)

            dense_stats(At(0, 0))
            for part in (1, 2, 3):
                dense_moments(At(0, 0), part)
            dense_rest(At(0, 0))
            p1_stats(At(0, 0, 2))
            for part in (1, 2, 3):
                p1_moments(At(0, 0, 2), part)
            p1_rest_rows(At(0, 0, 2))
            p1_selectors(At(0, 0, 2))
            for u in range(4):
                step(At(0, u))
            with v.Fori(1, U // 4) as i:
                for c in range(4):
                    step(At(i, c))
            for u in range(U - 2, U + 2):
                step(At(0, u))

            PI2 = 6.283185307179586
            CA = 6.28125
            CB = 0.0019350051879882812
            CC = PI2 - CA - CB
            ROUND = 1.5 * 2.0 ** 23
            PI_IN = 3.1415925

            def p2_stats(q):
                v.wait_ge(r_g[q.mod(4)], q.over(4, 64, 64))
                for t in range(GQ):
                    ins = V.bn_stats(st_e[q.mod(2)][:, t, :], x_q[q.mod(4)][:, t * XW:t * XW + D])
                ins.then_inc(r_ln1, 1)

            def p2_moments(q, part):
                j = q.mod(2)
                v.wait_ge(r_ln1, q.times(5, part))
                moment_part(part, st_e[j], su_e[j], df_e[j], sq_e[j], m2_e[j], neg_e[j], var_e[j], GQ, r_ln1)

            def p2_angle(q, part):
                j = q.mod(2)
                ang, turns, rest, arg = (trig[n][j] for n in range(4))
                k = turns[:, GQ:2 * GQ]
                if part == 0:
                    v.wait_ge(r_cv[q.mod(4)], q.over(4, 16, 16))
                    ins = V.tensor_tensor(ang[:, 0:GQ], x3(cv[q.mod(4)], CW, GQ)[:, :, 0], x3(x_q[q.mod(4)], XW, GQ)[:, :, D],
                                          ALU.mult)
                else:
                    v.wait_ge(r_ang, q.times(8, part))
                if part == 1:
                    ins = V.tensor_scalar(turns[:, 0:GQ], ang[:, 0:GQ], 1.0 / PI2, ROUND, ALU.mult, ALU.add)
                elif part == 2:
                    ins = V.tensor_scalar(turns[:, GQ:2 * GQ], turns[:, 0:GQ], -ROUND, None, ALU.add)
                elif part == 3:
                    ins = V.scalar_tensor_tensor(rest[:, 0:GQ], k, -CA, ang[:, 0:GQ], ALU.mult, ALU.add)
                elif part == 4:
                    ins = V.scalar_tensor_tensor(rest[:, GQ:2 * GQ], k, -CB, rest[:, 0:GQ], ALU.mult, ALU.add)
                elif part == 5:
                    ins = V.scalar_tensor_tensor(ang[:, GQ:2 * GQ], k, -CC, rest[:, GQ:2 * GQ], ALU.mult, ALU.add)
                elif part == 6:
                    ins = V.tensor_scalar(arg[:, 0:GQ], ang[:, GQ:2 * GQ], PI_IN, -PI_IN, ALU.min, ALU.max)
                elif part == 7:
                    ins = V.tensor_scalar(arg[:, GQ:2 * GQ], arg[:, 0:GQ], 0.5, None, ALU.mult)
                ins.then_inc(r_ang, 1)

            def p2_scales(q, part):
                j = q.mod(2)
                sines, half2, scales = trig[4][j], trig[5][j], trig[6][j]
                attr = x3(x_q[q.mod(4)], XW, GQ)[:, :, D]
                if part == 0:
                    v.wait_ge(r_sq1, q.times(1, 1))
                    v.wait_ge(r_sin, q.times(1, 1))
                    V.reciprocal(inv_e[j][:, :], sd_e[j][:, :])
                    V.tensor_tensor(scales[:, GQ:2 * GQ], sines[:, 0:GQ], attr, ALU.mult)
                    ins = V.tensor_tensor(half2[:, 0:GQ], sines[:, GQ:2 * GQ], sines[:, GQ:2 * GQ], ALU.mult)
                elif part == 1:
                    v.wait_ge(r_scl, q.times(4, 1))
                    V.tensor_tensor(scl_e[j][:, :], inv_e[j][:, :], attr, ALU.mult)
                    ins = V.tensor_scalar(half2[:, GQ:2 * GQ], half2[:, 0:GQ], -2.0, 1.0, ALU.mult, ALU.add)
                else:
                    v.wait_ge(r_scl, q.times(4, 2))
                    ins = V.tensor_tensor(scales[:, 0:GQ], scl_e[j][:, :], half2[:, GQ:2 * GQ], ALU.mult)
                ins.then_inc(r_scl, 1)

            def p2_self(q):
                j = q.mod(2)
                v.wait_ge(r_scl, q.times(4, 3))
                v.wait_ge(r_mm, q.times(1, 1))
                for t in range(GQ):
                    ins = V.scalar_tensor_tensor(part2[j][:, t * D:(t + 1) * D],
                                                 bank[2 + 2 * j + t // 2][:, t % 2 * D:(t % 2 + 1) * D],
                                                 trig[6][j][:, t:t + 1], x_q[q.mod(4)][:, t * XW:t * XW + D], ALU.mult, ALU.add)
                ins.then_inc(r_scl, 1)

            def p2_x1(q):
                j = q.mod(2)
                v.wait_ge(r_scl, q.times(4, 4))
                wait(v, r_y, q.times(1, -1))
                for t in range(GQ):
                    ins = V.scalar_tensor_tensor(x1[j][:, t * D:(t + 1) * D], cv[q.mod(4)][:, t * CW + 1:(t + 1) * CW],
                                                 trig[6][j][:, GQ + t:GQ + t + 1], part2[j][:, t * D:(t + 1) * D],
                                                 ALU.mult, ALU.add)
                ins.then_inc(r_x1, 2)

            def p2_stats2(q):
                j = q.mod(2)
                v.wait_ge(r_x1, q.times(2, 2))
                for t in range(GQ):
                    ins = V.bn_stats(st2[j][:, t, :], x1[j][:, t * D:(t + 1) * D])
                ins.then_inc(r_ln2, 1)

            def p2_moments2(q, part):
                j = q.mod(2)
                v.wait_ge(r_ln2, q.times(4, part))
                moment_part(part, st2[j], su2[j], df2[j], sq2[j], m22[j], neg2[j], var2[j], GQ, r_ln2)

            def p2_norm2(q, part):
                j = q.mod(2)
                if part == 0:
                    v.wait_ge(r_sq2, q.times(1, 1))
                    ins = V.reciprocal(inv2[j][:, 0:GQ], sd2[j][:, 0:GQ])
                else:
                    v.wait_ge(r_nmr, q.times(2, 1))
                    ins = V.tensor_tensor(nmr2[j][:, 0:GQ], neg2[j][:, 0:GQ], inv2[j][:, 0:GQ], ALU.mult)
                ins.then_inc(r_nmr, 1)

            def p2_y(q):
                j = q.mod(2)
                v.wait_ge(r_h1, q.times(1, 1))
                wait(v, r_sty[j], q.over(2, 16))
                V.tensor_tensor(yo[j][:, 0:GQ * D], x1[j][:, 0:GQ * D], h1[j][:, 0:GQ * D], ALU.add).then_inc(r_y, 1)

            def p2_step(q):
                a, b, c = q.within(Q), (q - 1).within(Q), (q - 2).within(Q)
                if a:
                    p2_stats(q)
                if b:
                    p2_scales(q - 1, 0)
                if a:
                    p2_moments(q, 1)
                    p2_angle(q, 0)
                if (q - 3).within(Q):
                    p2_y(q - 3)
                if a:
                    p2_moments(q, 2)
                    p2_angle(q, 1)
                if b:
                    p2_scales(q - 1, 1)
                if a:
                    p2_moments(q, 3)
                    p2_angle(q, 2)
                if b:
                    p2_scales(q - 1, 2)
                if a:
                    rest_of(hr_e[q.mod(2)], x_q[q.mod(4)], neg_e[q.mod(2)], GQ, r_ln1)
                    p2_angle(q, 3)
                if b:
                    p2_self(q - 1)
                if a:
                    p2_angle(q, 4)
                if c:
                    p2_norm2(q - 2, 0)
                if a:
                    p2_angle(q, 5)
                if c:
                    p2_norm2(q - 2, 1)
                if b:
                    p2_x1(q - 1)
                if a:
                    p2_angle(q, 6)
                if b:
                    p2_stats2(q - 1)
                if a:
                    p2_angle(q, 7)
                if b:
                    for part in (1, 2, 3):
                        p2_moments2(q - 1, part)

            v.wait_ge(d_y, 2 * U)
            for q in range(8):
                if q == 2:
                    for j in range(2):
                        v.wait_ge(d_sth[j], 16 * (U // 2))
                        v.wait_ge(d_sto[j], 16 * (U // 2))
                p2_step(At(0, q))
            with v.Fori(2, Q // 4) as i:
                for c in range(4):
                    p2_step(At(i, c))
            for q in range(Q - 1, Q + 3):
                p2_step(At(0, q))

            V.memset(xr[0][:, 0:DS], 0.0)
            V.memset(xr[1][:, 0:DS], 0.0)
            V.memset(tot[1][:, :], 0.0).then_inc(m_z, 1)
            v.wait_ge(m_z, 1)

            def p3_features(n):
                j, t = n.c // 4 % 2, n.mod(4)
                if t == 0:
                    v.wait_ge(m_g[j], n.over(8, 64, 64))
                wait(v, m_ftr, n.times(1, -1))
                f, h = feat[n.mod(2)], h1[j][:, t * D:(t + 1) * D]
                V.tensor_scalar(f[:, 0:D], h, ed(j, t, 0, 1), None, ALU.mult)
                turned = bass.AP(tensor=q_ed[j], offset=t * EW + 1, ap=[[GQ * EW, P], [1, 3], [0, DU], [1, 3]])
                V.tensor_tensor(f[:, D:D + 3 * DV].rearrange("p (s u i) -> p s u i", s=3, i=3),
                                h[:, DS:D].rearrange("p (u i) -> p u i", i=3).unsqueeze(1).to_broadcast([P, 3, DU, 3]),
                                turned, ALU.mult).then_inc(m_ft, 1)

            def p3_message(n):
                j, t = n.c // GQ % 2, n.mod(4)
                b = bank[2 + n.mod(2)]
                v.wait_ge(m_u, n.times(1, 1))
                x = xr[n.mod(2)]
                V.tensor_tensor(x[:, DS:D].rearrange("p (u i) -> p u i", i=3), bc_last(b[:, D:D + DU], 3),
                                bc_mid(ed(j, t, 1, 4), DU), ALU.mult).then_inc(m_vx, 1)

            def p3_message_sum(n):
                v.wait_ge(m_vx, n.times(1, 1))
                wait(v, m_seg, n.times(1, -1))
                V.tensor_tensor(v_e[n.mod(2)][:, 0:D], bank[2 + n.mod(2)][:, 0:D], xr[n.mod(2)][:, 0:D], ALU.add) \
                    .then_inc(m_v, 1)

            def p3_out(n):
                j, t = n.c // GQ % 2, n.mod(4)
                if t == 0:
                    v.wait_ge(m_y[j], n.over(8, 16, 16))
                    wait(v, m_put[j], n.over(8, 64))
                v.wait_ge(m_tot, n.times(1, 1))
                V.scalar_tensor_tensor(yo[j][:, t * D:(t + 1) * D], tot[j][:, t * CW:t * CW + D], 0.0,
                                       x1[j][:, t * D:(t + 1) * D], ALU.max, ALU.add).then_inc(m_o, 1)

            def p3_same(n):
                j = n.c // GQ % 2
                wait(v, m_seg, n.times(1, -GQ))
                v.wait_ge(m_tb[j], n.over(8, 48, 48))
                selector(same, j, 0)

            def p3_slot(n):
                if n.within(T):
                    p3_features(n)
                if (n - 2).within(T):
                    p3_message(n - 2)
                if (n - 4).within(T):
                    p3_out(n - 4)
                if (n - 2).within(T):
                    p3_message_sum(n - 2)
                if n.mod(4) == 3 and (n + 1).within(T):
                    p3_same(n + 1)
                if n.mod(4) == 0 and n.within(T):
                    selector(carry, n.c // GQ % 2, 1).then_inc(m_sc, 1)

            p3_same(At(0, 0, 8))

            for n in range(16):
                if n == GQ:
                    for j in range(2):
                        v.wait_ge(r_sty[j], 16 * ((Q + 1 - j) // 2))
                p3_slot(At(0, n, 8))
            with v.Fori(2, (Q - 1) // 2) as i:
                for c in range(8):
                    p3_slot(At(i, c, 8))
            for n in range(T - GQ, T + 4):
                p3_slot(At(0, n, 8))


def pack_weights(np, w):
    pack = np.zeros((P, W_END), np.float32)
    u3 = np.arange(DU) * 3

    def kron(a, shift=0):
        k = np.zeros((DV, DV), np.float32)
        for i in range(3):
            k[np.ix_(u3 + i, u3 + (i + shift) % 3)] = a
        return k

    for col, w0, w1 in ((W_SC, "L0_gnn_sc_w0", "L0_gnn_sc_w1"), (W_L1, "L0_gnn_lin1_w0", "L0_gnn_lin1_w1")):
        pack[0:32, col:col + DS] = w[w0][32:64]
        pack[32:128, col + DS:col + D] = kron(w[w1])
        for t in range(4):
            pack[32 * t:32 * t + 32, col + D + t * DS:col + D + (t + 1) * DS] = w[w0][0:32]
    for t in range(4):
        pack[8 * t:8 * t + 8, W_FC1 + 64 * t:W_FC1 + 64 * (t + 1)] = w["L0_gnn_fc_w1"]
    for h in range(2):
        pack[64 * h:64 * h + 64, W_FC2 + 192 * h:W_FC2 + 192 * (h + 1)] = w["L0_gnn_fc_w2"]
    lin2a, lin2b, lin3 = w["L0_gnn_lin2_w0"], w["L0_gnn_lin2_w1"], w["L0_gnn_lin3_w"]
    rest = np.repeat(np.concatenate([lin3[64:], lin2a[64:]], 1), 3, 0)
    pack[64:128, W_R1:W_R1 + 32] = lin2b[0:64]
    pack[0:64, W_R1 + 32:W_R1 + 33] = lin3[0:64]
    pack[0:64, W_R1 + 33:W_R1 + 97] = lin2a[0:64]
    pack[0:96, W_R2:W_R2 + 96] = kron(lin2b[64:])
    pack[96:128, W_R2 + 96:W_R2 + 161] = rest[0:32]
    pack[64:128, W_R3:W_R3 + 65] = rest[32:96]
    pack[0:64, W_W1T:W_W1T + 64] = w["L1_gnn_W1"].T
    pack[0:64, W_W2T:W_W2T + 96] = np.repeat(w["L1_gnn_W2"].T, 3, 1)
    pack[0:32, W_W3T:W_W3T + 64] = w["L1_gnn_W3"].T
    pack[0:96, W_W4T:W_W4T + 96] = kron(w["L1_gnn_W4"].T)
    pack[0:96, W_W5T:W_W5T + 96] = kron(w["L1_gnn_W5"].T)
    pack[0:64, W_WS:W_WS + 64] = w["L1_gnn_Ws"]
    pack[0:96, W_WVK:W_WVK + 96] = kron(w["L1_gnn_Wv"])
    pack[0:32, W_WV:W_WV + 32] = w["L1_gnn_Wv"]
    pack[0:96, W_WVA:W_WVA + 96] = kron(w["L1_gnn_Wv"], 2)
    pack[0:96, W_WVB:W_WVB + 96] = kron(w["L1_gnn_Wv"], 1)
    return pack


def kernel(**inputs):
    import numpy as np
    import concourse.bacc as bacc
    from concourse.bass_utils import run_bass_kernel_spmd as run

    w = {k: np.asarray(v) for k, v in inputs.items()}
    N, E = w["x"].shape[0], w["src"].shape[0]
    T = -(-E // (P * GQ)) * GQ
    pad = T * P - E

    def by_tile(a, fill):
        a = np.concatenate([a, np.full((pad,) + a.shape[1:], fill, a.dtype)])
        return np.ascontiguousarray(np.swapaxes(a.reshape((T, P) + a.shape[1:]), 0, 1))

    y, rows = w["edge_attr_4"], by_tile(w["edge_attr_8"], 0)
    arrays = {
        "xa": np.ascontiguousarray(np.concatenate([w["x"], w["node_vec1"]], 1)),
        "src": by_tile(w["src"].astype(np.int32), 0),
        "dst": by_tile(w["dst"].astype(np.int32), N),
        "number": np.ascontiguousarray(np.arange(T * P, dtype=np.float32).reshape(T, P).T),
        "edges_in": by_tile(np.concatenate([y, y[:, 1:3]], 1), 0),
        "scalars_in": rows,
        "scalars_t_in": np.ascontiguousarray(rows.reshape(P, T // GQ, GQ * SW).transpose(1, 2, 0)),
        "wpack": pack_weights(np, w),
    }
    nc = bacc.Bacc("TRN2", target_bir_lowering=False, num_devices=1)
    aps = {k: nc.dram_tensor(f"in_{k}", a.shape, mybir.dt.from_np(a.dtype), kind="ExternalInput").ap()
           for k, a in arrays.items()}
    out = nc.dram_tensor("out", (N, D), mybir.dt.float32, kind="ExternalOutput").ap()
    gnn_kernel(nc, out=out, **aps)
    r = run(nc, [{f"in_{k}": a for k, a in arrays.items()}], core_ids=[0])
    return r.results[0]["out"]
```
